# Optimizing a Trainium2 kernel written in Bass

```python
import numpy as np
import jax
import jax.numpy as jnp

def _softmax(x, axis=-1):
    return jax.nn.softmax(x, axis=axis)

def _gelu(x):
    return jax.nn.gelu(x, approximate=True)

def _silu(x):
    return jax.nn.silu(x)

def _sigmoid(x):
    return jax.nn.sigmoid(x)

def _layernorm(x, axis=-1, eps=1e-05):
    m = jnp.mean(x, axis=axis, keepdims=True)
    v = jnp.var(x, axis=axis, keepdims=True)
    return (x - m) / jnp.sqrt(v + eps)

def _scatter_add(tgt, idx, src, axis=0):
    return tgt.at[idx].add(src)

def _segment_sum(src, seg, n):
    return jax.ops.segment_sum(src, seg, n)
kernel_name = 'mk_xattn_ffn_d2_seqx_r8_96eee0'

def setup_inputs(seed: int=0):
    np.random.seed(seed)
    _w = jnp.asarray

    def _rec_inputs():
        import jax
        import jax.numpy as jnp
        _rk = jax.random.key(seed)
        x = -0.0002928 + 1 * jax.random.normal(jax.random.fold_in(_rk, 1), (8, 256, 128), jnp.float32)
        _lenS = 256 - jax.random.randint(jax.random.fold_in(_rk, 7), (8,), 0, max(1, 256 // 4) + 1, jnp.int32)
        _lenS2 = 256 - jax.random.randint(jax.random.fold_in(_rk, 8), (8,), 0, max(1, 256 // 4) + 1, jnp.int32)
        _ctx_1024P = jax.random.normal(jax.random.fold_in(_rk, 11), (8, 16, 128), jnp.float32)
        _ctx_1024c = jax.random.dirichlet(jax.random.fold_in(_rk, 511), 0.3 * jnp.ones((16,), jnp.float32), (8, 256))
        _ctx_1024t = jnp.einsum('bsk,bkd->bsd', _ctx_1024c, _ctx_1024P)
        _ctx_1024t = _ctx_1024t * jax.lax.rsqrt(jnp.mean(jnp.square(_ctx_1024t)) + 1e-12) * 0.953939
        ctx_1024 = -1.39393e-06 + 0.999914 * (_ctx_1024t + 0.3 * jax.random.normal(jax.random.fold_in(_rk, 611), (8, 256, 128), jnp.float32))
        itok_BxS_8_8191 = jax.random.randint(jax.random.fold_in(_rk, 12), (8, 256), 8, 1024, jnp.int32)
        itok_BxS2_1_8191 = jax.random.randint(jax.random.fold_in(_rk, 13), (8, 256), 1, 1024, jnp.int32)
        _validS = jnp.arange(256)[None, :] < _lenS[:, None]
        _validS2 = jnp.arange(256)[None, :] < _lenS2[:, None]
        _causal = jnp.tril(jnp.ones((256, 256), dtype=bool))
        mask_BxSxS2_if1 = jnp.where(jnp.ones((8, 256, 256), dtype=bool), 1, 0).astype(jnp.int32)
        return (x, ctx_1024, itok_BxS_8_8191, itok_BxS2_1_8191, mask_BxSxS2_if1)
    x, ctx_1024, itok_BxS_8_8191, itok_BxS2_1_8191, mask_BxSxS2_if1 = _rec_inputs()

    def _L0_xattn_setup():
        import jax, jax.numpy as jnp
        import numpy as np
        B, T, D, H = (2, 256, 128, 16)
        DH = D // H
        key = jax.random.key(seed)
        ks = jax.random.split(key, 11)
        s = 1.0 / np.sqrt(D)
        return {'q': jax.random.normal(ks[0], (B, T, D), jnp.float32), 'k': jax.random.normal(ks[1], (B, T, D), jnp.float32), 'v': jax.random.normal(ks[2], (B, T, D), jnp.float32), 'wq_w': jax.random.normal(ks[3], (D, D), jnp.float32) * s, 'wq_b': jnp.zeros((D,), jnp.float32), 'wk_w': jax.random.normal(ks[4], (D, D), jnp.float32) * s, 'wk_b': jnp.zeros((D,), jnp.float32), 'wv_w': jax.random.normal(ks[5], (D, D), jnp.float32) * s, 'wv_b': jnp.zeros((D,), jnp.float32), 'wo_w': jax.random.normal(ks[6], (D, D), jnp.float32) * s, 'wo_b': jnp.zeros((D,), jnp.float32)}
    _L0_xattn_all = _L0_xattn_setup()
    _L0_xattn_in = {k: v for k, v in _L0_xattn_all.items() if k in ('wq_w', 'wq_b', 'wk_w', 'wk_b', 'wv_w', 'wv_b', 'wo_w', 'wo_b')}
    del _L0_xattn_all

    def _L0_ffn_setup():
        import jax, jax.numpy as jnp
        import numpy as np
        D_MODEL = 128
        D_HIDDEN = 512
        NUM_EXPERTS = 8
        B, T = (2, 256)
        key = jax.random.key(seed)
        ks = jax.random.split(key, 8)
        s = 0.02
        x = jax.random.normal(ks[0], (B, T, D_MODEL), dtype=jnp.float32)
        Wg = jax.random.normal(ks[1], (D_MODEL, NUM_EXPERTS), dtype=jnp.float32) * s
        bg = jnp.zeros((NUM_EXPERTS,), dtype=jnp.float32)
        W1 = jax.random.normal(ks[2], (NUM_EXPERTS, D_MODEL, D_HIDDEN), dtype=jnp.float32) * s
        b1 = jnp.zeros((NUM_EXPERTS, D_HIDDEN), dtype=jnp.float32)
        W2 = jax.random.normal(ks[3], (NUM_EXPERTS, D_HIDDEN, D_MODEL), dtype=jnp.float32) * s
        b2 = jnp.zeros((NUM_EXPERTS, D_MODEL), dtype=jnp.float32)
        return {'x': x, 'Wg': Wg, 'bg': bg, 'W1': W1, 'b1': b1, 'W2': W2, 'b2': b2}
    _L0_ffn_all = _L0_ffn_setup()
    _L0_ffn_in = {k: v for k, v in _L0_ffn_all.items() if k in ('Wg', 'bg', 'W1', 'b1', 'W2', 'b2')}
    del _L0_ffn_all

    def _L1_xattn_setup():
        import jax, jax.numpy as jnp
        import numpy as np
        DIM = 128
        NUM_HEADS = 16
        HEAD_DIM = DIM // NUM_HEADS

        def _slopes(num_heads):
            ratio = 2.0 ** (-8.0 / num_heads)
            return jnp.asarray([ratio ** i for i in range(1, num_heads + 1)], dtype=jnp.float32)
        key = jax.random.key(seed)
        ks = jax.random.split(key, 10)
        b, q_len, k_len = (2, 256, 512)
        query = jax.random.normal(ks[0], (b, q_len, DIM), dtype=jnp.float32)
        keys = jax.random.normal(ks[1], (b, k_len, DIM), dtype=jnp.float32)
        values = jax.random.normal(ks[2], (b, k_len, DIM), dtype=jnp.float32)
        query_pos = jnp.sort(jax.random.randint(ks[3], (b, q_len), 0, 1024), axis=-1)
        key_pos = jnp.sort(jax.random.randint(ks[4], (b, k_len), 0, 1024), axis=-1)
        mask = jnp.ones((b, q_len, k_len), dtype=jnp.int32)
        lim = float(np.sqrt(6.0 / (DIM + DIM)))
        W_q = jax.random.uniform(ks[5], (DIM, DIM), minval=-lim, maxval=lim, dtype=jnp.float32)
        W_k = jax.random.uniform(ks[6], (DIM, DIM), minval=-lim, maxval=lim, dtype=jnp.float32)
        W_v = jax.random.uniform(ks[7], (DIM, DIM), minval=-lim, maxval=lim, dtype=jnp.float32)
        W_o = jax.random.uniform(ks[8], (DIM, DIM), minval=-lim, maxval=lim, dtype=jnp.float32)
        return {'query': query, 'keys': keys, 'values': values, 'W_q': W_q, 'W_k': W_k, 'W_v': W_v, 'W_o': W_o, 'query_pos': query_pos, 'key_pos': key_pos, 'mask': mask}
    _L1_xattn_all = _L1_xattn_setup()
    _L1_xattn_in = {k: v for k, v in _L1_xattn_all.items() if k in ('W_q', 'W_k', 'W_v', 'W_o')}
    del _L1_xattn_all

    def _L1_ffn_setup():
        import jax, jax.numpy as jnp
        import numpy as np
        import math
        BETA = 0.9
        THRESHOLD = 1.0
        NUM_STEPS = 5
        ALPHA = 2.0

        @jax.custom_vjp
        def spike_fn(u):
            return (u > 0).astype(u.dtype)

        def _spike_fwd(u):
            return (spike_fn(u), u)

        def _spike_bwd(u, g):
            s = jnp.pi / 2.0 * ALPHA * u
            return (g * (ALPHA / 2.0) / (1.0 + s * s),)
        spike_fn.defvjp(_spike_fwd, _spike_bwd)
        key = jax.random.key(seed)
        k1, k2, k3 = jax.random.split(key, 3)
        n_embd = 128
        x = jax.random.normal(k1, (4, 256, n_embd), dtype=jnp.float32)
        W_fc = jax.random.normal(k2, (4 * n_embd, n_embd), dtype=jnp.float32) / math.sqrt(n_embd)
        W_proj = jax.random.normal(k3, (n_embd, 4 * n_embd), dtype=jnp.float32) / math.sqrt(4 * n_embd)
        return {'x': x, 'W_fc': W_fc, 'W_proj': W_proj}
    _L1_ffn_all = _L1_ffn_setup()
    _L1_ffn_in = {k: v for k, v in _L1_ffn_all.items() if k in ('W_fc', 'W_proj')}
    del _L1_ffn_all
    return {'x': x, 'ctx_1024': ctx_1024, 'itok_BxS_8_8191': itok_BxS_8_8191, 'itok_BxS2_1_8191': itok_BxS2_1_8191, 'mask_BxSxS2_if1': mask_BxSxS2_if1, 'L0_xattn_wq_w': _L0_xattn_in['wq_w'], 'L0_xattn_wq_b': _L0_xattn_in['wq_b'], 'L0_xattn_wk_w': _L0_xattn_in['wk_w'], 'L0_xattn_wk_b': _L0_xattn_in['wk_b'], 'L0_xattn_wv_w': _L0_xattn_in['wv_w'], 'L0_xattn_wv_b': _L0_xattn_in['wv_b'], 'L0_xattn_wo_w': _L0_xattn_in['wo_w'], 'L0_xattn_wo_b': _L0_xattn_in['wo_b'], 'L0_ffn_Wg': _L0_ffn_in['Wg'], 'L0_ffn_bg': _L0_ffn_in['bg'], 'L0_ffn_W1': _L0_ffn_in['W1'], 'L0_ffn_b1': _L0_ffn_in['b1'], 'L0_ffn_W2': _L0_ffn_in['W2'], 'L0_ffn_b2': _L0_ffn_in['b2'], 'L1_xattn_W_q': _L1_xattn_in['W_q'], 'L1_xattn_W_k': _L1_xattn_in['W_k'], 'L1_xattn_W_v': _L1_xattn_in['W_v'], 'L1_xattn_W_o': _L1_xattn_in['W_o'], 'L1_ffn_W_fc': _L1_ffn_in['W_fc'], 'L1_ffn_W_proj': _L1_ffn_in['W_proj']}

def reference(x, ctx_1024, itok_BxS_8_8191, itok_BxS2_1_8191, mask_BxSxS2_if1, L0_xattn_wq_w, L0_xattn_wq_b, L0_xattn_wk_w, L0_xattn_wk_b, L0_xattn_wv_w, L0_xattn_wv_b, L0_xattn_wo_w, L0_xattn_wo_b, L0_ffn_Wg, L0_ffn_bg, L0_ffn_W1, L0_ffn_b1, L0_ffn_W2, L0_ffn_b2, L1_xattn_W_q, L1_xattn_W_k, L1_xattn_W_v, L1_xattn_W_o, L1_ffn_W_fc, L1_ffn_W_proj):
    import jax
    import jax.numpy as jnp

    def _L0_xattn_ref(q, k, v, wq_w, wq_b, wk_w, wk_b, wv_w, wv_b, wo_w, wo_b):
        import jax, jax.numpy as jnp
        import numpy as np
        B, T, D, H = (2, 256, 128, 16)
        DH = D // H
        b, t, d = q.shape
        wq = (q @ wq_w.T + wq_b).reshape(b, t, H, DH)
        wk = (k @ wk_w.T + wk_b).reshape(b, t, H, DH)
        wv = (v @ wv_w.T + wv_b).reshape(b, t, H, DH)
        scores = jnp.einsum('bthd,bshd->bhts', wq, wk) / jnp.sqrt(jnp.float32(DH))
        probs = jax.nn.softmax(scores, axis=-1)
        attn = jnp.einsum('bhts,bshd->bthd', probs, wv)
        attn = attn.reshape(b, t, d)
        return attn @ wo_w.T + wo_b

    def _L0_ffn_ref(x, Wg, bg, W1, b1, W2, b2):
        import jax, jax.numpy as jnp
        import numpy as np
        D_MODEL = 128
        D_HIDDEN = 512
        NUM_EXPERTS = 8
        B, T = (2, 256)
        gate_logits = jnp.einsum('btd,de->bte', x, Wg) + bg
        gate_scores = jax.nn.softmax(gate_logits, axis=-1)
        top1_idx = jnp.argmax(gate_scores, axis=-1)
        top1_mask = jax.nn.one_hot(top1_idx, NUM_EXPERTS, dtype=x.dtype)
        top1_weight = jnp.sum(gate_scores * top1_mask, axis=-1, keepdims=True)
        h = jax.nn.silu(jnp.einsum('btd,edh->bteh', x, W1) + b1)
        o = jnp.einsum('bteh,ehd->bted', h, W2) + b2
        y = jnp.sum(o * top1_mask[..., None], axis=2) * top1_weight
        return y

    def _L1_xattn_ref(query, keys, values, W_q, W_k, W_v, W_o, query_pos, key_pos, mask):
        import jax, jax.numpy as jnp
        import numpy as np
        DIM = 128
        NUM_HEADS = 16
        HEAD_DIM = DIM // NUM_HEADS

        def _slopes(num_heads):
            ratio = 2.0 ** (-8.0 / num_heads)
            return jnp.asarray([ratio ** i for i in range(1, num_heads + 1)], dtype=jnp.float32)
        b, q_len, _ = query.shape
        k_len = keys.shape[1]
        scale = 1.0 / np.sqrt(HEAD_DIM)
        Q = (query @ W_q.T).reshape(b, q_len, NUM_HEADS, HEAD_DIM).transpose(0, 2, 1, 3)
        K = (keys @ W_k.T).reshape(b, k_len, NUM_HEADS, HEAD_DIM).transpose(0, 2, 1, 3)
        V = (values @ W_v.T).reshape(b, k_len, NUM_HEADS, HEAD_DIM).transpose(0, 2, 1, 3)
        scores = jnp.einsum('bhqd,bhkd->bhqk', Q, K) * scale
        dist = (query_pos[:, :, None] - key_pos[:, None, :]).astype(scores.dtype)
        bias = -_slopes(NUM_HEADS)[None, :, None, None] * dist[:, None, :, :]
        scores = scores + bias
        scores = jnp.where(mask[:, None, :, :] == 0, -jnp.inf, scores)
        m = jnp.max(scores, axis=-1, keepdims=True)
        e = jnp.exp(scores - m)
        attn = e / (1.0 + jnp.sum(e, axis=-1, keepdims=True))
        out = jnp.einsum('bhqk,bhkd->bhqd', attn, V)
        out = out.transpose(0, 2, 1, 3).reshape(b, q_len, DIM)
        return out @ W_o.T

    def _L1_ffn_ref(x, W_fc, W_proj):
        import jax, jax.numpy as jnp
        import numpy as np
        import math
        BETA = 0.9
        THRESHOLD = 1.0
        NUM_STEPS = 5
        ALPHA = 2.0

        @jax.custom_vjp
        def spike_fn(u):
            return (u > 0).astype(u.dtype)

        def _spike_fwd(u):
            return (spike_fn(u), u)

        def _spike_bwd(u, g):
            s = jnp.pi / 2.0 * ALPHA * u
            return (g * (ALPHA / 2.0) / (1.0 + s * s),)
        spike_fn.defvjp(_spike_fwd, _spike_bwd)
        h = jnp.square(jax.nn.relu(jnp.einsum('bsd,fd->bsf', x, W_fc)))
        y = jnp.einsum('bsf,df->bsd', h, W_proj)

        def step(mem, _):
            reset = jax.lax.stop_gradient(spike_fn(mem - THRESHOLD))
            mem_new = BETA * mem + y - reset * THRESHOLD
            spk = spike_fn(mem_new - THRESHOLD)
            return (mem_new, spk)
        mem0 = jnp.zeros_like(y)
        _, spks = jax.lax.scan(step, mem0, None, length=NUM_STEPS)
        return jnp.sum(spks, axis=0) / NUM_STEPS
    x = x + _L0_xattn_ref(_layernorm(x, axis=-1), ctx_1024, ctx_1024, L0_xattn_wq_w, L0_xattn_wq_b, L0_xattn_wk_w, L0_xattn_wk_b, L0_xattn_wv_w, L0_xattn_wv_b, L0_xattn_wo_w, L0_xattn_wo_b)
    x = x + _L0_ffn_ref(_layernorm(x, axis=-1), L0_ffn_Wg, L0_ffn_bg, L0_ffn_W1, L0_ffn_b1, L0_ffn_W2, L0_ffn_b2)
    x = x + _L1_xattn_ref(_layernorm(x, axis=-1), ctx_1024, ctx_1024, L1_xattn_W_q, L1_xattn_W_k, L1_xattn_W_v, L1_xattn_W_o, itok_BxS_8_8191, itok_BxS2_1_8191, mask_BxSxS2_if1)
    x = x + _L1_ffn_ref(_layernorm(x, axis=-1), L1_ffn_W_fc, L1_ffn_W_proj)
    return x

_drawn_inputs = setup_inputs


def setup_inputs(seed=0):
    import zlib

    import numpy as np

    out = dict(_drawn_inputs(seed))
    spreads = {'L0_xattn_wq_b': (0.0, 0.295),
     'L0_xattn_wk_b': (0.0, 0.8),
     'L0_xattn_wv_b': (0.0, 0.1),
     'L0_xattn_wo_b': (0.0, 0.1),
     'L0_ffn_bg': (0.0, 0.544),
     'L0_ffn_b1': (0.0, 0.788),
     'L0_ffn_b2': (0.0, 0.337)}
    factors = {'L0_ffn_W1': 4.044, 'L0_ffn_W2': 3.864}
    for name, (base, spread) in spreads.items():
        noise = np.random.default_rng([zlib.crc32(name.encode()), seed]).standard_normal(out[name].shape)
        drawn = base * np.exp(spread * noise) if base else spread * noise
        out[name] = jnp.asarray(drawn.astype(out[name].dtype))
    for name, factor in factors.items():
        out[name] = (out[name] * factor).astype(out[name].dtype)
    return out
```

```python
from contextlib import ExitStack

import numpy as np

import concourse.bass as bass
from concourse import mybir

F32 = mybir.dt.float32
F16 = mybir.dt.float16
BF16 = mybir.dt.bfloat16
I32 = mybir.dt.int32
U32 = mybir.dt.uint32
ALU = mybir.AluOpType
ACT = mybir.ActivationFunctionType
AX = mybir.AxisListType

P = 128
B, S, D, H = 8, 256, 128, 16
DH = D // H
QT = S // P
NT = B * QT
HG = 4
NG = H // HG
NE, HID = 8, 512
HC = HID // P
EPS = 1e-5
STEPS, BETA = 5, 0.9
SLOT_TILES = NT + NE - 1
QK = 16.0
SC = QK * QK
MROW = 64.0
WS = 64.0
M0, MROWS = 96, 3 * HG
PB0 = M0 + MROWS
K_ROWS = PB0 + 3
PARTS = 3
MASKED = -1e30


def constants():
    eye = np.eye(P, dtype=np.float32)
    before = np.triu(np.ones((P, P), np.float32), 1)
    head_mask = np.zeros((P, HG), np.float32)
    for r in range(3 * 32):
        head_mask[r, (r % 32) // DH] = 1.0
    for r in range(MROWS):
        head_mask[M0 + r, r // 3] = MROW
    slopes = (2.0 ** (-8.0 / H)) ** np.arange(1, H + 1, dtype=np.float64)
    slope_col = np.tile(slopes.astype(np.float32), B)[:, None]
    route = np.zeros((P, 3, P), np.float32)
    route[:, 0] = np.tile(np.arange(NE) - NE, NT)
    run = np.ones((NE, NT), np.float32)
    run[:, 0] = 0.0
    route[:, 1] = run.reshape(-1)
    route[:, 2] = np.arange(P)
    return {"c_eye": eye, "c_before": before, "c_head_mask": head_mask, "c_slope": slope_col,
            "c_route": route}


def layer(index, sem):
    names = ["ctx_loaded", "norm_own", "xvar", "xrstd", "xn_ready", "xnT_done", "xnT_copied",
             "q_done", "q_copied", "k_done", "k_copied", "v_done", "v_copied", "q_hi", "q_lo",
             "k_hi", "k_lo", "k_rep", "k_tile", "m_zeroed", "p1_done", "max_done", "m_parts", "own",
             "mT_done", "mT_copied", "p2_done", "exp_done", "pv_done", "o_copied", "ot_done",
             "ot_norm", "o_rc", "aT_done", "aT_copied", "op_done", "x_added"]
    ly = {n: sem(f"L{index}_{n}") for n in names}
    ly.update(index=index, bias=index == 0, position=index == 1)
    ly["q_tile"] = [sem(f"L{index}_q_tile{i}") for i in range(2)]
    if ly["position"]:
        ly["k_pos"] = [[sem(f"L{index}_k_pos{i}{par}") for par in range(2)] for i in range(2)]
        ly["ot_sum"] = sem(f"L{index}_ot_sum")
    else:
        ly["x_biased"] = sem(f"L{index}_x_biased")
    return ly


def build(nc, t, out):
    with ExitStack() as ctx:
        def sb(name, shape, dt=F32):
            return ctx.enter_context(nc.sbuf_tensor(name, shape, dt))

        def psum(name, shape, dt=F32):
            return ctx.enter_context(nc.psum_tensor(name, shape, dt))

        def sem(name):
            return ctx.enter_context(nc.semaphore(name))

        X = sb("X", [P, NT + QT, D])
        eye = sb("eye", [P, P])
        eye16 = sb("eye16", [P, P], F16)
        head_mask = sb("head_mask", [P, HG])
        W = {}
        for L in range(2):
            for n in "qkvo":
                W[n, L] = sb(f"w{n}{L}", [P, D])
        qkb = sb("qkb", [P, 2])
        qkbs = sb("qkbs", [P, 2])
        vb = sb("vb", [P, D])
        ob = sb("ob", [P, D])
        ctxT = [sb(f"ctxT{i}", [P, S]) for i in range(2)]
        xn = [sb(f"xn{i}", [P, QT, D]) for i in range(2)]
        st6 = sb("st6", [P, QT, 6])
        mv = sb("mv", [P, QT, 2])
        ve = sb("ve", [P, QT])
        rstd = sb("rstd", [P, QT])
        carried_v = sb("carried_v", [P, QT])
        mhalf = sb("mhalf", [P, QT])
        xnT = sb("xnT", [P, S])
        qf, kf = sb("qf", [P, S]), sb("kf", [P, S])
        q_hi = [sb(f"q_hi{i}", [P, S], F16) for i in range(2)]
        q_lo = [sb(f"q_lo{i}", [P, S], F16) for i in range(2)]
        k_hi, k_lo = sb("k_hi", [P, S], F16), sb("k_lo", [P, S], F16)
        k_rep = sb("k_rep", [P, NG, S], F16)
        Qt = [sb(f"Qt{i}", [P, NG, S], F16) for i in range(2)]
        Kt = [sb(f"Kt{i}", [P, H, S], F16) for i in range(2)]
        Vt = [sb(f"Vt{i}", [P, QT, H, 32]) for i in range(2)]
        nm = [sb(f"nm{i}", [P, QT, H]) for i in range(2)]
        mr = sb("mr", [P, QT, 8])
        mr2 = sb("mr2", [P, QT, 8])
        mparts = [sb(f"mparts{i}", [P, QT, H, PARTS], F16) for i in range(2)]
        Pt = [sb(f"Pt{i}", [P, HG, QT * S]) for i in range(NG)]
        Osb = [sb(f"Osb{i}", [P, NG, S]) for i in range(2)]
        rc = sb("rc", [P, QT, H])
        rsum = sb("rsum", [P, QT, H])
        attn = sb("attn", [P, QT, D])
        aT = sb("aT", [P, S])
        S1 = [psum(f"S1_{i}", [P, QT, S]) for i in range(2)]
        S2 = [psum(f"S2_{i}", [P, 2, QT, S]) for i in range(2)]
        M = [psum(f"M{i}", [P, 512]) for i in range(2)]
        M16 = [m[:, :].bitcast(F16) for m in M]
        O_BANK = (1, 0, 1, 1)

        pos_i = sb("pos_i", [P, S], I32)
        pos_f = sb("pos_f", [P, S])
        slope = sb("slope", [P, 1])
        pos_r = sb("pos_r", [P, S])
        pos_parts = sb("pos_parts", [P, PARTS, S], F16)

        mask_bias = sb("mask_bias", [P, NT, S], BF16)
        eye_bf = sb("eye_bf", [P, P], BF16)
        mask_min = sb("mask_min", [P, 1])
        mask_hit = sb("mask_hit", [P, 1])
        mask_any = sb("mask_any", [P, 1], I32)
        mk = {n: sem(f"mask_{n}") for n in ("raw", "bias", "min", "hit", "count", "any")}

        ly = [layer(0, sem), layer(1, sem)]
        loaded, inited, pos_stored = sem("loaded"), sem("inited"), sem("pos_stored")
        N_LOADS, N_INIT = 30, 27
        pos_dram = nc.dram_tensor("pos_parts_dram", (B, H, PARTS, S), F16).ap()
        pos_own, pos_ready = sem("pos_own"), sem("pos_ready")
        w1_hi, w1_lo = sb("w1_hi", [P, NE * HID], F16), sb("w1_lo", [P, NE * HID], F16)
        w2_hi, w2_lo = sb("w2_hi", [P, NE * HID], F16), sb("w2_lo", [P, NE * HID], F16)
        wraw = [sb(f"wraw{i}", [P, 2048]) for i in range(2)]
        braw = sb("braw", [P, 40])
        brest = sb("brest", [P, 40])
        bparts = sb("bparts", [P, PARTS, 40], F16)
        b1rows = sb("b1rows", [P, NE * HID], F16)
        b2rows = sb("b2rows", [P, NE * D], F16)
        ones16 = sb("ones16", [P, P], F16)
        wg = sb("wg", [P, NE])
        bg = sb("bg", [P, NE])
        xn2 = Pt[2][:, :, :].rearrange("p i (t d) -> p (i t) d", d=D)
        before = sb("before", [P, P])
        ones32 = sb("ones32", [P, P])
        route_c = sb("route_c", [P, 3, P])
        logit = sb("logit", [P, NT, NE])
        top = sb("top", [P, NT])
        onehot = sb("onehot", [P, NT, NE])
        t1 = sb("t1", [P, NT, NE])
        t2 = sb("t2", [P, NT, NE])
        first = sb("first", [P, NT])
        gate = sb("gate", [P, NT])
        gsum = sb("gsum", [P, NT])
        tot = sb("tot", [P, NE, NT])
        cum = sb("cum", [P, NE, NT])
        rbase = sb("rbase", [P, NE, NT])
        cnt_i = sb("cnt_i", [P, NE], I32)
        cnt_s = sb("cnt_s", [P, NE], I32)
        ntile = sb("ntile", [P, NE])
        tend = sb("tend", [P, NE])
        tstart = sb("tstart", [P, NE])
        slotf = sb("slotf", [P, NT])
        slot = sb("slot", [P, NT], I32)
        cmp = sb("cmp", [P, SLOT_TILES, NE])
        expf = sb("expf", [P, SLOT_TILES])
        expert = sb("expert", [P, SLOT_TILES], I32)
        zero = sb("zero", [P, D])
        xs_dram = nc.dram_tensor("sorted_x", (SLOT_TILES * P, D), F32).ap()
        ys_dram = nc.dram_tensor("sorted_y", (SLOT_TILES * P, D), F32).ap()
        gT = [sb(f"gT{i}", [P, S]) for i in range(2)]
        xt = [sb(f"xt{i}", [P, D]) for i in range(2)]
        x_hi = [sb(f"x_hi{i}", [P, P], F16) for i in range(2)]
        x_lo = [sb(f"x_lo{i}", [P, P], F16) for i in range(2)]
        hf = [sb(f"hf{i}", [P, HID]) for i in range(2)]
        h_hi = [sb(f"h_hi{i}", [P, HID], F16) for i in range(2)]
        h_lo = [sb(f"h_lo{i}", [P, HID], F16) for i in range(2)]
        ysb = [sb(f"ysb{i}", [P, D]) for i in range(2)]
        yg = wraw[0][:, :].rearrange("p (t d) -> p t d", d=D)
        moe = {n: sem(f"moe_{n}") for n in (
            "wraw0", "wraw1", "split", "split_own", "braw", "bsplit", "brows", "rows0", "zfill",
            "norm_own", "var", "rstd", "xn", "xT", "xTc", "xcopy", "gm", "logit",
            "r", "exp", "gate", "onehot", "ranks", "slots", "scattered", "tT", "x_hi", "x_lo", "h", "hf",
            "h_hi", "h_lo", "y", "ysb", "gathered", "x", "xt0", "xt1", "stored0", "stored1")}
        wfc = sb("wfc", [P, HID])
        wpr = sb("wpr", [P, HC, D])
        hr, h2 = (Pt[i][:, 0:HG // 2, :].rearrange("p a (k n) -> p (a k) n", k=QT) for i in range(2))
        ymem = sb("ymem", [P, S])
        mem = sb("mem", [P, S])
        acc = sb("acc", [P, S])
        tmp = sb("tmp", [P, S])
        fin = [sb(f"fin{i}", [P, QT, D]) for i in range(2)]
        ff = {n: sem(f"ff_{n}") for n in ("norm_own", "var", "rstd", "xn", "xT", "xTc", "h", "relu", "sq", "y",
                                          "yc", "own", "acc", "out", "stored0", "stored1")}
        block = ctx.enter_context(nc.Block())

        def slots_loop(eng, slot_fn):
            for s in (-3, -2, -1, 0, 1):
                slot_fn(s, s % 2, s)
            with eng.Fori(1, 3) as i:
                for par in range(2):
                    slot_fn(2 * i + par, par, None)
            for s in (6, 7, 8):
                slot_fn(s, s % 2, s)

        def exists(s, d):
            return s is None or 0 <= s + d < B

        def attention_on_tensor(pe, ly, masked):
            def p1(b, par, h):
                if h % 8 == 0:
                    pe.wait_ge(ly["q_tile"][h // 8], 48 * b + 48)
                    pe.wait_ge(ly["k_tile"], 2 * b + h // 8 + 1)
                    pe.wait_ge(ly["m_zeroed"], 2 * b + h // 8 + 1)
                    if ly["position"]:
                        pe.wait_ge(ly["k_pos"][h // 8][par], 8 * (b - par) + 16)
                if not (isinstance(b, int) and b == 0 and h < 2):
                    pe.wait_ge(ly["max_done"], 16 * b + h - 1)
                for q in range(QT):
                    mm = pe.matmul(S1[h % 2][:, q, :], Qt[par][0:K_ROWS, h // HG, q * P:(q + 1) * P],
                                   Kt[par][0:K_ROWS, h, :], start=True, stop=not masked)
                    if masked:
                        mm = pe.matmul(S1[h % 2][:, q, :], eye_bf[:, :], mask_bias[:, bass.ds(b * QT + q, 1), :]
                                       .rearrange("p t n -> p (t n)"), start=False, stop=True)
                mm.then_inc(ly["p1_done"], 1)

            def p2(b, par, pair):
                if pair % 4 == 0:
                    pe.wait_ge(ly["mT_copied"], 2 * b + pair // 4 + 1)
                if not (isinstance(b, int) and b == 0 and pair < 2):
                    pe.wait_ge(ly["exp_done"], 8 * b + pair - 1)
                for hh in range(2):
                    h = 2 * pair + hh
                    for k in range(QT):
                        mm = pe.matmul(S2[pair % 2][:, hh, k, :], Kt[par][0:K_ROWS, h, k * P:(k + 1) * P],
                                       Qt[par][0:K_ROWS, h // HG, :], start=True, stop=not masked)
                        for q in range(QT if masked else 0):
                            mm = pe.matmul(S2[pair % 2][:, hh, k, q * P:(q + 1) * P],
                                           mask_bias[:, bass.ds(b * QT + q, 1), k * P:(k + 1) * P]
                                           .rearrange("p t n -> p (t n)"), eye_bf[:, :],
                                           start=False, stop=q == QT - 1)
                mm.then_inc(ly["p2_done"], 1)

            def pv(b, par, g):
                pe.wait_ge(ly["exp_done"], 8 * b + 2 * g + 2)
                if g == 0:
                    pe.wait_ge(ly["v_copied"], b + 1)
                for k in range(QT):
                    for i in range(HG):
                        mm = pe.matmul(M[O_BANK[g]][32 * i:32 * i + 32, 0:S], Vt[par][:, k, HG * g + i, :],
                                       Pt[g][:, i, k * S:(k + 1) * S], start=(k == 0), stop=(k == QT - 1))
                mm.then_inc(ly["pv_done"], 1)

            def m_turn(b, par, half, bank):
                pe.wait_ge(ly["m_parts"], 2 * b + half + 1)
                for g in range(2):
                    for q in range(QT):
                        h = 8 * half + HG * g
                        mm = pe.transpose(M16[bank][0:MROWS, g * S + q * P:g * S + (q + 1) * P],
                                          mparts[par][:, q, h:h + HG, :].rearrange("p h c -> p (h c)"), eye16[:, :])
                mm.then_inc(ly["mT_done"], 1)

            def slot_fn(b, par, s):
                new, nxt, cur, old, older = (exists(s, d) for d in (2, 1, 0, -1, -2))
                par1 = 1 - par

                def pair(i):
                    if nxt:
                        p1(b + 1, par1, 2 * i)
                        p1(b + 1, par1, 2 * i + 1)
                    if cur:
                        p2(b, par, i)

                pair(0)
                if new:
                    pe.wait_ge(ly["xn_ready"], b + 3)
                    if older:
                        pe.wait_ge(ly["x_added"], b - 1)
                    elif old:
                        pe.wait_ge(ly["o_copied"], 4 * b - 2)
                    elif cur:
                        pe.wait_ge(ly["mT_copied"], 2 * b + 1)
                    elif nxt:
                        pe.wait_ge(ly["k_copied"], b + 2)
                    for q in range(QT):
                        mm = pe.transpose(M[0][:, q * P:(q + 1) * P], xn[par][:, q, :], eye[:, :])
                    mm.then_inc(ly["xnT_done"], 1)
                pair(1)
                if old:
                    pe.wait_ge(ly["o_copied"], 4 * b - 1)
                    pv(b - 1, par1, 3)
                if new:
                    pe.wait_ge(ly["xnT_copied"], b + 3)
                    pe.matmul(M[0][:, 0:S], W["q", ly["index"]][:, :], xnT[:, :], start=True,
                              stop=True).then_inc(ly["q_done"], 1)
                if cur:
                    if old:
                        pe.wait_ge(ly["o_copied"], 4 * b)
                    m_turn(b, par, 1, 1)
                pair(2)
                if new:
                    pe.wait_ge(ly["q_copied"], b + 3)
                    pe.wait_ge(ly["ctx_loaded"], 16 * b + 48)
                    pe.matmul(M[0][:, 0:S], W["k", ly["index"]][:, :], ctxT[par][:, :], start=True,
                              stop=True).then_inc(ly["k_done"], 1)
                pair(3)
                if cur:
                    pe.wait_ge(ly["mT_copied"], 2 * b + 2)
                    pv(b, par, 0)
                if nxt:
                    if new:
                        pe.wait_ge(ly["k_copied"], b + 3)
                    else:
                        pe.wait_ge(ly["x_added"], b - 1)
                    for k in range(QT):
                        mm = pe.matmul(M[0][:, k * D:(k + 1) * D], ctxT[par1][:, k * P:(k + 1) * P],
                                       W["v", ly["index"]][:, :], start=True, stop=True)
                    mm.then_inc(ly["v_done"], 1)

                def o_turn(q):
                    for g in range(NG):
                        mm = pe.transpose(M[1][:, g * P:(g + 1) * P], Osb[par1][:, g, q * P:(q + 1) * P], eye[:, :])
                    mm.then_inc(ly["ot_done"], 1)

                if old:
                    pe.wait_ge(ly["o_copied"], 4 * b + 1 if cur else 4 * b)
                    o_turn(0)
                pair(4)
                if nxt:
                    pe.wait_ge(ly["v_copied"], b + 2)
                    m_turn(b + 1, par1, 0, 0)
                if old:
                    pe.wait_ge(ly["ot_norm"], 2 * b - 1)
                    o_turn(1)
                pair(5)
                if cur:
                    if nxt:
                        pe.wait_ge(ly["mT_copied"], 2 * b + 3)
                    else:
                        pe.wait_ge(ly["x_added"], b - 1)
                    pv(b, par, 1)
                if old:
                    pe.wait_ge(ly["ot_norm"], 2 * b)
                    for q in range(QT):
                        mm = pe.transpose(M[1][:, q * P:(q + 1) * P], attn[:, q, :], eye[:, :])
                    mm.then_inc(ly["aT_done"], 1)
                pair(6)
                if old:
                    pe.wait_ge(ly["aT_copied"], b)
                    if cur:
                        pe.wait_ge(ly["o_copied"], 4 * b + 2)
                    else:
                        pe.wait_ge(ly["x_added"], b - 1)
                    for q in range(QT):
                        mm = pe.matmul(M[0][:, q * D:(q + 1) * D], aT[:, q * P:(q + 1) * P], W["o", ly["index"]][:, :],
                                       start=True, stop=True)
                    mm.then_inc(ly["op_done"], 1)
                pair(7)
                if cur:
                    if old:
                        pe.wait_ge(ly["aT_copied"], b)
                    else:
                        pe.wait_ge(ly["o_copied"], 4 * b + 1)
                    pv(b, par, 2)

            slots_loop(pe, slot_fn)

        def attention_on_scalar(act, ly):
            def o_copy(b, par, g):
                act.wait_ge(ly["pv_done"], 4 * b + g + 1)
                act.activation(Osb[par][:, g, :], M[O_BANK[g]][:, 0:S], ACT.Copy).then_inc(ly["o_copied"], 1)

            def slot_fn(b, par, s):
                new, nxt, cur, old, older = (exists(s, d) for d in (2, 1, 0, -1, -2))

                def exp(i):
                    if not cur:
                        return
                    if i % 2 == 0 and old:
                        act.wait_ge(ly["pv_done"], 4 * b - 3 + i // 2)
                    act.wait_ge(ly["p2_done"], 8 * b + i + 1)
                    act.activation(Pt[i // 2][:, 2 * (i % 2):2 * (i % 2) + 2, :].rearrange("p a n -> p (a n)"),
                                   S2[i % 2][:, :, :, :].rearrange("p a k n -> p (a k n)"), ACT.Exp,
                                   scale=1.0 / SC).then_inc(ly["exp_done"], 1)

                def m_copy(bb, pp, half, bank):
                    act.wait_ge(ly["mT_done"], 2 * bb + half + 1)
                    act.activation(Qt[pp][M0:M0 + MROWS, 2 * half:2 * half + 2, :].rearrange("p g n -> p (g n)"),
                                   M16[bank][0:MROWS, 0:2 * S], ACT.Copy).then_inc(ly["mT_copied"], 1)

                exp(0)
                if new:
                    act.wait_ge(ly["xnT_done"], b + 3)
                    if nxt:
                        act.wait_ge(ly["q_done"], b + 2)
                    act.activation(xnT[:, :], M[0][:, 0:S], ACT.Copy).then_inc(ly["xnT_copied"], 1)
                exp(1)
                if old:
                    o_copy(b - 1, 1 - par, 3)
                if new:
                    act.wait_ge(ly["q_done"], b + 3)
                    if nxt:
                        act.wait_ge(ly["q_lo"], b + 2)
                    act.activation(qf[:, :], M[0][:, 0:S], ACT.Identity, bias=qkbs[:, 0:1] if ly["bias"] else 0.0,
                                   scale=QK / float(np.sqrt(DH))).then_inc(ly["q_copied"], 1)
                    act.wait_ge(ly["q_copied"], b + 3)
                    if cur:
                        act.wait_ge(ly["q_tile"][1], 48 * b + 48)
                    act.activation(q_hi[par][:, :], qf[:, :], ACT.Copy).then_inc(ly["q_hi"], 1)
                if cur:
                    m_copy(b, par, 1, 1)
                exp(2)
                if new:
                    act.wait_ge(ly["k_done"], b + 3)
                    if nxt:
                        act.wait_ge(ly["k_lo"], b + 2)
                    act.activation(kf[:, :], M[0][:, 0:S], ACT.Identity, bias=qkbs[:, 1:2] if ly["bias"] else 0.0,
                                   scale=QK).then_inc(ly["k_copied"], 1)
                    act.wait_ge(ly["k_copied"], b + 3)
                    if nxt:
                        act.wait_ge(ly["k_rep"], 48 * (b + 2))
                    act.activation(k_hi[:, :], kf[:, :], ACT.Copy).then_inc(ly["k_hi"], 1)
                exp(3)
                if cur:
                    if older:
                        act.wait_ge(ly["ot_done"], 2 * b - 2)
                    o_copy(b, par, 0)
                exp(4)
                if nxt:
                    m_copy(b + 1, 1 - par, 0, 0)
                exp(5)
                if cur:
                    o_copy(b, par, 1)
                if old:
                    act.wait_ge(ly["aT_done"], b)
                    if older:
                        act.wait_ge(ly["op_done"], b - 1)
                    act.activation(aT[:, :], M[1][:, 0:S], ACT.Copy).then_inc(ly["aT_copied"], 1)
                exp(6)
                exp(7)
                if cur:
                    o_copy(b, par, 2)

            slots_loop(act, slot_fn)

        def carrier_on_vector(v):
            v.tensor_copy(carried_v[:, :], mhalf[:, :])

        def norm_stats(v, b, own, var):
            for q in range(QT):
                i = v.bn_stats(st6[:, q, :], X[:, b * QT + q, :])
            i.then_inc(own, 1)
            v.wait_ge(own, 2 * b + 1)
            carrier_on_vector(v)
            for q in range(QT):
                i = v.bn_aggr(mv[:, q, :], st6[:, q, :])
            i.then_inc(own, 1)
            v.wait_ge(own, 2 * b + 2)
            v.tensor_scalar(ve[:, :], mv[:, :, 1], EPS, None, ALU.add).then_inc(var, 1)

        def norm_apply(v, b, dst, rst, done):
            v.wait_ge(rst, b + 1)
            for q in range(QT):
                i = v.tensor_scalar(dst[:, q, :], X[:, b * QT + q, :], mv[:, q, 0:1], rstd[:, q:q + 1],
                                    ALU.subtract, ALU.mult)
            i.then_inc(done, 1)

        def norm_root(pool, b, var, rst):
            pool.wait_ge(var, b + 1)
            pool.tensor_tensor(rstd[:, :], ve[:, :], mhalf[:, :], ALU.pow).then_inc(rst, 1)

        def attention_on_vector(v, ly):
            def reduce(b, par, h):
                v.wait_ge(ly["p1_done"], 16 * b + h + 1)
                v.tensor_reduce(nm[par][:, :, h], S1[h % 2][:, :, :], AX.X, ALU.max, negate=True)\
                 .then_inc(ly["max_done"], 1)

            def parts(b, par, half):
                hs = slice(8 * half, 8 * half + 8)
                base = 6 * b + 3 * half
                v.wait_ge(ly["max_done"], 16 * b + 8 * half + 8)
                if not (isinstance(b, int) and b < 2):
                    v.wait_ge(ly["mT_done"], 2 * b - 3 + half)
                v.tensor_scalar(mparts[par][:, :, hs, 0], nm[par][:, :, hs], 1.0 / MROW, None, ALU.mult)\
                 .then_inc(ly["own"], 1)
                v.wait_ge(ly["own"], base + 1)
                v.scalar_tensor_tensor(mr[:, :, :], nm[par][:, :, hs], 1.0 / MROW, mparts[par][:, :, hs, 0],
                                       ALU.mult, ALU.subtract).then_inc(ly["own"], 1)
                v.wait_ge(ly["own"], base + 2)
                v.tensor_copy(mparts[par][:, :, hs, 1], mr[:, :, :]).then_inc(ly["own"], 1)
                v.wait_ge(ly["own"], base + 3)
                v.tensor_tensor(mparts[par][:, :, hs, 2], mr[:, :, :], mparts[par][:, :, hs, 1],
                                ALU.subtract).then_inc(ly["m_parts"], 1)

            def zero_m(b, par, half):
                if not (isinstance(b, int) and b < 2):
                    v.wait_ge(ly["p2_done"], 8 * (b - 2) + 4 * half + 4)
                v.memset(Qt[par][M0:M0 + MROWS, 2 * half:2 * half + 2, :], 0.0).then_inc(ly["m_zeroed"], 1)

            def o_norm(b, q):
                ot = M[1][:, :].rearrange("p (h r) -> p h r", r=32)
                v.wait_ge(ly["ot_done"], 2 * b + q + 1)
                if ly["position"]:
                    v.tensor_scalar(rsum[:, q, :], ot[:, :, DH], 1.0, None, ALU.add).then_inc(ly["ot_sum"], 1)
                    v.wait_ge(ly["ot_sum"], 2 * b + q + 1)
                    v.reciprocal(rc[:, q, :], rsum[:, q, :]).then_inc(ly["o_rc"], 1)
                else:
                    v.reciprocal(rc[:, q, :], ot[:, :, DH]).then_inc(ly["o_rc"], 1)
                v.wait_ge(ly["o_rc"], 2 * b + q + 1)
                if q == 0 and not (isinstance(b, int) and b == 0):
                    v.wait_ge(ly["aT_done"], b)
                v.tensor_tensor(attn[:, q, :].rearrange("p (h d) -> p h d", d=DH), ot[:, :, 0:DH],
                                rc[:, q, :].unsqueeze(2).to_broadcast([P, H, DH]), ALU.mult).then_inc(ly["ot_norm"], 1)

            def slot_fn(b, par, s):
                nxt, cur, old = (exists(s, d) for d in (1, 0, -1))
                ahead = s is None or s <= 5

                def r(i):
                    if nxt:
                        reduce(b + 1, 1 - par, 2 * i)
                        reduce(b + 1, 1 - par, 2 * i + 1)

                r(0)
                if nxt:
                    zero_m(b + 1, 1 - par, 1)
                if ahead:
                    norm_stats(v, b + 3, ly["norm_own"], ly["xvar"])
                r(1)
                if old and ly["bias"]:
                    for q in range(QT):
                        i = v.tensor_tensor(X[:, (b - 1) * QT + q, :], X[:, (b - 1) * QT + q, :], ob[:, :], ALU.add)
                    i.then_inc(ly["x_biased"], 1)
                r(2)
                if ahead:
                    if nxt:
                        v.wait_ge(ly["xnT_done"], b + 2)
                    norm_apply(v, b + 3, xn[1 - par], ly["xrstd"], ly["xn_ready"])
                r(3)
                if nxt:
                    parts(b + 1, 1 - par, 0)
                    v.wait_ge(ly["v_done"], b + 2)
                    if old:
                        v.wait_ge(ly["pv_done"], 4 * b)
                    src = M[0][:, 0:S].rearrange("p (k h d) -> p k h d", k=QT, h=H)
                    dst = Vt[1 - par]
                    if ly["bias"]:
                        for k in range(QT):
                            i = v.tensor_tensor(dst[:, k, :, 0:DH], src[:, k], vb[:, :].rearrange("p (h d) -> p h d", d=DH),
                                                ALU.add)
                    else:
                        i = v.tensor_copy(dst[:, :, :, 0:DH], src)
                    i.then_inc(ly["v_copied"], 1)
                r(4)
                if exists(s, 2):
                    zero_m(b + 2, par, 0)
                if old:
                    o_norm(b - 1, 0)
                r(5)
                if old:
                    o_norm(b - 1, 1)
                r(6)
                r(7)
                if nxt:
                    parts(b + 1, 1 - par, 1)
                if old:
                    v.wait_ge(ly["op_done"], b)
                    if ly["bias"]:
                        v.wait_ge(ly["x_biased"], b)
                    for q in range(QT):
                        x = X[:, (b - 1) * QT + q, :]
                        i = v.tensor_tensor(x, M[0][:, q * D:(q + 1) * D], x, ALU.add)
                    i.then_inc(ly["x_added"], 1)

            slots_loop(v, slot_fn)

        def attention_on_gpsimd(pool, ly):
            def slot_fn(b, par, s):
                new, nxt, cur = (exists(s, d) for d in (2, 1, 0))
                if s is None or s <= 5:
                    norm_root(pool, b + 3, ly["xvar"], ly["xrstd"])
                if not new:
                    return
                if cur:
                    pool.wait_ge(ly["q_tile"][1], 48 * b + 48)
                pool.wait_ge(ly["q_hi"], b + 3)
                pool.tensor_tensor(q_lo[par][:, :], qf[:, :], q_hi[par][:, :], ALU.subtract).then_inc(ly["q_lo"], 1)
                if nxt:
                    pool.wait_ge(ly["k_rep"], 48 * (b + 2))
                pool.wait_ge(ly["k_hi"], b + 3)
                pool.tensor_tensor(k_lo[:, :], kf[:, :], k_hi[:, :], ALU.subtract).then_inc(ly["k_lo"], 1)
                for half in range(2):
                    if cur:
                        pool.wait_ge(ly["p2_done"], 8 * b + 4 * half + 4)
                    if half == 0:
                        pool.wait_ge(ly["k_rep"], 48 * (b + 3))
                    gs = slice(2 * half, 2 * half + 2)
                    for i in range(HG):
                        dst = Kt[par][0:M0, :, :].rearrange("p (g i) n -> p g i n", i=HG)[:, gs, i, :]
                        if i == 0:
                            pool.tensor_tensor(dst, k_rep[0:M0, gs, :], head_mask[0:M0, 0:1].unsqueeze(2)
                                               .to_broadcast([M0, 2, S]), ALU.mult)
                            continue
                        kk = pool.tensor_scalar(dst, k_rep[0:M0, gs, :], head_mask[0:M0, i:i + 1], 1.0,
                                                ALU.mult, ALU.mult)
                    kk.then_inc(ly["k_tile"], 1)

            slots_loop(pool, slot_fn)

        def attention_on_sync(sp, ly):
            def slot_fn(b, par, s):
                new, nxt, cur = (exists(s, d) for d in (2, 1, 0))
                if not new:
                    return
                if cur:
                    sp.wait_ge(ly["v_done"], b + 1)
                    sp.wait_ge(ly["k_done"], b + 1)
                sp.dma_start(ctxT[par][:, :], t["ctxT"][:, b + 2, :]).then_inc(ly["ctx_loaded"], 16)
                sp.wait_ge(ly["k_lo"], b + 3)
                if nxt:
                    sp.wait_ge(ly["k_tile"], 2 * b + 4)
                for block, src in enumerate((k_hi, k_lo, k_hi)):
                    sp.dma_start(k_rep[32 * block:32 * block + 32, :, :], src[:, :]).then_inc(ly["k_rep"], 16)
                for half in range(2):
                    if cur:
                        sp.wait_ge(ly["p2_done"], 8 * b + 4 * half + 4)
                    if half == 0:
                        sp.wait_ge(ly["q_lo"], b + 3)
                    for block, src in enumerate((q_hi, q_hi, q_lo)):
                        sp.dma_start(Qt[par][32 * block:32 * block + 32, 2 * half:2 * half + 2, :],
                                     src[par][64 * half:64 * half + 64, :]).then_inc(ly["q_tile"][half], 16)
                    if ly["position"]:
                        sp.dma_start(Kt[par][PB0:PB0 + PARTS, 8 * half:8 * half + 8, :],
                                     pos_dram[b + 2, 8 * half:8 * half + 8, :, :].rearrange("h c n -> c h n")) \
                          .then_inc(ly["k_pos"][half][par], 16)

            slots_loop(sp, slot_fn)


        def gate_on_vector(v):
            v.wait_ge(mk["bias"], 2)
            v.tensor_reduce(mask_min[:, :], mask_bias[:, :, :].rearrange("p t n -> p (t n)"), AX.X, ALU.min).then_inc(mk["min"], 1)
            v.wait_ge(mk["min"], 1)
            v.tensor_scalar(mask_hit[:, :], mask_min[:, :], 0.0, None, ALU.is_lt).then_inc(mk["hit"], 1)
            v.wait_ge(mk["count"], 1)
            v.tensor_scalar(mask_any[:, :], S2[0][:, 0, 0, 0:1], 1.0, None, ALU.min).then_inc(mk["any"], 1)
            v.wait_ge(ly[0]["x_added"], B)
            for b in range(B + 1):
                if b < B:
                    norm_stats(v, b, moe["norm_own"], moe["var"])
                    if b >= 2:
                        v.wait_ge(moe["xT"], b - 1)
                        v.wait_ge(moe["xcopy"], b - 1)
                    norm_apply(v, b, xn[b % 2], moe["rstd"], moe["xn"])
                if b >= 1:
                    c = b - 1
                    v.wait_ge(moe["gm"], b)
                    for q in range(QT):
                        i = v.tensor_tensor(logit[:, c * QT + q, :], S1[c % 2][:, q, 0:NE], bg[:, :], ALU.add)
                    i.then_inc(moe["logit"], 1)

        def gate_on_gpsimd(pool):
            for b in range(B):
                norm_root(pool, b, moe["var"], moe["rstd"])

        def gate_on_tensor(pe):
            pe.wait_ge(mk["hit"], 1)
            pe.wait_ge(ly[0]["exp_done"], 8 * B)
            pe.matmul(S2[0][:, 0, 0, 0:1], ones32[:, :], mask_hit[:, :], start=True, stop=True).then_inc(mk["count"], 1)
            for b in range(B + 1):
                if b < B:
                    pe.wait_ge(moe["xn"], b + 1)
                    if b >= 2:
                        pe.wait_ge(moe["xTc"], b - 1)
                    for q in range(QT):
                        mm = pe.transpose(M[b % 2][:, q * P:(q + 1) * P], xn[b % 2][:, q, :], eye[:, :])
                    mm.then_inc(moe["xT"], 1)
                if b >= 1:
                    c = b - 1
                    pe.wait_ge(moe["xTc"], b)
                    if c >= 2:
                        pe.wait_ge(moe["logit"], c - 1)
                    for q in range(QT):
                        mm = pe.matmul(S1[c % 2][:, q, 0:NE], gT[c % 2][:, q * P:(q + 1) * P], wg[:, :],
                                       start=True, stop=True)
                    mm.then_inc(moe["gm"], 1)
            pe.wait_ge(moe["onehot"], 1)
            oh = onehot[:, :, :].rearrange("p t e -> p (t e)")
            pe.matmul(M[0][:, 0:P], before[:, :], oh, start=True, stop=True).then_inc(moe["ranks"], 1)
            pe.matmul(M[1][:, 0:P], ones32[:, :], oh, start=True, stop=True).then_inc(moe["ranks"], 1)

        def gate_on_scalar(act):
            for b in range(B):
                act.wait_ge(moe["xT"], b + 1)
                if b >= 2:
                    act.wait_ge(moe["gm"], b - 1)
                act.activation(gT[b % 2][:, :], M[b % 2][:, 0:S], ACT.Copy).then_inc(moe["xTc"], 1)
                act.activation(xn2[:, b * QT:(b + 1) * QT, :].rearrange("p q d -> p (q d)"),
                               xn[b % 2][:, :, :].rearrange("p q d -> p (q d)"), ACT.Copy).then_inc(moe["xcopy"], 1)
            act.wait_ge(moe["r"], 5)
            act.activation(t2[:, :, :].rearrange("p t e -> p (t e)"), t1[:, :, :].rearrange("p t e -> p (t e)"),
                           ACT.Exp).then_inc(moe["exp"], 1)

        def route_on_vector(v):
            count = [0]

            def step(ins):
                ins.then_inc(moe["r"], 1)
                count[0] += 1
                v.wait_ge(moe["r"], count[0])

            v.wait_ge(moe["logit"], B)
            te = [P, NT, NE]
            num = route_c[:, 0, :].rearrange("p (t e) -> p t e", e=NE)
            step(v.tensor_reduce(top[:, :], logit[:, :, :], AX.X, ALU.max))
            step(v.tensor_tensor(t1[:, :, :], logit[:, :, :], top[:, :].unsqueeze(2).to_broadcast(te), ALU.is_equal))
            step(v.tensor_tensor(t2[:, :, :], t1[:, :, :], num, ALU.mult))
            step(v.tensor_reduce(first[:, :], t2[:, :, :], AX.X, ALU.min))
            v.tensor_tensor(onehot[:, :, :], num, first[:, :].unsqueeze(2).to_broadcast(te), ALU.is_equal).then_inc(moe["onehot"], 1)
            step(v.tensor_tensor(t1[:, :, :], logit[:, :, :], top[:, :].unsqueeze(2).to_broadcast(te), ALU.subtract))
            v.wait_ge(moe["ranks"], 2)
            step(v.tensor_copy(tot[:, :, :], M[1][:, 0:P].rearrange("p (t e) -> p e t", e=NE)))
            step(v.tensor_tensor_scan(cum[:, :, :].rearrange("p e t -> p (e t)"), route_c[:, 1, :],
                                      tot[:, :, :].rearrange("p e t -> p (e t)"), 0.0, ALU.mult, ALU.add))
            step(v.tensor_scalar(cnt_i[:, :], cum[:, :, NT - 1], float(P - 1), None, ALU.add))
            step(v.tensor_scalar(cnt_s[:, :], cnt_i[:, :], 7, None, ALU.arith_shift_right))
            step(v.tensor_copy(ntile[:, :], cnt_s[:, :]))
            step(v.tensor_tensor_scan(tend[:, :], ones32[:, 0:NE], ntile[:, :], 0.0, ALU.mult, ALU.add))
            step(v.tensor_tensor(tstart[:, :], tend[:, :], ntile[:, :], ALU.subtract))
            step(v.tensor_tensor(rbase[:, :, :], cum[:, :, :], tot[:, :, :], ALU.subtract))
            step(v.scalar_tensor_tensor(rbase[:, :, :], tstart[:, :].unsqueeze(2).to_broadcast([P, NE, NT]), float(P),
                                        rbase[:, :, :], ALU.mult, ALU.add))
            step(v.tensor_tensor(cum[:, :, :], M[0][:, 0:P].rearrange("p (t e) -> p e t", e=NE), rbase[:, :, :], ALU.add))
            step(v.tensor_tensor(cum[:, :, :], cum[:, :, :], onehot[:, :, :].rearrange("p t e -> p e t"), ALU.mult))
            step(v.tensor_reduce(slotf[:, :], cum[:, :, :].rearrange("p e t -> p t e"), AX.X, ALU.add))
            v.tensor_copy(slot[:, :], slotf[:, :]).then_inc(moe["slots"], 1)
            je = [P, SLOT_TILES, NE]
            step(v.tensor_tensor(cmp[:, :, :], tend[:, :].unsqueeze(1).to_broadcast(je),
                                 route_c[:, 2, 0:SLOT_TILES].unsqueeze(2).to_broadcast(je), ALU.is_le))
            step(v.tensor_reduce(expf[:, :], cmp[:, :, :], AX.X, ALU.add))
            v.tensor_scalar(expert[:, :], expf[:, :], float(NE - 1), None, ALU.min).then_inc(moe["slots"], 1)
            v.wait_ge(moe["exp"], 1)
            step(v.tensor_reduce(gsum[:, :], t2[:, :, :], AX.X, ALU.add))
            v.reciprocal(gate[:, :], gsum[:, :]).then_inc(moe["gate"], 1)

        def scatter_on_gpsimd(pool):
            pool.wait_ge(moe["slots"], 1)
            pool.wait_ge(moe["xcopy"], B)
            pool.wait_ge(moe["zfill"], 16)
            for i in range(NT):
                pool.indirect_dma_start(xs_dram, bass.IndirectOffsetOnAxis(ap=slot[:, i:i + 1].bitcast(U32), axis=0),
                                        xn2[:, i, :], None).then_inc(moe["scattered"], 16)

        def gather_on_gpsimd(pool):
            pool.wait_ge(moe["stored0"], 16 * ((SLOT_TILES + 1) // 2))
            pool.wait_ge(moe["stored1"], 16 * (SLOT_TILES // 2))
            for i in range(NT):
                pool.indirect_dma_start(yg[:, i, :], None, ys_dram,
                                        bass.IndirectOffsetOnAxis(ap=slot[:, i:i + 1].bitcast(U32), axis=0)) \
                    .then_inc(moe["gathered"], 16)

        def tiles_loop(eng, fn):
            fn(0, 0, True)
            fn(1, 1, True)
            with eng.Fori(1, SLOT_TILES // 2) as i:
                for par in range(2):
                    fn(2 * i + par, par, False)
            fn(SLOT_TILES - 1, 0, False)

        def experts_on_sync(sp):
            sp.wait_ge(moe["scattered"], 16 * NT)
            sp.wait_ge(moe["slots"], 2)

            def load(j, par, start):
                if not start:
                    sp.wait_ge(moe["tT"], j - 1)
                sp.dma_start(xt[par][:, :], xs_dram.rearrange("(j p) d -> j p d", p=P)[j, :, :]).then_inc(moe[f"xt{par}"], 16)
            tiles_loop(sp, load)

        def stores_on_scalar_queue(eng, j, par):
            eng.wait_ge(moe["ysb"], j + 1)
            eng.dma_start(ys_dram.rearrange("(j p) d -> j p d", p=P)[j, :, :], ysb[par][:, :]) \
                .then_inc(moe[f"stored{par}"], 16)

        def experts_on_tensor(pe):
            pe.wait_ge(moe["slots"], 2)
            pe.wait_ge(moe["split"], 8)
            pe.wait_ge(moe["brows"], 16 * 6)

            def tile(j, par, start):
                e = pe.value_load(expert[0:1, bass.ds(j, 1)], min_val=0, max_val=NE - 1)
                pe.wait_ge(moe[f"xt{par}"], 8 * (j - par) + 16)
                if not start:
                    pe.wait_ge(moe["x_lo"], j - 1)
                pe.transpose(M[par][:, 0:P], xt[par][:, :], eye[:, :]).then_inc(moe["tT"], 1)
                pe.wait_ge(moe["x_lo"], j + 1)
                if not start:
                    pe.wait_ge(moe["h_lo"], j - 1)
                hb = S1[par][:, :, :].rearrange("p q n -> p (q n)")
                for c in range(HC):
                    o = hb[:, c * P:(c + 1) * P]
                    w = bass.ds(e * HID + c * P, P)
                    pe.matmul(o, w1_hi[:, w], x_hi[par][:, :], start=True, stop=False)
                    pe.matmul(o, w1_hi[:, w], x_lo[par][:, :], start=False, stop=False)
                    pe.matmul(o, w1_lo[:, w], x_hi[par][:, :], start=False, stop=False)
                    mm = pe.matmul(o, b1rows[:, w], ones16[:, :], start=False, stop=True)
                mm.then_inc(moe["h"], 1)
                pe.wait_ge(moe["h_lo"], j + 1)
                if not start:
                    pe.wait_ge(moe["ysb"], j - 1)
                o = S2[par][:, 0, 0, 0:D]
                for c in range(HC):
                    w = bass.ds(e * HID + c * D, D)
                    hs = slice(c * P, (c + 1) * P)
                    pe.matmul(o, h_hi[par][:, hs], w2_hi[:, w], start=(c == 0), stop=False)
                    pe.matmul(o, h_lo[par][:, hs], w2_hi[:, w], start=False, stop=False)
                    pe.matmul(o, h_hi[par][:, hs], w2_lo[:, w], start=False, stop=False)
                pe.matmul(o, ones16[:, :], b2rows[:, bass.ds(e * D, D)], start=False, stop=True).then_inc(moe["y"], 1)
            tiles_loop(pe, tile)

        def experts_on_scalar(act):
            def tile(j, par, start):
                act.wait_ge(moe["tT"], j + 1)
                if not start:
                    act.wait_ge(moe["h"], j - 1)
                act.activation(x_hi[par][:, :], M[par][:, 0:P], ACT.Copy).then_inc(moe["x_hi"], 1)
                act.wait_ge(moe["h"], j + 1)
                if not start:
                    act.wait_ge(moe["h_lo"], j - 1)
                    act.wait_ge(moe["y"], j - 1)
                hb = S1[par][:, :, :].rearrange("p q n -> p (q n)")
                act.activation(hf[par][:, :], hb, ACT.Silu, scale=1.0 / WS).then_inc(moe["hf"], 1)
                act.wait_ge(moe["hf"], j + 1)
                act.activation(h_hi[par][:, :], hf[par][:, :], ACT.Copy).then_inc(moe["h_hi"], 1)
                act.wait_ge(moe["y"], j + 1)
                if not start:
                    act.wait_ge(moe[f"stored{par}"], 8 * (j - par))
                act.activation(ysb[par][:, :], S2[par][:, 0, 0, 0:D], ACT.Copy, scale=1.0 / WS).then_inc(moe["ysb"], 1)
                stores_on_scalar_queue(act, j, par)
            tiles_loop(act, tile)

        def experts_on_vector(v):
            def tile(j, par, start):
                v.wait_ge(moe["x_hi"], j + 1)
                if not start:
                    v.wait_ge(moe["h"], j - 1)
                v.tensor_tensor(x_lo[par][:, :], M[par][:, 0:P], x_hi[par][:, :], ALU.subtract).then_inc(moe["x_lo"], 1)
                v.wait_ge(moe["h_hi"], j + 1)
                if not start:
                    v.wait_ge(moe["y"], j - 1)
                v.tensor_tensor(h_lo[par][:, :], hf[par][:, :], h_hi[par][:, :], ALU.subtract).then_inc(moe["h_lo"], 1)
            tiles_loop(v, tile)
            v.wait_ge(moe["gate"], 1)
            for i in range(NT):
                if i % QT == 0:
                    v.wait_ge(moe["gathered"], 16 * NT)
                ii = v.scalar_tensor_tensor(X[:, i, :], yg[:, i, :], gate[:, i:i + 1], X[:, i, :], ALU.mult, ALU.add)
            ii.then_inc(moe["x"], 1)
            v.wait_ge(moe["x"], 1)

        def split_on_gpsimd(pool):
            for n in range(4):
                hi, lo = ((w1_hi, w1_lo), (w2_hi, w2_lo))[n // 2]
                cols = slice((n % 2) * 2048, (n % 2) * 2048 + 2048)
                pool.wait_ge(moe[f"wraw{n % 2}"], 16 * (n // 2) + 16)
                pool.tensor_scalar(wraw[n % 2][:, :], wraw[n % 2][:, :], WS, 1.0, ALU.mult, ALU.mult) \
                    .then_inc(moe["split_own"], 1)
                pool.wait_ge(moe["split_own"], 2 * n + 1)
                pool.tensor_copy(hi[:, cols], wraw[n % 2][:, :]).then_inc(moe["split_own"], 1)
                pool.wait_ge(moe["split_own"], 2 * n + 2)
                pool.tensor_tensor(lo[:, cols], wraw[n % 2][:, :], hi[:, cols], ALU.subtract).then_inc(moe["split"], 2)

        def weights_on_sync(sp):
            sp.wait_ge(mk["bias"], 2)
            for n in range(4):
                src = (t["w1"], t["w2"])[n // 2]
                if n >= 2:
                    sp.wait_ge(moe["split"], 2 * n - 2)
                sp.dma_start(wraw[n % 2][:, :], src[:, (n % 2) * 2048:(n % 2) * 2048 + 2048]).then_inc(moe[f"wraw{n % 2}"], 16)

        def batches_loop(eng, fn):
            fn(0, 0, True)
            fn(1, 1, True)
            with eng.Fori(1, B // 2) as i:
                for par in range(2):
                    fn(2 * i + par, par, False)

        def ffn_on_vector(v):
            v.wait_ge(ly[1]["x_added"], B)

            def batch(b, par, start):
                norm_stats(v, b, ff["norm_own"], ff["var"])
                if not start:
                    v.wait_ge(ff["xT"], b - 1)
                norm_apply(v, b, xn[par], ff["rstd"], ff["xn"])
                v.wait_ge(ff["yc"], b + 1)
                base = (2 * STEPS - 1) * b
                v.tensor_scalar(acc[:, :], ymem[:, :], 1.0, None, ALU.is_gt).then_inc(ff["own"], 1)
                for k in range(1, STEPS):
                    src = ymem if k == 1 else mem
                    v.scalar_tensor_tensor(tmp[:, :], src[:, :], BETA, ymem[:, :], ALU.mult, ALU.add).then_inc(ff["own"], 1)
                    v.wait_ge(ff["own"], base + 2 * k)
                    v.scalar_tensor_tensor(mem[:, :], src[:, :], 1.0, tmp[:, :], ALU.is_gt, ALU.subtract, reverse1=True) \
                        .then_inc(ff["own"], 1)
                    v.wait_ge(ff["own"], base + 2 * k + 1)
                    i = v.scalar_tensor_tensor(acc[:, :], mem[:, :], 1.0, acc[:, :], ALU.is_gt, ALU.add)
                i.then_inc(ff["acc"], 1)
                v.wait_ge(ff["acc"], b + 1)
                if not start:
                    v.wait_ge(ff[f"stored{par}"], 8 * (b - par))
                for q in range(QT):
                    i = v.scalar_tensor_tensor(fin[par][:, q, :], acc[:, q * D:(q + 1) * D], 1.0 / STEPS,
                                               X[:, b * QT + q, :], ALU.mult, ALU.add)
                i.then_inc(ff["out"], 1)
            batches_loop(v, batch)

        def ffn_on_gpsimd(pool):
            batches_loop(pool, lambda b, par, start: norm_root(pool, b, ff["var"], ff["rstd"]))

        def ffn_on_tensor(pe):
            def batch(b, par, start):
                pe.wait_ge(ff["xn"], b + 1)
                if not start or par:
                    pe.wait_ge(ff["xTc"], b)
                for q in range(QT):
                    mm = pe.transpose(M[0][:, q * P:(q + 1) * P], xn[par][:, q, :], eye[:, :])
                mm.then_inc(ff["xT"], 1)
                pe.wait_ge(ff["xTc"], b + 1)
                if not start:
                    pe.wait_ge(ff["relu"], b - 1)
                for c in range(HC):
                    mm = pe.matmul(S2[par][:, c // 2, c % 2, :], wfc[:, c * P:(c + 1) * P], xnT[:, :], start=True, stop=True)
                mm.then_inc(ff["h"], 1)
                pe.wait_ge(ff["sq"], b + 1)
                if not start or par:
                    pe.wait_ge(ff["yc"], b)
                for q in range(QT):
                    for c in range(HC):
                        mm = pe.matmul(M[1][:, q * D:(q + 1) * D], h2[:, c, q * P:(q + 1) * P], wpr[:, c, :],
                                       start=(c == 0), stop=(c == HC - 1))
                mm.then_inc(ff["y"], 1)
            batches_loop(pe, batch)

        def ffn_on_scalar(act):
            def batch(b, par, start):
                act.wait_ge(ff["xT"], b + 1)
                if not start or par:
                    act.wait_ge(ff["h"], b)
                act.activation(xnT[:, :], M[0][:, 0:S], ACT.Copy).then_inc(ff["xTc"], 1)
                act.wait_ge(ff["h"], b + 1)
                flat = hr.rearrange("p c n -> p (c n)")
                act.activation(flat, S2[par][:, :, :, :].rearrange("p a k n -> p (a k n)"), ACT.Relu).then_inc(ff["relu"], 1)
                act.wait_ge(ff["relu"], b + 1)
                if not start or par:
                    act.wait_ge(ff["y"], b)
                act.activation(h2.rearrange("p c n -> p (c n)"), flat, ACT.Square).then_inc(ff["sq"], 1)
                act.wait_ge(ff["y"], b + 1)
                if not start or par:
                    act.wait_ge(ff["acc"], b)
                act.activation(ymem[:, :], M[1][:, 0:S], ACT.Copy).then_inc(ff["yc"], 1)
            batches_loop(act, batch)

        def ffn_on_sync(sp):
            def batch(b, par, start):
                sp.wait_ge(ff["out"], b + 1)
                sp.dma_start(out[b, :, :].rearrange("(q p) d -> p q d", p=P), fin[par][:, :, :]) \
                  .then_inc(ff[f"stored{par}"], 16)
            batches_loop(sp, batch)
            for par in range(2):
                sp.wait_ge(ff[f"stored{par}"], 16 * (B // 2))

        @block.sync
        def _(sp):
            loads = [(X[:, 0:NT, :], t["x"]), (eye[:, :], t["c_eye"]), (head_mask[:, :], t["c_head_mask"])]
            loads += [(W[n, L][:, :], t[f"w{n}{L}"]) for n in "qkvo" for L in range(2)]
            loads += [(qkb[:, :], t["qkb"]), (vb[:, :], t["vb"].partition_broadcast(P)), (ob[:, :], t["ob"].partition_broadcast(P)),
                      (slope[:, :], t["c_slope"]), (before[:, :], t["c_before"]), (route_c[:, :, :], t["c_route"]),
                      (wg[:, :], t["wg"]), (bg[:, :], t["bg"].partition_broadcast(P)), (braw[:, :], t["braw"]),
                      (wfc[:, :], t["wfc"]), (wpr[:, :, :], t["wpr"])]
            for b in range(B):
                loads.append((pos_i[b * H:(b + 1) * H, :], t["pos"][b:b + 1, :].partition_broadcast(H)))
            for dst, src in loads:
                sp.dma_start(dst, src).then_inc(loaded, 16)
            for n in range(2):
                sp.dma_start(wraw[n][:, :].bitcast(I32), t["mask"][:, n * 2048:(n + 1) * 2048]).then_inc(mk["raw"], 16)
            assert len(loads) == N_LOADS
            sp.wait_ge(inited, N_INIT)
            sp.dma_start(xs_dram.rearrange("(j p) d -> p j d", p=P), zero[:, :].unsqueeze(1).to_broadcast([P, SLOT_TILES, D])) \
              .then_inc(moe["zfill"], 16)
            attention_on_sync(sp, ly[0])
            weights_on_sync(sp)
            sp.wait_ge(pos_ready, 1)
            sp.dma_start(pos_dram.rearrange("b h c n -> (b h) c n"), pos_parts[:, :, :]).then_inc(pos_stored, 16)
            sp.wait_ge(moe["bsplit"], 3)
            for c in range(PARTS):
                sp.dma_start(b1rows[c:c + 1, :], bparts[:, c, 0:32]).then_inc(moe["brows"], 16)
                sp.dma_start(b2rows[c:c + 1, :], bparts[:, c, 32:40]).then_inc(moe["brows"], 16)
            experts_on_sync(sp)
            sp.wait_ge(pos_stored, 16)
            attention_on_sync(sp, ly[1])
            ffn_on_sync(sp)

        @block.gpsimd
        def _(pool):
            pool.wait_ge(loaded, 16 * N_LOADS)
            pool.wait_ge(inited, N_INIT)
            pool.wait_ge(mk["raw"], 32)
            for n in range(2):
                pool.tensor_scalar(mask_bias[:, n * NT // 2:(n + 1) * NT // 2, :].rearrange("p t n -> p (t n)"),
                                   wraw[n][:, :].bitcast(I32), 0.0, MASKED, ALU.is_equal, ALU.mult).then_inc(mk["bias"], 1)
            attention_on_gpsimd(pool, ly[0])
            split_on_gpsimd(pool)
            gate_on_gpsimd(pool)
            scatter_on_gpsimd(pool)
            gather_on_gpsimd(pool)
            attention_on_gpsimd(pool, ly[1])
            ffn_on_gpsimd(pool)

        @block.scalar
        def _(act):
            act.wait_ge(loaded, 16 * N_LOADS)
            act.wait_ge(inited, N_INIT)
            attention_on_scalar(act, ly[0])
            gate_on_scalar(act)
            experts_on_scalar(act)
            attention_on_scalar(act, ly[1])
            ffn_on_scalar(act)

        @block.vector
        def _(v):
            v.memset(X[:, NT:NT + QT, :], 0.0).then_inc(inited, 1)
            v.memset(mhalf[:, :], -0.5).then_inc(inited, 1)
            v.memset(zero[:, :], 0.0).then_inc(inited, 1)
            v.memset(ones32[:, :], 1.0).then_inc(inited, 1)
            v.memset(ones16[:, :], 1.0).then_inc(inited, 1)
            v.memset(b1rows[:, :], 0.0).then_inc(inited, 1)
            v.memset(b2rows[:, :], 0.0).then_inc(inited, 1)
            for i in range(2):
                v.memset(Qt[i][M0:P, :, :], MROW).then_inc(inited, 1)
                v.memset(Kt[i][M0:P, :, :], 0.0).then_inc(inited, 1)
                v.memset(Vt[i][:, :, :, :], 0.0).then_inc(inited, 1)
            v.wait_ge(inited, 13)
            for i in range(2):
                v.memset(Vt[i][:, :, :, DH], 1.0).then_inc(inited, 1)
            v.wait_ge(loaded, 16 * N_LOADS)
            for i in range(2):
                for g in range(NG):
                    v.tensor_copy(Kt[i][M0:M0 + MROWS, HG * g:HG * g + HG, :],
                                  head_mask[M0:M0 + MROWS, :].unsqueeze(2).to_broadcast([MROWS, HG, S])).then_inc(inited, 1)
            v.tensor_copy(eye16[:, :], eye[:, :]).then_inc(inited, 1)
            v.tensor_copy(eye_bf[:, :], eye[:, :]).then_inc(inited, 1)
            v.tensor_scalar(qkbs[:, 0:1], qkb[:, 0:1], QK / float(np.sqrt(DH)), None, ALU.mult).then_inc(inited, 1)
            v.tensor_scalar(qkbs[:, 1:2], qkb[:, 1:2], QK, None, ALU.mult).then_inc(inited, 1)
            v.tensor_copy(pos_f[:, :], pos_i[:, :]).then_inc(pos_own, 1)
            v.wait_ge(pos_own, 1)
            v.tensor_scalar(pos_r[:, :], pos_f[:, :], slope[:, 0:1], SC / MROW, ALU.mult, ALU.mult).then_inc(pos_own, 1)
            v.wait_ge(pos_own, 2)
            v.tensor_copy(pos_parts[:, 0, :], pos_r[:, :]).then_inc(pos_own, 1)
            v.wait_ge(pos_own, 3)
            v.tensor_tensor(pos_r[:, :], pos_r[:, :], pos_parts[:, 0, :], ALU.subtract).then_inc(pos_own, 1)
            v.wait_ge(pos_own, 4)
            v.tensor_copy(pos_parts[:, 1, :], pos_r[:, :]).then_inc(pos_own, 1)
            v.wait_ge(pos_own, 5)
            v.tensor_tensor(pos_parts[:, 2, :], pos_r[:, :], pos_parts[:, 1, :], ALU.subtract).then_inc(pos_ready, 1)
            v.tensor_scalar(brest[:, :], braw[:, :], WS, None, ALU.mult).then_inc(moe["bsplit"], 1)
            v.wait_ge(moe["bsplit"], 1)
            v.tensor_copy(bparts[:, 0, :], brest[:, :]).then_inc(pos_own, 1)
            v.wait_ge(pos_own, 6)
            v.tensor_tensor(brest[:, :], brest[:, :], bparts[:, 0, :], ALU.subtract).then_inc(pos_own, 1)
            v.wait_ge(pos_own, 7)
            v.tensor_copy(bparts[:, 1, :], brest[:, :]).then_inc(moe["bsplit"], 1)
            v.wait_ge(moe["bsplit"], 2)
            v.tensor_tensor(bparts[:, 2, :], brest[:, :], bparts[:, 1, :], ALU.subtract).then_inc(moe["bsplit"], 1)
            v.wait_ge(inited, N_INIT)
            attention_on_vector(v, ly[0])
            gate_on_vector(v)
            route_on_vector(v)
            experts_on_vector(v)
            attention_on_vector(v, ly[1])
            ffn_on_vector(v)

        @block.tensor
        def _(pe):
            pe.wait_ge(loaded, 16 * N_LOADS)
            pe.wait_ge(inited, N_INIT)
            attention_on_tensor(pe, ly[0], False)
            gate_on_tensor(pe)
            experts_on_tensor(pe)
            pe.wait_ge(mk["any"], 1)
            any_masked = pe.value_load(mask_any[0:1, 0:1], min_val=0, max_val=1)
            with pe.If(any_masked == 1):
                attention_on_tensor(pe, ly[1], True)
            with pe.Else():
                attention_on_tensor(pe, ly[1], False)
            ffn_on_tensor(pe)


def q_order():
    return [(HG * (2 * hf + g2) + i) * DH + d for hf in range(2) for i in range(HG) for d in range(DH) for g2 in range(2)]


def k_order():
    return [(HG * g + i) * DH + d for i in range(HG) for d in range(DH) for g in range(NG)]


def kernel(**inputs):
    import concourse.bacc as bacc
    from concourse.bass_utils import run_bass_kernel_spmd

    a = {k: np.asarray(v) for k, v in inputs.items()}
    lay = np.ascontiguousarray
    qo, ko = q_order(), k_order()
    arrays = {
        "x": lay(a["x"].reshape(NT, P, D).transpose(1, 0, 2)),
        "ctxT": lay(a["ctx_1024"].transpose(2, 0, 1)),
        "pos": lay(a["itok_BxS2_1_8191"]),
        "qkb": lay(np.stack([a["L0_xattn_wq_b"][qo], a["L0_xattn_wk_b"][ko]], axis=1)),
        "vb": a["L0_xattn_wv_b"], "ob": a["L0_xattn_wo_b"],
        "mask": lay(a["mask_BxSxS2_if1"].reshape(NT, P, S).transpose(1, 0, 2).reshape(P, NT * S)),
        "wg": a["L0_ffn_Wg"], "bg": a["L0_ffn_bg"],
        "w1": lay(a["L0_ffn_W1"].transpose(1, 0, 2).reshape(D, NE * HID)),
        "w2": lay(a["L0_ffn_W2"].reshape(NE, HC, P, D).transpose(2, 0, 1, 3).reshape(P, NE * HID)),
        "braw": lay(np.concatenate([a["L0_ffn_b1"].reshape(P, 32), a["L0_ffn_b2"].reshape(P, 8)], axis=1)),
        "wfc": lay(a["L1_ffn_W_fc"].T),
        "wpr": lay(a["L1_ffn_W_proj"].T.reshape(HC, P, D).transpose(1, 0, 2)),
    }
    for L, names in enumerate((("L0_xattn_wq_w", "L0_xattn_wk_w", "L0_xattn_wv_w", "L0_xattn_wo_w"),
                               ("L1_xattn_W_q", "L1_xattn_W_k", "L1_xattn_W_v", "L1_xattn_W_o"))):
        for n, name in zip("qkvo", names):
            w = a[name].T
            arrays[f"w{n}{L}"] = lay(w[:, qo] if n == "q" else w[:, ko] if n == "k" else w)
    arrays.update(constants())
    nc = bacc.Bacc("TRN2", target_bir_lowering=False, num_devices=1)
    t = {n: nc.dram_tensor(f"in_{n}", v.shape, mybir.dt.from_np(v.dtype), kind="ExternalInput").ap()
         for n, v in arrays.items()}
    out = nc.dram_tensor("out", (B, S, D), F32, kind="ExternalOutput").ap()
    build(nc, t, out)
    r = run_bass_kernel_spmd(nc, [{f"in_{n}": v for n, v in arrays.items()}], core_ids=[0])
    return r.results[0]["out"]
```

```python
from contextlib import ExitStack

import numpy as np

import concourse.bass as bass
from concourse import mybir

F32 = mybir.dt.float32
F16 = mybir.dt.float16
BF16 = mybir.dt.bfloat16
I32 = mybir.dt.int32
U32 = mybir.dt.uint32
ALU = mybir.AluOpType
ACT = mybir.ActivationFunctionType
AX = mybir.AxisListType

P = 128
B, S, D, H = 8, 256, 128, 16
DH = D // H
QT = S // P
NT = B * QT
HG = 4
NG = H // HG
NE, HID = 8, 512
HC = HID // P
EPS = 1e-5
STEPS, BETA = 5, 0.9
W_BLOCKS = 2 * NE * HC
W_CHUNK = W_BLOCKS // B
SLOT_TILES = NT + NE - 1
QK = 16.0
SC = QK * QK
MROW = 64.0
WS = 64.0
M0, MROWS = 96, 3 * HG
PB0 = M0 + MROWS
K_ROWS = PB0 + 3
PARTS = 3
MASKED = -1e30


def constants():
    eye = np.eye(P, dtype=np.float32)
    before = np.triu(np.ones((P, P), np.float32), 1)
    head_mask = np.zeros((P, HG), np.float32)
    for r in range(3 * 32):
        head_mask[r, (r % 32) // DH] = 1.0
    for r in range(MROWS):
        head_mask[M0 + r, r // 3] = MROW
    slopes = (2.0 ** (-8.0 / H)) ** np.arange(1, H + 1, dtype=np.float64)
    slope_col = np.tile(slopes.astype(np.float32), B)[:, None]
    route = np.zeros((P, 3, P), np.float32)
    route[:, 0] = np.tile(np.arange(NE) - NE, NT)
    run = np.ones((NE, NT), np.float32)
    run[:, 0] = 0.0
    route[:, 1] = run.reshape(-1)
    route[:, 2] = np.arange(P)
    return {"c_eye": eye, "c_before": before, "c_head_mask": head_mask, "c_slope": slope_col,
            "c_route": route}


def layer(index, sem):
    names = ["ctx_loaded", "norm_own", "xvar", "xrstd", "xn_ready", "xnT_done", "xnT_copied",
             "q_done", "q_copied", "k_done", "k_copied", "v_done", "v_copied", "q_hi", "q_lo",
             "k_hi", "k_lo", "k_rep", "k_tile", "m_zeroed", "p1_done", "max_done", "m_parts", "own",
             "mT_done", "mT_copied", "p2_done", "exp_done", "pv_done", "o_copied", "ot_done",
             "ot_norm", "o_rc", "aT_done", "aT_copied", "op_done", "x_added"]
    ly = {n: sem(f"L{index}_{n}") for n in names}
    ly.update(index=index, bias=index == 0, position=index == 1)
    ly["q_tile"] = [sem(f"L{index}_q_tile{i}") for i in range(2)]
    if ly["position"]:
        ly["k_pos"] = [[sem(f"L{index}_k_pos{i}{par}") for par in range(2)] for i in range(2)]
        ly["ot_sum"] = sem(f"L{index}_ot_sum")
    else:
        ly["x_biased"] = sem(f"L{index}_x_biased")
    return ly


def build(nc, t, out):
    with ExitStack() as ctx:
        def sb(name, shape, dt=F32):
            return ctx.enter_context(nc.sbuf_tensor(name, shape, dt))

        def psum(name, shape, dt=F32):
            return ctx.enter_context(nc.psum_tensor(name, shape, dt))

        def sem(name):
            return ctx.enter_context(nc.semaphore(name))

        X = sb("X", [P, NT + QT, D])
        eye = sb("eye", [P, P])
        eye16 = sb("eye16", [P, P], F16)
        head_mask = sb("head_mask", [P, HG])
        W = {}
        for L in range(2):
            for n in "qkvo":
                W[n, L] = sb(f"w{n}{L}", [P, D])
        qkb = sb("qkb", [P, 2])
        qkbs = sb("qkbs", [P, 2])
        vb = sb("vb", [P, D])
        ob = sb("ob", [P, D])
        ctxT = [sb(f"ctxT{i}", [P, S]) for i in range(2)]
        xn = [sb(f"xn{i}", [P, QT, D]) for i in range(2)]
        st6 = sb("st6", [P, QT, 6])
        mv = sb("mv", [P, QT, 2])
        ve = sb("ve", [P, QT])
        rstd = sb("rstd", [P, QT])
        carried_v = sb("carried_v", [P, QT])
        mhalf = sb("mhalf", [P, NT])
        xnT = sb("xnT", [P, S])
        qf, kf = sb("qf", [P, S]), sb("kf", [P, S])
        q_hi = [sb(f"q_hi{i}", [P, S], F16) for i in range(2)]
        q_lo = [sb(f"q_lo{i}", [P, S], F16) for i in range(2)]
        k_hi, k_lo = sb("k_hi", [P, S], F16), sb("k_lo", [P, S], F16)
        k_rep = sb("k_rep", [P, NG, S], F16)
        Qt = [sb(f"Qt{i}", [P, NG, S], F16) for i in range(2)]
        Kt = [sb(f"Kt{i}", [P, H, S], F16) for i in range(2)]
        Vt = [sb(f"Vt{i}", [P, QT, H, 32]) for i in range(2)]
        nm = [sb(f"nm{i}", [P, QT, H]) for i in range(2)]
        mr = sb("mr", [P, QT, 8])
        mr2 = sb("mr2", [P, QT, 8])
        mparts = [sb(f"mparts{i}", [P, QT, H, PARTS], F16) for i in range(2)]
        Pt = [sb(f"Pt{i}", [P, HG, QT * S]) for i in range(NG)]
        Osb = [sb(f"Osb{i}", [P, NG, S]) for i in range(2)]
        rc = sb("rc", [P, QT, H])
        rsum = sb("rsum", [P, QT, H])
        attn = sb("attn", [P, QT, D])
        aT = sb("aT", [P, S])
        S1 = [psum(f"S1_{i}", [P, QT, S]) for i in range(2)]
        S2 = [psum(f"S2_{i}", [P, 2, QT, S]) for i in range(2)]
        M = [psum(f"M{i}", [P, 512]) for i in range(2)]
        M16 = [m[:, :].bitcast(F16) for m in M]
        O_BANK = (1, 0, 1, 1)

        pos_i = sb("pos_i", [P, S], I32)
        pos_f = sb("pos_f", [P, S])
        slope = sb("slope", [P, 1])
        pos_r = sb("pos_r", [P, S])
        pos_parts = sb("pos_parts", [P, PARTS, S], F16)

        mask_bias = sb("mask_bias", [P, NT, S], BF16)
        eye_bf = sb("eye_bf", [P, P], BF16)
        mask_min = sb("mask_min", [P, 1])
        mask_hit = sb("mask_hit", [P, 1])
        mask_any = sb("mask_any", [P, 1], I32)
        mk = {n: sem(f"mask_{n}") for n in ("raw", "own", "count", "any")}

        ly = [layer(0, sem), layer(1, sem)]
        loaded, loaded_x, loaded_late, pos_stored = sem("loaded"), sem("loaded_x"), sem("loaded_late"), sem("pos_stored")
        inited, vt_zeroed = sem("inited"), sem("vt_zeroed")
        N_LOADS, N_LATE = 10, 20
        N_INIT = 6 + 2 + 2 + 2 * NG + 4
        pos_dram = nc.dram_tensor("pos_parts_dram", (B, H, PARTS, S), F16).ap()
        pos_own, pos_ready = sem("pos_own"), sem("pos_ready")
        w_hl = sb("w_hl", [P, W_BLOCKS, 2, P], F16)
        wraw = [sb(f"wraw{i}", [P, W_CHUNK, P]) for i in range(2)]
        braw = sb("braw", [P, 40])
        brest = sb("brest", [P, 40])
        bparts = sb("bparts", [P, PARTS, 40], F16)
        b1rows = sb("b1rows", [P, NE * HID], F16)
        b2rows = sb("b2rows", [P, NE * D], F16)
        ones16 = sb("ones16", [P, P], F16)
        wg = sb("wg", [P, NE])
        bg = sb("bg", [P, NE])
        xn2 = Pt[2][:, :, :].rearrange("p i (t d) -> p (i t) d", d=D)
        before = sb("before", [P, P])
        ones32 = sb("ones32", [P, P])
        route_c = sb("route_c", [P, 3, P])
        logit = sb("logit", [P, NT, NE])
        top = sb("top", [P, NT])
        onehot = sb("onehot", [P, NT, NE])
        t1 = sb("t1", [P, NT, NE])
        t2 = sb("t2", [P, NT, NE])
        first = sb("first", [P, NT])
        gate = sb("gate", [P, NT])
        gsum = sb("gsum", [P, NT])
        tot = sb("tot", [P, NE, NT])
        cum = sb("cum", [P, NE, NT])
        rbase = sb("rbase", [P, NE, NT])
        cnt_i = sb("cnt_i", [P, NE], I32)
        cnt_s = sb("cnt_s", [P, NE], I32)
        ntile = sb("ntile", [P, NE])
        tend = sb("tend", [P, NE])
        tstart = sb("tstart", [P, NE])
        slotf = sb("slotf", [P, NT])
        slot = sb("slot", [P, NT], I32)
        cmp = sb("cmp", [P, SLOT_TILES, NE])
        expf = sb("expf", [P, SLOT_TILES])
        expert = sb("expert", [P, SLOT_TILES], I32)
        zero = sb("zero", [P, D])
        xs_dram = nc.dram_tensor("sorted_x", (SLOT_TILES * P, D), F32).ap()
        ys_dram = nc.dram_tensor("sorted_y", (SLOT_TILES * P, D), F32).ap()
        gT = [sb(f"gT{i}", [P, S]) for i in range(2)]
        st_all = sb("st_all", [P, NT, 6])
        mv_all = sb("mv_all", [P, NT, 2])
        ve_all = sb("ve_all", [P, NT])
        rstd_all = sb("rstd_all", [P, NT])
        xt = [sb(f"xt{i}", [P, D]) for i in range(2)]
        x_hl = [sb(f"x_hl{i}", [P, 2, P], F16) for i in range(2)]
        hs = [sb(f"hs{i}", [P, HID]) for i in range(2)]
        hf = [sb(f"hf{i}", [P, HID]) for i in range(2)]
        h_hi = [sb(f"h_hi{i}", [P, HID], F16) for i in range(2)]
        h_lo = [sb(f"h_lo{i}", [P, HID], F16) for i in range(2)]
        ysb = [sb(f"ysb{i}", [P, D]) for i in range(2)]
        yg = Pt[3][:, :, :].rearrange("p i (t d) -> p (i t) d", d=D)
        moe = {n: sem(f"moe_{n}") for n in (
            "wraw0", "wraw1", "split", "scaled", "w_hi", "bsplit", "brows", "zfill",
            "norm_own", "var", "rstd", "xn", "xT", "xTc", "gm", "logit",
            "r", "exp", "gate", "onehot", "ranks", "slots", "scattered", "tT", "x_hi", "x_lo", "h", "hr", "hs", "hf",
            "h_hi", "h_lo", "y", "yh", "ysb", "gathered_first", "gathered", "x", "xt0", "xt1", "stored0", "stored1")}
        wfc = sb("wfc", [P, HID])
        wpr = sb("wpr", [P, HC, D])
        hr, h2 = ([Pt[n][:, 2 * i:2 * i + 2, :].rearrange("p a (k n) -> p (a k) n", k=QT) for i in range(2)]
                  for n in range(2))
        mem = [Pt[2 + i][:, :, :].rearrange("p i (k n) -> p (i k) n", n=S) for i in range(2)]
        spike = [sb(f"spike{i}", [P, STEPS, S], F16) for i in range(2)]
        above = sb("above", [P, STEPS, S])
        minus_one = sb("minus_one", [P, 1])
        tmp = sb("tmp", [P, S])
        fin = [sb(f"fin{i}", [P, QT, D]) for i in range(2)]
        ff = {n: sem(f"ff_{n}") for n in ("norm_own", "var", "rstd", "xn", "xT", "xTc", "h", "relu", "sq", "y",
                                          "yc", "mem", "above", "spike", "count", "out", "stored0", "stored1")}
        block = ctx.enter_context(nc.Block())

        def slots_loop(eng, slot_fn):
            for s in (-3, -2, -1, 0, 1):
                slot_fn(s, s % 2, s)
            with eng.Fori(1, 3) as i:
                for par in range(2):
                    slot_fn(2 * i + par, par, None)
            for s in (6, 7, 8):
                slot_fn(s, s % 2, s)

        def exists(s, d):
            return s is None or 0 <= s + d < B

        def attention_on_tensor(pe, ly, masked):
            def p1(b, par, h):
                if h % 8 == 0:
                    pe.wait_ge(ly["q_tile"][h // 8], 48 * b + 48)
                    pe.wait_ge(ly["k_tile"], 2 * b + h // 8 + 1)
                    pe.wait_ge(ly["m_zeroed"], 2 * b + h // 8 + 1)
                    if ly["position"]:
                        pe.wait_ge(ly["k_pos"][h // 8][par], 8 * (b - par) + 16)
                if not (isinstance(b, int) and b == 0 and h < 2):
                    pe.wait_ge(ly["max_done"], 16 * b + h - 1)
                for q in range(QT):
                    mm = pe.matmul(S1[h % 2][:, q, :], Qt[par][0:K_ROWS, h // HG, q * P:(q + 1) * P],
                                   Kt[par][0:K_ROWS, h, :], start=True, stop=not masked)
                    if masked:
                        mm = pe.matmul(S1[h % 2][:, q, :], eye_bf[:, :], mask_bias[:, bass.ds(b * QT + q, 1), :]
                                       .rearrange("p t n -> p (t n)"), start=False, stop=True)
                mm.then_inc(ly["p1_done"], 1)

            def p2(b, par, pair):
                if pair % 4 == 0:
                    pe.wait_ge(ly["mT_copied"], 2 * b + pair // 4 + 1)
                if not (isinstance(b, int) and b == 0 and pair < 2):
                    pe.wait_ge(ly["exp_done"], 8 * b + pair - 1)
                for hh in range(2):
                    h = 2 * pair + hh
                    for k in range(QT):
                        mm = pe.matmul(S2[pair % 2][:, hh, k, :], Kt[par][0:K_ROWS, h, k * P:(k + 1) * P],
                                       Qt[par][0:K_ROWS, h // HG, :], start=True, stop=not masked)
                        for q in range(QT if masked else 0):
                            mm = pe.matmul(S2[pair % 2][:, hh, k, q * P:(q + 1) * P],
                                           mask_bias[:, bass.ds(b * QT + q, 1), k * P:(k + 1) * P]
                                           .rearrange("p t n -> p (t n)"), eye_bf[:, :],
                                           start=False, stop=q == QT - 1)
                mm.then_inc(ly["p2_done"], 1)

            def pv(b, par, g):
                pe.wait_ge(ly["exp_done"], 8 * b + 2 * g + 2)
                if g == 0:
                    pe.wait_ge(ly["v_copied"], b + 1)
                for k in range(QT):
                    for i in range(HG):
                        mm = pe.matmul(M[O_BANK[g]][32 * i:32 * i + 32, 0:S], Vt[par][:, k, HG * g + i, :],
                                       Pt[g][:, i, k * S:(k + 1) * S], start=(k == 0), stop=(k == QT - 1))
                mm.then_inc(ly["pv_done"], 1)

            def m_turn(b, par, half, bank):
                pe.wait_ge(ly["m_parts"], 2 * b + half + 1)
                for g in range(2):
                    for q in range(QT):
                        h = 8 * half + HG * g
                        mm = pe.transpose(M16[bank][0:MROWS, g * S + q * P:g * S + (q + 1) * P],
                                          mparts[par][:, q, h:h + HG, :].rearrange("p h c -> p (h c)"), eye16[:, :])
                mm.then_inc(ly["mT_done"], 1)

            def slot_fn(b, par, s):
                new, nxt, cur, old, older = (exists(s, d) for d in (2, 1, 0, -1, -2))
                par1 = 1 - par

                def pair(i):
                    if nxt:
                        p1(b + 1, par1, 2 * i)
                        p1(b + 1, par1, 2 * i + 1)
                    if cur:
                        p2(b, par, i)

                pair(0)
                if new:
                    pe.wait_ge(ly["xn_ready"], b + 3)
                    if older:
                        pe.wait_ge(ly["x_added"], b - 1)
                    elif old:
                        pe.wait_ge(ly["o_copied"], 4 * b - 2)
                    elif cur:
                        pe.wait_ge(ly["mT_copied"], 2 * b + 1)
                    elif nxt:
                        pe.wait_ge(ly["k_copied"], b + 2)
                    for q in range(QT):
                        mm = pe.transpose(M[0][:, q * P:(q + 1) * P], xn[par][:, q, :], eye[:, :])
                    mm.then_inc(ly["xnT_done"], 1)
                pair(1)
                if old:
                    pe.wait_ge(ly["o_copied"], 4 * b - 1)
                    pv(b - 1, par1, 3)
                if new:
                    pe.wait_ge(ly["xnT_copied"], b + 3)
                    pe.matmul(M[0][:, 0:S], W["q", ly["index"]][:, :], xnT[:, :], start=True,
                              stop=True).then_inc(ly["q_done"], 1)
                pair(2)
                if cur:
                    if old:
                        pe.wait_ge(ly["o_copied"], 4 * b)
                    m_turn(b, par, 1, 1)
                if new:
                    pe.wait_ge(ly["q_copied"], b + 3)
                    pe.wait_ge(ly["ctx_loaded"], 16 * b + 48)
                    pe.matmul(M[0][:, 0:S], W["k", ly["index"]][:, :], ctxT[par][:, :], start=True,
                              stop=True).then_inc(ly["k_done"], 1)
                pair(3)
                if cur:
                    pe.wait_ge(ly["mT_copied"], 2 * b + 2)
                    pv(b, par, 0)
                if nxt:
                    if new:
                        pe.wait_ge(ly["k_copied"], b + 3)
                    else:
                        pe.wait_ge(ly["x_added"], b - 1)
                    for k in range(QT):
                        mm = pe.matmul(M[0][:, k * D:(k + 1) * D], ctxT[par1][:, k * P:(k + 1) * P],
                                       W["v", ly["index"]][:, :], start=True, stop=True)
                    mm.then_inc(ly["v_done"], 1)

                def o_turn(q):
                    for g in range(NG):
                        mm = pe.transpose(M[1][:, g * P:(g + 1) * P], Osb[par1][:, g, q * P:(q + 1) * P], eye[:, :])
                    mm.then_inc(ly["ot_done"], 1)

                if old:
                    pe.wait_ge(ly["o_copied"], 4 * b + 1 if cur else 4 * b)
                    o_turn(0)
                pair(4)
                if nxt:
                    pe.wait_ge(ly["v_copied"], b + 2)
                    m_turn(b + 1, par1, 0, 0)
                pair(5)
                if cur:
                    if nxt:
                        pe.wait_ge(ly["mT_copied"], 2 * b + 3)
                    else:
                        pe.wait_ge(ly["x_added"], b - 1)
                    pv(b, par, 1)
                if old:
                    pe.wait_ge(ly["ot_norm"], 2 * b - 1)
                    o_turn(1)
                pair(6)
                if old:
                    pe.wait_ge(ly["ot_norm"], 2 * b)
                    for q in range(QT):
                        mm = pe.transpose(M[1][:, q * P:(q + 1) * P], attn[:, q, :], eye[:, :])
                    mm.then_inc(ly["aT_done"], 1)
                pair(7)
                if old:
                    pe.wait_ge(ly["aT_copied"], b)
                    if cur:
                        pe.wait_ge(ly["o_copied"], 4 * b + 2)
                    else:
                        pe.wait_ge(ly["x_added"], b - 1)
                    for q in range(QT):
                        mm = pe.matmul(M[0][:, q * D:(q + 1) * D], aT[:, q * P:(q + 1) * P], W["o", ly["index"]][:, :],
                                       start=True, stop=True)
                    mm.then_inc(ly["op_done"], 1)
                if cur:
                    if old:
                        pe.wait_ge(ly["aT_copied"], b)
                    else:
                        pe.wait_ge(ly["o_copied"], 4 * b + 1)
                    pv(b, par, 2)

            slots_loop(pe, slot_fn)

        def attention_on_scalar(act, ly):
            def o_copy(b, par, g):
                act.wait_ge(ly["pv_done"], 4 * b + g + 1)
                act.activation(Osb[par][:, g, :], M[O_BANK[g]][:, 0:S], ACT.Copy).then_inc(ly["o_copied"], 1)

            def slot_fn(b, par, s):
                new, nxt, cur, old, older = (exists(s, d) for d in (2, 1, 0, -1, -2))

                def exp(i):
                    if not cur:
                        return
                    if i % 2 == 0 and old:
                        act.wait_ge(ly["pv_done"], 4 * b - 3 + i // 2)
                    act.wait_ge(ly["p2_done"], 8 * b + i + 1)
                    act.activation(Pt[i // 2][:, 2 * (i % 2):2 * (i % 2) + 2, :].rearrange("p a n -> p (a n)"),
                                   S2[i % 2][:, :, :, :].rearrange("p a k n -> p (a k n)"), ACT.Exp,
                                   scale=1.0 / SC).then_inc(ly["exp_done"], 1)

                def m_copy(bb, pp, half, bank):
                    act.wait_ge(ly["mT_done"], 2 * bb + half + 1)
                    act.activation(Qt[pp][M0:M0 + MROWS, 2 * half:2 * half + 2, :].rearrange("p g n -> p (g n)"),
                                   M16[bank][0:MROWS, 0:2 * S], ACT.Copy).then_inc(ly["mT_copied"], 1)

                exp(0)
                if new:
                    act.wait_ge(ly["xnT_done"], b + 3)
                    if nxt:
                        act.wait_ge(ly["q_done"], b + 2)
                    act.activation(xnT[:, :], M[0][:, 0:S], ACT.Copy).then_inc(ly["xnT_copied"], 1)
                exp(1)
                if old:
                    o_copy(b - 1, 1 - par, 3)
                if new:
                    act.wait_ge(ly["q_done"], b + 3)
                    if nxt:
                        act.wait_ge(ly["q_lo"], b + 2)
                    act.activation(qf[:, :], M[0][:, 0:S], ACT.Identity, bias=qkbs[:, 0:1] if ly["bias"] else 0.0,
                                   scale=QK / float(np.sqrt(DH))).then_inc(ly["q_copied"], 1)
                    act.wait_ge(ly["q_copied"], b + 3)
                    if cur:
                        act.wait_ge(ly["q_tile"][1], 48 * b + 48)
                    act.activation(q_hi[par][:, :], qf[:, :], ACT.Copy).then_inc(ly["q_hi"], 1)
                exp(2)
                if cur:
                    m_copy(b, par, 1, 1)
                if new:
                    act.wait_ge(ly["k_done"], b + 3)
                    if nxt:
                        act.wait_ge(ly["k_lo"], b + 2)
                    act.activation(kf[:, :], M[0][:, 0:S], ACT.Identity, bias=qkbs[:, 1:2] if ly["bias"] else 0.0,
                                   scale=QK).then_inc(ly["k_copied"], 1)
                    act.wait_ge(ly["k_copied"], b + 3)
                    if nxt:
                        act.wait_ge(ly["k_rep"], 48 * (b + 2))
                    act.activation(k_hi[:, :], kf[:, :], ACT.Copy).then_inc(ly["k_hi"], 1)
                exp(3)
                if cur:
                    if older:
                        act.wait_ge(ly["ot_done"], 2 * b - 2)
                    o_copy(b, par, 0)
                exp(4)
                if nxt:
                    m_copy(b + 1, 1 - par, 0, 0)
                    if ly["bias"]:
                        act.wait_ge(moe[f"wraw{1 - par}"], 8 * (b + par) + 16)
                        raw = wraw[1 - par][:, :, :].rearrange("p k n -> p (k n)")
                        act.activation(raw, raw, ACT.Copy, scale=WS).then_inc(moe["scaled"], 1)
                exp(5)
                if nxt and ly["bias"]:
                    act.wait_ge(moe["scaled"], b + 2)
                    act.activation(w_hl[:, bass.ds(W_CHUNK * (b + 1), W_CHUNK), 0, :], wraw[1 - par][:, :, :], ACT.Copy) \
                       .then_inc(moe["w_hi"], 1)
                if cur:
                    o_copy(b, par, 1)
                exp(6)
                if old:
                    act.wait_ge(ly["aT_done"], b)
                    if older:
                        act.wait_ge(ly["op_done"], b - 1)
                    act.activation(aT[:, :], M[1][:, 0:S], ACT.Copy).then_inc(ly["aT_copied"], 1)
                exp(7)
                if cur:
                    o_copy(b, par, 2)

            slots_loop(act, slot_fn)

        def carrier_on_vector(v):
            v.tensor_copy(carried_v[:, :], mhalf[:, 0:QT])

        def norm_stats(v, b, own, var):
            for q in range(QT):
                i = v.bn_stats(st6[:, q, :], X[:, b * QT + q, :])
            i.then_inc(own, 1)
            v.wait_ge(own, 2 * b + 1)
            carrier_on_vector(v)
            for q in range(QT):
                i = v.bn_aggr(mv[:, q, :], st6[:, q, :])
            i.then_inc(own, 1)
            v.wait_ge(own, 2 * b + 2)
            v.tensor_scalar(ve[:, :], mv[:, :, 1], EPS, None, ALU.add).then_inc(var, 1)

        def norm_apply(v, b, dst, rst, done):
            v.wait_ge(rst, b + 1)
            for q in range(QT):
                i = v.tensor_scalar(dst[:, q, :], X[:, b * QT + q, :], mv[:, q, 0:1], rstd[:, q:q + 1],
                                    ALU.subtract, ALU.mult)
            i.then_inc(done, 1)

        def norm_root(pool, b, var, rst):
            pool.wait_ge(var, b + 1)
            pool.tensor_tensor(rstd[:, :], ve[:, :], mhalf[:, 0:QT], ALU.pow).then_inc(rst, 1)

        def attention_on_vector(v, ly):
            def reduce(b, par, h):
                v.wait_ge(ly["p1_done"], 16 * b + h + 1)
                v.tensor_reduce(nm[par][:, :, h], S1[h % 2][:, :, :], AX.X, ALU.max, negate=True)\
                 .then_inc(ly["max_done"], 1)

            def parts(b, par, half):
                hs = slice(8 * half, 8 * half + 8)
                base = 6 * b + 3 * half
                v.wait_ge(ly["max_done"], 16 * b + 8 * half + 8)
                if not (isinstance(b, int) and b < 2):
                    v.wait_ge(ly["mT_done"], 2 * b - 3 + half)
                v.tensor_scalar(mparts[par][:, :, hs, 0], nm[par][:, :, hs], 1.0 / MROW, None, ALU.mult)\
                 .then_inc(ly["own"], 1)
                v.wait_ge(ly["own"], base + 1)
                v.scalar_tensor_tensor(mr[:, :, :], nm[par][:, :, hs], 1.0 / MROW, mparts[par][:, :, hs, 0],
                                       ALU.mult, ALU.subtract).then_inc(ly["own"], 1)
                v.wait_ge(ly["own"], base + 2)
                v.tensor_copy(mparts[par][:, :, hs, 1], mr[:, :, :]).then_inc(ly["own"], 1)
                v.wait_ge(ly["own"], base + 3)
                v.tensor_tensor(mparts[par][:, :, hs, 2], mr[:, :, :], mparts[par][:, :, hs, 1],
                                ALU.subtract).then_inc(ly["m_parts"], 1)

            def zero_m(b, par, half):
                if not (isinstance(b, int) and b < 2):
                    v.wait_ge(ly["p2_done"], 8 * (b - 2) + 4 * half + 4)
                v.memset(Qt[par][M0:M0 + MROWS, 2 * half:2 * half + 2, :], 0.0).then_inc(ly["m_zeroed"], 1)

            def o_norm(b, q):
                ot = M[1][:, :].rearrange("p (h r) -> p h r", r=32)
                v.wait_ge(ly["ot_done"], 2 * b + q + 1)
                if ly["position"]:
                    v.tensor_scalar(rsum[:, q, :], ot[:, :, DH], 1.0, None, ALU.add).then_inc(ly["ot_sum"], 1)
                    v.wait_ge(ly["ot_sum"], 2 * b + q + 1)
                    v.reciprocal(rc[:, q, :], rsum[:, q, :]).then_inc(ly["o_rc"], 1)
                else:
                    v.reciprocal(rc[:, q, :], ot[:, :, DH]).then_inc(ly["o_rc"], 1)
                v.wait_ge(ly["o_rc"], 2 * b + q + 1)
                if q == 0 and not (isinstance(b, int) and b == 0):
                    v.wait_ge(ly["aT_done"], b)
                v.tensor_tensor(attn[:, q, :].rearrange("p (h d) -> p h d", d=DH), ot[:, :, 0:DH],
                                rc[:, q, :].unsqueeze(2).to_broadcast([P, H, DH]), ALU.mult).then_inc(ly["ot_norm"], 1)

            def slot_fn(b, par, s):
                nxt, cur, old = (exists(s, d) for d in (1, 0, -1))
                ahead = s is None or s <= 5

                def r(i):
                    if nxt:
                        reduce(b + 1, 1 - par, 2 * i)
                        reduce(b + 1, 1 - par, 2 * i + 1)

                r(0)
                if nxt:
                    zero_m(b + 1, 1 - par, 1)
                if s == -1 and ly["bias"]:
                    v.wait_ge(loaded_x, 16)
                if s == -1 and not ly["bias"]:
                    v.wait_ge(moe["gathered"], 16 * (NT - 2 * QT))
                    add_experts(v, 2 * QT, NT)
                if ahead:
                    norm_stats(v, b + 3, ly["norm_own"], ly["xvar"])
                r(1)
                if cur:
                    parts(b, par, 1)
                r(2)
                if ahead:
                    if nxt:
                        v.wait_ge(ly["xnT_done"], b + 2)
                    norm_apply(v, b + 3, xn[1 - par], ly["xrstd"], ly["xn_ready"])
                r(3)
                if nxt:
                    parts(b + 1, 1 - par, 0)
                    v.wait_ge(ly["v_done"], b + 2)
                    if old:
                        v.wait_ge(ly["pv_done"], 4 * b)
                    src = M[0][:, 0:S].rearrange("p (k h d) -> p k h d", k=QT, h=H)
                    dst = Vt[1 - par]
                    if ly["bias"]:
                        for k in range(QT):
                            i = v.tensor_tensor(dst[:, k, :, 0:DH], src[:, k], vb[:, :].rearrange("p (h d) -> p h d", d=DH),
                                                ALU.add)
                    else:
                        i = v.tensor_copy(dst[:, :, :, 0:DH], src)
                    i.then_inc(ly["v_copied"], 1)
                r(4)
                if exists(s, 2):
                    zero_m(b + 2, par, 0)
                if old:
                    o_norm(b - 1, 0)
                r(5)
                if old:
                    o_norm(b - 1, 1)
                r(6)
                if old and ly["bias"]:
                    for q in range(QT):
                        i = v.tensor_tensor(X[:, (b - 1) * QT + q, :], X[:, (b - 1) * QT + q, :], ob[:, :], ALU.add)
                    i.then_inc(ly["x_biased"], 1)
                r(7)
                if old:
                    v.wait_ge(ly["op_done"], b)
                    if ly["bias"]:
                        v.wait_ge(ly["x_biased"], b)
                    for q in range(QT):
                        x = X[:, (b - 1) * QT + q, :]
                        i = v.tensor_tensor(x, M[0][:, q * D:(q + 1) * D], x, ALU.add)
                    i.then_inc(ly["x_added"], 1)

            slots_loop(v, slot_fn)

        def attention_on_gpsimd(pool, ly):
            def slot_fn(b, par, s):
                new, nxt, cur = (exists(s, d) for d in (2, 1, 0))
                if s is None or s <= 5:
                    norm_root(pool, b + 3, ly["xvar"], ly["xrstd"])
                if cur and ly["bias"]:
                    pool.wait_ge(moe["w_hi"], b + 1)
                    w = bass.ds(W_CHUNK * b, W_CHUNK)
                    pool.tensor_tensor(w_hl[:, w, 1, :], wraw[par][:, :, :], w_hl[:, w, 0, :], ALU.subtract) \
                        .then_inc(moe["split"], 1)
                if not new:
                    return
                if cur:
                    pool.wait_ge(ly["q_tile"][1], 48 * b + 48)
                pool.wait_ge(ly["q_hi"], b + 3)
                pool.tensor_tensor(q_lo[par][:, :], qf[:, :], q_hi[par][:, :], ALU.subtract).then_inc(ly["q_lo"], 1)
                if nxt:
                    pool.wait_ge(ly["k_rep"], 48 * (b + 2))
                pool.wait_ge(ly["k_hi"], b + 3)
                pool.tensor_tensor(k_lo[:, :], kf[:, :], k_hi[:, :], ALU.subtract).then_inc(ly["k_lo"], 1)
                for half in range(2):
                    if cur:
                        pool.wait_ge(ly["p2_done"], 8 * b + 4 * half + 4)
                    if half == 0:
                        pool.wait_ge(ly["k_rep"], 48 * (b + 3))
                    gs = slice(2 * half, 2 * half + 2)
                    for i in range(HG):
                        dst = Kt[par][0:M0, :, :].rearrange("p (g i) n -> p g i n", i=HG)[:, gs, i, :]
                        if i == 0:
                            pool.tensor_tensor(dst, k_rep[0:M0, gs, :], head_mask[0:M0, 0:1].unsqueeze(2)
                                               .to_broadcast([M0, 2, S]), ALU.mult)
                            continue
                        kk = pool.tensor_scalar(dst, k_rep[0:M0, gs, :], head_mask[0:M0, i:i + 1], 1.0,
                                                ALU.mult, ALU.mult)
                    kk.then_inc(ly["k_tile"], 1)

            slots_loop(pool, slot_fn)

        def load_weights(sp, n, par):
            sp.dma_start(wraw[par][:, :, :], t["w"][:, bass.ds(W_CHUNK * n, W_CHUNK), :]).then_inc(moe[f"wraw{par}"], 16)

        def attention_on_sync(sp, ly, late):
            def slot_fn(b, par, s):
                new, nxt, cur = (exists(s, d) for d in (2, 1, 0))
                if not new:
                    return
                if s in (-1, 0, 1):
                    for dst, src in late[s + 1::3]:
                        sp.dma_start(dst, src).then_inc(loaded_late, 16)
                if cur:
                    sp.wait_ge(ly["v_done"], b + 1)
                    sp.wait_ge(ly["k_done"], b + 1)
                sp.dma_start(ctxT[par][:, :], t["ctxT"][:, b + 2, :]).then_inc(ly["ctx_loaded"], 16)
                sp.wait_ge(ly["k_lo"], b + 3)
                if nxt:
                    sp.wait_ge(ly["k_tile"], 2 * b + 4)
                for block, src in enumerate((k_hi, k_lo, k_hi)):
                    sp.dma_start(k_rep[32 * block:32 * block + 32, :, :], src[:, :]).then_inc(ly["k_rep"], 16)
                for half in range(2):
                    if cur:
                        sp.wait_ge(ly["p2_done"], 8 * b + 4 * half + 4)
                    if half == 0:
                        sp.wait_ge(ly["q_lo"], b + 3)
                    for block, src in enumerate((q_hi, q_hi, q_lo)):
                        sp.dma_start(Qt[par][32 * block:32 * block + 32, 2 * half:2 * half + 2, :],
                                     src[par][64 * half:64 * half + 64, :]).then_inc(ly["q_tile"][half], 16)
                    if ly["position"]:
                        sp.dma_start(Kt[par][PB0:PB0 + PARTS, 8 * half:8 * half + 8, :],
                                     pos_dram[b + 2, 8 * half:8 * half + 8, :, :].rearrange("h c n -> c h n")) \
                          .then_inc(ly["k_pos"][half][par], 16)
                if ly["bias"] and s == -2:
                    load_weights(sp, 0, 0)
                    load_weights(sp, 1, 1)
                if ly["bias"] and cur:
                    sp.wait_ge(moe["split"], b + 1)
                    load_weights(sp, b + 2, par)

            slots_loop(sp, slot_fn)


        def gate_on_vector(v):
            v.wait_ge(ly[0]["x_added"], B)
            v.wait_ge(loaded_late, 16 * N_LATE)
            for i in range(NT):
                ii = v.bn_stats(st_all[:, i, :], X[:, i, :])
            ii.then_inc(moe["norm_own"], 1)
            v.wait_ge(moe["norm_own"], 1)
            for i in range(NT):
                ii = v.bn_aggr(mv_all[:, i, :], st_all[:, i, :])
            ii.then_inc(moe["norm_own"], 1)
            v.wait_ge(moe["norm_own"], 2)
            v.tensor_scalar(ve_all[:, :], mv_all[:, :, 1], EPS, None, ALU.add).then_inc(moe["var"], 1)
            v.wait_ge(moe["rstd"], 1)
            for b in range(B):
                for i in range(b * QT, b * QT + QT):
                    ii = v.tensor_scalar(xn2[:, i, :], X[:, i, :], mv_all[:, i, 0:1], rstd_all[:, i:i + 1],
                                         ALU.subtract, ALU.mult)
                ii.then_inc(moe["xn"], 1)
            v.wait_ge(moe["gm"], B)
            v.tensor_tensor(logit[:, :, :], S1[0][:, 0, 0:NT * NE].rearrange("p (t e) -> p t e", e=NE),
                            bg[:, :].unsqueeze(1).to_broadcast([P, NT, NE]), ALU.add).then_inc(moe["logit"], 1)

        def gate_on_gpsimd(pool):
            pool.wait_ge(moe["var"], 1)
            pool.tensor_tensor(rstd_all[:, :], ve_all[:, :], mhalf[:, :], ALU.pow).then_inc(moe["rstd"], 1)

        def gate_on_tensor(pe):
            pe.wait_ge(loaded_late, 16 * N_LATE)
            for b in range(B + 1):
                if b < B:
                    pe.wait_ge(moe["xn"], b + 1)
                    if b >= 2:
                        pe.wait_ge(moe["xTc"], b - 1)
                    for q in range(QT):
                        mm = pe.transpose(M[b % 2][:, q * P:(q + 1) * P], xn2[:, b * QT + q, :], eye[:, :])
                    mm.then_inc(moe["xT"], 1)
                if b >= 1:
                    c = b - 1
                    pe.wait_ge(moe["xTc"], b)
                    for q in range(QT):
                        i = c * QT + q
                        mm = pe.matmul(S1[0][:, 0, i * NE:(i + 1) * NE], gT[c % 2][:, q * P:(q + 1) * P], wg[:, :],
                                       start=True, stop=True)
                    mm.then_inc(moe["gm"], 1)
            pe.wait_ge(moe["onehot"], 1)
            oh = onehot[:, :, :].rearrange("p t e -> p (t e)")
            pe.matmul(M[0][:, 0:P], before[:, :], oh, start=True, stop=True).then_inc(moe["ranks"], 1)
            pe.matmul(M[1][:, 0:P], ones32[:, :], oh, start=True, stop=True).then_inc(moe["ranks"], 1)

        def gate_on_scalar(act):
            for b in range(B):
                act.wait_ge(moe["xT"], b + 1)
                if b >= 2:
                    act.wait_ge(moe["gm"], b - 1)
                act.activation(gT[b % 2][:, :], M[b % 2][:, 0:S], ACT.Copy).then_inc(moe["xTc"], 1)
            act.wait_ge(moe["r"], 5)
            act.activation(t2[:, :, :].rearrange("p t e -> p (t e)"), t1[:, :, :].rearrange("p t e -> p (t e)"),
                           ACT.Exp).then_inc(moe["exp"], 1)

        def route_on_vector(v):
            count = [0]

            def step(ins):
                ins.then_inc(moe["r"], 1)
                count[0] += 1
                v.wait_ge(moe["r"], count[0])

            v.wait_ge(moe["logit"], 1)
            te = [P, NT, NE]
            num = route_c[:, 0, :].rearrange("p (t e) -> p t e", e=NE)
            step(v.tensor_reduce(top[:, :], logit[:, :, :], AX.X, ALU.max))
            step(v.tensor_tensor(t1[:, :, :], logit[:, :, :], top[:, :].unsqueeze(2).to_broadcast(te), ALU.is_equal))
            step(v.tensor_tensor(t2[:, :, :], t1[:, :, :], num, ALU.mult))
            step(v.tensor_reduce(first[:, :], t2[:, :, :], AX.X, ALU.min))
            v.tensor_tensor(onehot[:, :, :], num, first[:, :].unsqueeze(2).to_broadcast(te), ALU.is_equal).then_inc(moe["onehot"], 1)
            step(v.tensor_tensor(t1[:, :, :], logit[:, :, :], top[:, :].unsqueeze(2).to_broadcast(te), ALU.subtract))
            v.wait_ge(moe["ranks"], 2)
            step(v.tensor_copy(tot[:, :, :], M[1][:, 0:P].rearrange("p (t e) -> p e t", e=NE)))
            step(v.tensor_tensor_scan(cum[:, :, :].rearrange("p e t -> p (e t)"), route_c[:, 1, :],
                                      tot[:, :, :].rearrange("p e t -> p (e t)"), 0.0, ALU.mult, ALU.add))
            step(v.tensor_scalar(cnt_i[:, :], cum[:, :, NT - 1], float(P - 1), None, ALU.add))
            step(v.tensor_scalar(cnt_s[:, :], cnt_i[:, :], 7, None, ALU.arith_shift_right))
            step(v.tensor_copy(ntile[:, :], cnt_s[:, :]))
            step(v.tensor_tensor_scan(tend[:, :], ones32[:, 0:NE], ntile[:, :], 0.0, ALU.mult, ALU.add))
            step(v.tensor_tensor(tstart[:, :], tend[:, :], ntile[:, :], ALU.subtract))
            step(v.tensor_tensor(rbase[:, :, :], cum[:, :, :], tot[:, :, :], ALU.subtract))
            step(v.scalar_tensor_tensor(rbase[:, :, :], tstart[:, :].unsqueeze(2).to_broadcast([P, NE, NT]), float(P),
                                        rbase[:, :, :], ALU.mult, ALU.add))
            step(v.tensor_tensor(cum[:, :, :], M[0][:, 0:P].rearrange("p (t e) -> p e t", e=NE), rbase[:, :, :], ALU.add))
            step(v.tensor_tensor(cum[:, :, :], cum[:, :, :], onehot[:, :, :].rearrange("p t e -> p e t"), ALU.mult))
            step(v.tensor_reduce(slotf[:, :], cum[:, :, :].rearrange("p e t -> p t e"), AX.X, ALU.add))
            v.tensor_copy(slot[:, :], slotf[:, :]).then_inc(moe["slots"], 1)
            je = [P, SLOT_TILES, NE]
            step(v.tensor_tensor(cmp[:, :, :], tend[:, :].unsqueeze(1).to_broadcast(je),
                                 route_c[:, 2, 0:SLOT_TILES].unsqueeze(2).to_broadcast(je), ALU.is_le))
            step(v.tensor_reduce(expf[:, :], cmp[:, :, :], AX.X, ALU.add))
            v.tensor_scalar(expert[:, :], expf[:, :], float(NE - 1), None, ALU.min).then_inc(moe["slots"], 1)
            v.wait_ge(moe["exp"], 1)
            step(v.tensor_reduce(gsum[:, :], t2[:, :, :], AX.X, ALU.add))
            v.reciprocal(gate[:, :], gsum[:, :]).then_inc(moe["gate"], 1)

        def biases_on_vector(v):
            v.memset(b1rows[:, :], 0.0).then_inc(moe["bsplit"], 1)
            v.memset(b2rows[:, :], 0.0).then_inc(moe["bsplit"], 1)
            v.tensor_scalar(brest[:, :], braw[:, :], WS, None, ALU.mult).then_inc(moe["bsplit"], 1)
            v.wait_ge(moe["bsplit"], 3)
            v.tensor_copy(bparts[:, 0, :], brest[:, :]).then_inc(pos_own, 1)
            v.wait_ge(pos_own, 1)
            v.tensor_tensor(brest[:, :], brest[:, :], bparts[:, 0, :], ALU.subtract).then_inc(pos_own, 1)
            v.wait_ge(pos_own, 2)
            v.tensor_copy(bparts[:, 1, :], brest[:, :]).then_inc(moe["bsplit"], 1)
            v.wait_ge(moe["bsplit"], 4)
            v.tensor_tensor(bparts[:, 2, :], brest[:, :], bparts[:, 1, :], ALU.subtract).then_inc(moe["bsplit"], 1)
            v.tensor_copy(pos_f[:, :], pos_i[:, :]).then_inc(pos_own, 1)
            v.wait_ge(pos_own, 3)
            v.tensor_scalar(pos_r[:, :], pos_f[:, :], slope[:, 0:1], SC / MROW, ALU.mult, ALU.mult).then_inc(pos_own, 1)
            v.wait_ge(pos_own, 4)
            v.tensor_copy(pos_parts[:, 0, :], pos_r[:, :]).then_inc(pos_own, 1)
            v.wait_ge(pos_own, 5)
            v.tensor_tensor(pos_r[:, :], pos_r[:, :], pos_parts[:, 0, :], ALU.subtract).then_inc(pos_own, 1)
            v.wait_ge(pos_own, 6)
            v.tensor_copy(pos_parts[:, 1, :], pos_r[:, :]).then_inc(pos_own, 1)
            v.wait_ge(pos_own, 7)
            v.tensor_tensor(pos_parts[:, 2, :], pos_r[:, :], pos_parts[:, 1, :], ALU.subtract).then_inc(pos_ready, 1)

        def mask_raw(n):
            return Pt[n][:, :, :].rearrange("p i n -> p (i n)").bitcast(I32)

        def mask_on_sync(sp):
            sp.wait_ge(ly[0]["pv_done"], NG * B)
            for n in range(2):
                sp.dma_start(mask_raw(n), t["mask"][:, n * 2048:(n + 1) * 2048]).then_inc(mk["raw"], 16)

        def mask_on_vector(v):
            v.wait_ge(mk["raw"], 32)
            for n in range(2):
                v.tensor_scalar(mask_bias[:, n * NT // 2:(n + 1) * NT // 2, :].rearrange("p t n -> p (t n)"),
                                mask_raw(n), 0.0, MASKED, ALU.is_equal, ALU.mult).then_inc(mk["own"], 1)
            v.wait_ge(mk["own"], 2)
            v.tensor_reduce(mask_min[:, :], mask_bias[:, :, :].rearrange("p t n -> p (t n)"), AX.X, ALU.min).then_inc(mk["own"], 1)
            v.wait_ge(mk["own"], 3)
            v.tensor_scalar(mask_hit[:, :], mask_min[:, :], 0.0, None, ALU.is_lt).then_inc(mk["own"], 1)
            v.wait_ge(mk["count"], 1)
            v.tensor_scalar(mask_any[:, :], S2[0][:, 0, 0, 0:1], 1.0, None, ALU.min).then_inc(mk["any"], 1)

        def mask_on_tensor(pe):
            pe.wait_ge(mk["own"], 4)
            pe.matmul(S2[0][:, 0, 0, 0:1], ones32[:, :], mask_hit[:, :], start=True, stop=True).then_inc(mk["count"], 1)

        def scatter_on_gpsimd(pool):
            pool.wait_ge(moe["slots"], 1)
            pool.wait_ge(moe["xn"], B)
            pool.wait_ge(moe["zfill"], 16)
            for i in range(NT):
                pool.indirect_dma_start(xs_dram, bass.IndirectOffsetOnAxis(ap=slot[:, i:i + 1].bitcast(U32), axis=0),
                                        xn2[:, i, :], None).then_inc(moe["scattered"], 16)

        def gather_on_gpsimd(pool):
            pool.wait_ge(moe["stored0"], 16 * ((SLOT_TILES + 1) // 2))
            pool.wait_ge(moe["stored1"], 16 * (SLOT_TILES // 2))
            for i in range(NT):
                pool.indirect_dma_start(yg[:, i, :], None, ys_dram,
                                        bass.IndirectOffsetOnAxis(ap=slot[:, i:i + 1].bitcast(U32), axis=0)) \
                    .then_inc(moe["gathered_first" if i < 2 * QT else "gathered"], 16)

        def tile_exists(s, d):
            return s is None or 0 <= s + d < SLOT_TILES

        def tiles_loop(eng, slot_fn):
            for s in range(-3, 4):
                slot_fn(s, s % 2, s)
            with eng.Fori(2, SLOT_TILES // 2 - 2) as i:
                for par in range(2):
                    slot_fn(2 * i + par, par, None)
            for s in range(SLOT_TILES - 5, SLOT_TILES + 2):
                slot_fn(s, s % 2, s)

        def reused(b):
            return not isinstance(b, int) or b >= 2

        def experts_on_sync(sp):
            sp.wait_ge(moe["scattered"], 16 * NT)
            sp.wait_ge(moe["slots"], 2)

            def load(j, par):
                if reused(j):
                    sp.wait_ge(moe["tT"], j - 1)
                sp.dma_start(xt[par][:, :], xs_dram.rearrange("(j p) d -> j p d", p=P)[j, :, :]).then_inc(moe[f"xt{par}"], 16)

            def store(j, par):
                sp.wait_ge(moe["ysb"], j + 1)
                sp.dma_start(ys_dram.rearrange("(j p) d -> j p d", p=P)[j, :, :], ysb[par][:, :]) \
                  .then_inc(moe[f"stored{par}"], 16)

            def slot_fn(j, par, s):
                if tile_exists(s, 5):
                    load(j + 5, 1 - par)
                if tile_exists(s, -2):
                    store(j - 2, par)
            load(0, 0)
            load(1, 1)
            tiles_loop(sp, slot_fn)

        def experts_on_tensor(pe):
            pe.wait_ge(moe["slots"], 2)
            pe.wait_ge(moe["split"], B)
            pe.wait_ge(moe["brows"], 16 * 6)

            def expert_of(j):
                return pe.value_load(expert[0:1, bass.ds(j, 1)], min_val=0, max_val=NE - 1)

            def weights(layer_of, e, c, a=0, both=False):
                w = w_hl[:, :, :, :].rearrange("p (l e c) a n -> p l e (c a n)", l=2, e=NE)
                n = (2 * c + a) * P
                return w[:, layer_of, bass.ds(e, 1), n:n + (2 * P if both else P)].rearrange("p e n -> p (e n)")

            b1 = b1rows[:, :].rearrange("p (e n) -> p e n", e=NE)

            def first(j, par):
                e = expert_of(j)
                pe.wait_ge(moe["x_lo"], j + 1)
                if reused(j):
                    pe.wait_ge(moe["hs"], j - 1)
                hb = S2[par][:, :, :, :].rearrange("p a k n -> p (a k) n")
                for c in range(HC):
                    pe.matmul(hb[:, c, :], weights(0, e, c), x_hl[par][:, :, :].rearrange("p a n -> p (a n)"), start=True, stop=False)
                    pe.matmul(hb[:, c, 0:P], weights(0, e, c, 1), x_hl[par][:, 0, :], start=False, stop=False)
                    mm = pe.matmul(hb[:, c, 0:P], b1[:, bass.ds(e, 1), c * P:(c + 1) * P].rearrange("p e n -> p (e n)"), ones16[:, :], start=False, stop=True)
                mm.then_inc(moe["h"], 1)

            def turn(j, par):
                pe.wait_ge(moe[f"xt{par}"], 8 * (j - par) + 16)
                if reused(j):
                    pe.wait_ge(moe["x_lo"], j - 1)
                pe.transpose(M[par][:, 0:P], xt[par][:, :], eye[:, :]).then_inc(moe["tT"], 1)

            def second(j, par):
                e = expert_of(j)
                pe.wait_ge(moe["h_lo"], j + 1)
                if reused(j):
                    pe.wait_ge(moe["ysb"], j - 1)
                o = S1[par][:, :, :].rearrange("p q n -> p (q n)")
                for c in range(HC):
                    hs = slice(c * P, (c + 1) * P)
                    pe.matmul(o[:, 0:2 * D], h_hi[par][:, hs], weights(1, e, c, both=True), start=(c == 0), stop=False)
                    pe.matmul(o[:, 0:D], h_lo[par][:, hs], weights(1, e, c), start=False, stop=False)
                pe.matmul(o[:, 0:D], ones16[:, :], b2rows[:, bass.ds(e * D, D)], start=False, stop=True).then_inc(moe["y"], 1)

            def slot_fn(j, par, s):
                if tile_exists(s, 1):
                    first(j + 1, 1 - par)
                if tile_exists(s, 3):
                    turn(j + 3, 1 - par)
                if tile_exists(s, -1):
                    second(j - 1, 1 - par)
            tiles_loop(pe, slot_fn)

        def experts_on_scalar(act):
            def slot_fn(j, par, s):
                if tile_exists(s, 1):
                    act.wait_ge(moe["h"], j + 2)
                    hb = S2[1 - par][:, :, :, :].rearrange("p a k n -> p (a k) n")
                    act.activation(hs[1 - par][:, :].rearrange("p (c n) -> p c n", n=P), hb[:, :, P:2 * P], ACT.Copy) \
                       .then_inc(moe["hr"], 1)
                if tile_exists(s, 3):
                    act.wait_ge(moe["tT"], j + 4)
                    if reused(j + 3):
                        act.wait_ge(moe["h"], j + 2)
                    act.activation(x_hl[1 - par][:, 0, :], M[1 - par][:, 0:P], ACT.Copy).then_inc(moe["x_hi"], 1)
                if tile_exists(s, -2):
                    act.wait_ge(moe["y"], j - 1)
                    if reused(j - 2):
                        act.wait_ge(moe[f"stored{par}"], 8 * (j - 2 - par))
                    act.activation(ysb[par][:, :], S1[par][:, 0, 0:D], ACT.Copy, scale=1.0 / WS).then_inc(moe["yh"], 1)
                if tile_exists(s, 1):
                    act.wait_ge(moe["hs"], j + 2)
                    if reused(j + 1):
                        act.wait_ge(moe["h_lo"], j)
                        act.wait_ge(moe["y"], j)
                    act.activation(hf[1 - par][:, :], hs[1 - par][:, :], ACT.Silu, scale=1.0 / WS).then_inc(moe["hf"], 1)
                    act.wait_ge(moe["hf"], j + 2)
                    act.activation(h_hi[1 - par][:, :], hf[1 - par][:, :], ACT.Copy).then_inc(moe["h_hi"], 1)
            tiles_loop(act, slot_fn)

        def experts_on_vector(v):
            def slot_fn(j, par, s):
                if tile_exists(s, 1):
                    v.wait_ge(moe["hr"], j + 2)
                    hb = S2[1 - par][:, :, :, :].rearrange("p a k n -> p (a k) n")
                    v.tensor_tensor(hs[1 - par][:, :].rearrange("p (c n) -> p c n", n=P), hb[:, :, 0:P],
                                    hs[1 - par][:, :].rearrange("p (c n) -> p c n", n=P), ALU.add).then_inc(moe["hs"], 1)
                if tile_exists(s, 3):
                    v.wait_ge(moe["x_hi"], j + 4)
                    v.tensor_tensor(x_hl[1 - par][:, 1, :], M[1 - par][:, 0:P], x_hl[1 - par][:, 0, :], ALU.subtract) \
                     .then_inc(moe["x_lo"], 1)
                if tile_exists(s, -2):
                    v.wait_ge(moe["yh"], j - 1)
                    v.scalar_tensor_tensor(ysb[par][:, :], S1[par][:, 0, D:2 * D], 1.0 / WS, ysb[par][:, :],
                                           ALU.mult, ALU.add).then_inc(moe["ysb"], 1)
                if tile_exists(s, 1):
                    v.wait_ge(moe["h_hi"], j + 2)
                    v.tensor_tensor(h_lo[1 - par][:, :], hf[1 - par][:, :], h_hi[1 - par][:, :], ALU.subtract) \
                     .then_inc(moe["h_lo"], 1)
            tiles_loop(v, slot_fn)
            v.wait_ge(moe["gate"], 1)
            v.wait_ge(moe["gathered_first"], 16 * 2 * QT)
            add_experts(v, 0, 2 * QT)

        def add_experts(v, start, end):
            for i in range(start, end):
                ii = v.scalar_tensor_tensor(X[:, i, :], yg[:, i, :], gate[:, i:i + 1], X[:, i, :], ALU.mult, ALU.add)
            ii.then_inc(moe["x"], 1)
            v.wait_ge(moe["x"], 2 if start else 1)

        def ffn_loop(eng, slot_fn):
            for s in range(-3, 2):
                slot_fn(s, s % 2, s)
            with eng.Fori(1, 2) as i:
                for par in range(2):
                    slot_fn(2 * i + par, par, None)
            for s in range(4, 10):
                slot_fn(s, s % 2, s)

        def ffn_on_vector(v):
            def apply(b, par):
                if reused(b):
                    v.wait_ge(ff["xT"], b - 1)
                norm_apply(v, b, xn[par], ff["rstd"], ff["xn"])

            def membrane(b, par, new):
                base = 2 * (STEPS - 1) * b
                v.wait_ge(ff["yc"], b + 1)
                if reused(b):
                    v.wait_ge(ff["above"], b - 1)
                for k in range(1, STEPS):
                    if k > 1:
                        v.wait_ge(ff["mem"], base + 2 * k - 2)
                    elif not isinstance(b, int) or b >= 1:
                        v.wait_ge(ff["mem"], base)
                    v.scalar_tensor_tensor(tmp[:, :], mem[par][:, k - 1, :], BETA, mem[par][:, 0, :], ALU.mult, ALU.add) \
                        .then_inc(ff["mem"], 1)
                    v.wait_ge(ff["mem"], base + 2 * k - 1)
                    v.scalar_tensor_tensor(mem[par][:, k, :], mem[par][:, k - 1, :], 1.0, tmp[:, :], ALU.is_gt, ALU.subtract,
                                           reverse1=True).then_inc(ff["mem"], 1)
                    if k == 2 and new:
                        apply(b + 3, 1 - par)

            def result(b, par):
                v.wait_ge(ff["count"], b + 1)
                if reused(b):
                    v.wait_ge(ff[f"stored{par}"], 8 * (b - par))
                v.scalar_tensor_tensor(fin[par][:, :, :].rearrange("p q d -> p (q d)"), S1[1][:, 0, :], 1.0 / STEPS,
                                       X[:, bass.ds(QT * b, QT), :].rearrange("p q d -> p (q d)"),
                                       ALU.mult, ALU.add).then_inc(ff["out"], 1)

            def slot_fn(b, par, s):
                if exists(s, 3):
                    norm_stats(v, b + 3, ff["norm_own"], ff["var"])
                    if not exists(s, 0):
                        apply(b + 3, 1 - par)
                if exists(s, 0):
                    membrane(b, par, exists(s, 3))
                if exists(s, -2):
                    result(b - 2, par)
            ffn_loop(v, slot_fn)

        def ffn_on_gpsimd(pool):
            for b in range(B):
                norm_root(pool, b, ff["var"], ff["rstd"])

        def ffn_on_tensor(pe):
            def slot_fn(b, par, s):
                if exists(s, 1):
                    pe.wait_ge(ff["sq"], b + 2)
                    if reused(b + 1):
                        pe.wait_ge(ff["yc"], b)
                    for q in range(QT):
                        for c in range(HC):
                            mm = pe.matmul(M[1 - par][:, q * D:(q + 1) * D], h2[1 - par][:, c, q * P:(q + 1) * P], wpr[:, c, :],
                                           start=(c == 0), stop=(c == HC - 1))
                    mm.then_inc(ff["y"], 1)
                if exists(s, 2):
                    pe.wait_ge(ff["xTc"], b + 3)
                    if reused(b + 2):
                        pe.wait_ge(ff["relu"], b + 1)
                    for c in range(HC):
                        mm = pe.matmul(S2[par][:, c // 2, c % 2, :], wfc[:, c * P:(c + 1) * P], gT[par][:, :],
                                       start=True, stop=True)
                    mm.then_inc(ff["h"], 1)
                if exists(s, 3):
                    pe.wait_ge(ff["xn"], b + 4)
                    if s != -3:
                        pe.wait_ge(ff["xTc"], b + 3)
                    for q in range(QT):
                        mm = pe.transpose(S1[0][:, q, 0:P], xn[1 - par][:, q, :], eye[:, :])
                    mm.then_inc(ff["xT"], 1)
                if exists(s, -1):
                    pe.wait_ge(ff["spike"], b)
                    if not (isinstance(b, int) and b == 1):
                        pe.wait_ge(ff["out"], b - 1)
                    for k in range(STEPS):
                        mm = pe.matmul(S1[1][:, 0, :], eye16[:, :], spike[1 - par][:, k, :], start=(k == 0),
                                       stop=(k == STEPS - 1))
                    mm.then_inc(ff["count"], 1)
            ffn_loop(pe, slot_fn)

        def ffn_on_scalar(act):
            def slot_fn(b, par, s):
                if exists(s, -1):
                    act.wait_ge(ff["mem"], 2 * (STEPS - 1) * b)
                    if not (isinstance(b, int) and b == 1):
                        act.wait_ge(ff["spike"], b - 1)
                    act.activation(above[:, :, :], mem[1 - par][:, 0:STEPS, :], ACT.Relu, bias=minus_one[:, :]) \
                       .then_inc(ff["above"], 1)
                if exists(s, 1):
                    act.wait_ge(ff["y"], b + 2)
                    if reused(b + 1):
                        act.wait_ge(ff["above"], b)
                    act.activation(mem[1 - par][:, 0, :], M[1 - par][:, 0:S], ACT.Copy).then_inc(ff["yc"], 1)
                if exists(s, -1):
                    act.wait_ge(ff["above"], b)
                    if reused(b - 1):
                        act.wait_ge(ff["count"], b - 2)
                    act.activation(spike[1 - par][:, :, :], above[:, :, :], ACT.Sign).then_inc(ff["spike"], 1)
                if exists(s, 2):
                    flat = hr[par].rearrange("p c n -> p (c n)")
                    act.wait_ge(ff["h"], b + 3)
                    act.activation(flat, S2[par][:, :, :, :].rearrange("p a k n -> p (a k n)"), ACT.Relu) \
                       .then_inc(ff["relu"], 1)
                    act.wait_ge(ff["relu"], b + 3)
                    if reused(b + 2):
                        act.wait_ge(ff["y"], b + 1)
                    act.activation(h2[par].rearrange("p c n -> p (c n)"), flat, ACT.Square).then_inc(ff["sq"], 1)
                if exists(s, 3):
                    act.wait_ge(ff["xT"], b + 4)
                    if reused(b + 3):
                        act.wait_ge(ff["h"], b + 2)
                    act.activation(gT[1 - par][:, :].rearrange("p (q n) -> p q n", q=QT), S1[0][:, :, 0:P], ACT.Copy) \
                       .then_inc(ff["xTc"], 1)
            ffn_loop(act, slot_fn)

        def ffn_on_sync(sp):
            for b in range(B):
                sp.wait_ge(ff["out"], b + 1)
                sp.dma_start(out[b, :, :].rearrange("(q p) d -> p q d", p=P), fin[b % 2][:, :, :]) \
                  .then_inc(ff[f"stored{b % 2}"], 16)
            for par in range(2):
                sp.wait_ge(ff[f"stored{par}"], 16 * (B // 2))

        def rows_of_maximum(kt, g, copy):
            copy(kt[M0:P, HG * g:HG * g + HG, :], head_mask[M0:P, :].unsqueeze(2).to_broadcast([P - M0, HG, S])) \
                .then_inc(inited, 1)

        @block.sync
        def _(sp):
            first = QT * 2
            for dst, src in [(X[:, 0:first, :], t["x"][:, 0:first, :]), (W["q", 0][:, :], t["wq0"]), (W["k", 0][:, :], t["wk0"]),
                             (W["v", 0][:, :], t["wv0"])]:
                sp.dma_start(dst, src).then_inc(loaded, 16)
            sp.dma_start(X[:, first:NT, :], t["x"][:, first:NT, :]).then_inc(loaded_x, 16)
            late = [(W[n, 1][:, :], t[f"w{n}1"]) for n in "qkvo"]
            late += [(slope[:, :], t["c_slope"]), (before[:, :], t["c_before"]), (route_c[:, :, :], t["c_route"]),
                     (wg[:, :], t["wg"]), (bg[:, :], t["bg"].partition_broadcast(P)), (braw[:, :], t["braw"]),
                     (wfc[:, :], t["wfc"]), (wpr[:, :, :], t["wpr"])]
            late += [(pos_i[b * H:(b + 1) * H, :], t["pos"][b:b + 1, :].partition_broadcast(H)) for b in range(B)]
            assert len(late) == N_LATE
            attention_on_sync(sp, ly[0], late)
            sp.wait_ge(inited, N_INIT)
            sp.dma_start(xs_dram.rearrange("(j p) d -> p j d", p=P), zero[:, :].unsqueeze(1).to_broadcast([P, SLOT_TILES, D])) \
              .then_inc(moe["zfill"], 16)
            mask_on_sync(sp)
            sp.wait_ge(moe["bsplit"], 5)
            for c in range(PARTS):
                sp.dma_start(b1rows[c:c + 1, :], bparts[:, c, 0:32]).then_inc(moe["brows"], 16)
                sp.dma_start(b2rows[c:c + 1, :], bparts[:, c, 32:40]).then_inc(moe["brows"], 16)
            sp.wait_ge(pos_ready, 1)
            sp.dma_start(pos_dram.rearrange("b h c n -> (b h) c n"), pos_parts[:, :, :]).then_inc(pos_stored, 16)
            experts_on_sync(sp)
            sp.wait_ge(pos_stored, 16)
            attention_on_sync(sp, ly[1], [])
            ffn_on_sync(sp)

        @block.gpsimd
        def _(pool):
            pool.wait_ge(loaded, 16 * N_LOADS)
            pool.wait_ge(inited, N_INIT)
            attention_on_gpsimd(pool, ly[0])
            gate_on_gpsimd(pool)
            scatter_on_gpsimd(pool)
            gather_on_gpsimd(pool)
            attention_on_gpsimd(pool, ly[1])
            ffn_on_gpsimd(pool)

        @block.scalar
        def _(act):
            for dst, src in [(eye[:, :], t["c_eye"]), (head_mask[:, :], t["c_head_mask"]), (qkb[:, :], t["qkb"]),
                             (vb[:, :], t["vb"].partition_broadcast(P)), (W["o", 0][:, :], t["wo0"]),
                             (ob[:, :], t["ob"].partition_broadcast(P))]:
                act.dma_start(dst, src).then_inc(loaded, 16)
            act.wait_ge(loaded, 16 * N_LOADS)
            for g in range(NG):
                rows_of_maximum(Kt[1], g, lambda o, i: act.activation(o, i, ACT.Copy))
            act.wait_ge(inited, N_INIT)
            attention_on_scalar(act, ly[0])
            gate_on_scalar(act)
            experts_on_scalar(act)
            attention_on_scalar(act, ly[1])
            ffn_on_scalar(act)

        @block.vector
        def _(v):
            v.memset(X[:, NT:NT + QT, :], 0.0).then_inc(inited, 1)
            v.memset(mhalf[:, :], -0.5).then_inc(inited, 1)
            v.memset(minus_one[:, :], -1.0).then_inc(inited, 1)
            v.memset(zero[:, :], 0.0).then_inc(inited, 1)
            v.memset(ones32[:, :], 1.0).then_inc(inited, 1)
            v.memset(ones16[:, :], 1.0).then_inc(inited, 1)
            for i in range(2):
                v.memset(Qt[i][M0:P, :, :], MROW).then_inc(inited, 1)
                v.memset(Vt[i][:, :, :, :], 0.0).then_inc(vt_zeroed, 1)
            v.wait_ge(vt_zeroed, 2)
            for i in range(2):
                v.memset(Vt[i][:, :, :, DH], 1.0).then_inc(inited, 1)
            v.wait_ge(loaded, 16 * N_LOADS)
            for g in range(NG):
                rows_of_maximum(Kt[0], g, v.tensor_copy)
            v.tensor_copy(eye16[:, :], eye[:, :]).then_inc(inited, 1)
            v.tensor_copy(eye_bf[:, :], eye[:, :]).then_inc(inited, 1)
            v.tensor_scalar(qkbs[:, 0:1], qkb[:, 0:1], QK / float(np.sqrt(DH)), None, ALU.mult).then_inc(inited, 1)
            v.tensor_scalar(qkbs[:, 1:2], qkb[:, 1:2], QK, None, ALU.mult).then_inc(inited, 1)
            v.wait_ge(inited, N_INIT)
            attention_on_vector(v, ly[0])
            gate_on_vector(v)
            route_on_vector(v)
            biases_on_vector(v)
            mask_on_vector(v)
            experts_on_vector(v)
            attention_on_vector(v, ly[1])
            ffn_on_vector(v)

        @block.tensor
        def _(pe):
            pe.wait_ge(loaded, 16 * N_LOADS)
            pe.wait_ge(inited, N_INIT)
            attention_on_tensor(pe, ly[0], False)
            gate_on_tensor(pe)
            mask_on_tensor(pe)
            experts_on_tensor(pe)
            pe.wait_ge(mk["any"], 1)
            any_masked = pe.value_load(mask_any[0:1, 0:1], min_val=0, max_val=1)
            with pe.If(any_masked == 1):
                attention_on_tensor(pe, ly[1], True)
            with pe.Else():
                attention_on_tensor(pe, ly[1], False)
            ffn_on_tensor(pe)


def q_order():
    return [(HG * (2 * hf + g2) + i) * DH + d for hf in range(2) for i in range(HG) for d in range(DH) for g2 in range(2)]


def k_order():
    return [(HG * g + i) * DH + d for i in range(HG) for d in range(DH) for g in range(NG)]


def kernel(**inputs):
    import concourse.bacc as bacc
    from concourse.bass_utils import run_bass_kernel_spmd

    a = {k: np.asarray(v) for k, v in inputs.items()}
    lay = np.ascontiguousarray
    qo, ko = q_order(), k_order()
    arrays = {
        "x": lay(a["x"].reshape(NT, P, D).transpose(1, 0, 2)),
        "ctxT": lay(a["ctx_1024"].transpose(2, 0, 1)),
        "pos": lay(a["itok_BxS2_1_8191"]),
        "qkb": lay(np.stack([a["L0_xattn_wq_b"][qo], a["L0_xattn_wk_b"][ko]], axis=1)),
        "vb": a["L0_xattn_wv_b"], "ob": a["L0_xattn_wo_b"],
        "mask": lay(a["mask_BxSxS2_if1"].reshape(NT, P, S).transpose(1, 0, 2).reshape(P, NT * S)),
        "wg": a["L0_ffn_Wg"], "bg": a["L0_ffn_bg"],
        "w": lay(np.concatenate([a["L0_ffn_W1"].transpose(1, 0, 2).reshape(P, NE * HC, P),
                                 a["L0_ffn_W2"].reshape(NE, HC, P, D).transpose(2, 0, 1, 3).reshape(P, NE * HC, D)], axis=1)),
        "braw": lay(np.concatenate([a["L0_ffn_b1"].reshape(P, 32), a["L0_ffn_b2"].reshape(P, 8)], axis=1)),
        "wfc": lay(a["L1_ffn_W_fc"].T),
        "wpr": lay(a["L1_ffn_W_proj"].T.reshape(HC, P, D).transpose(1, 0, 2)),
    }
    for L, names in enumerate((("L0_xattn_wq_w", "L0_xattn_wk_w", "L0_xattn_wv_w", "L0_xattn_wo_w"),
                               ("L1_xattn_W_q", "L1_xattn_W_k", "L1_xattn_W_v", "L1_xattn_W_o"))):
        for n, name in zip("qkvo", names):
            w = a[name].T
            arrays[f"w{n}{L}"] = lay(w[:, qo] if n == "q" else w[:, ko] if n == "k" else w)
    arrays.update(constants())
    nc = bacc.Bacc("TRN2", target_bir_lowering=False, num_devices=1)
    t = {n: nc.dram_tensor(f"in_{n}", v.shape, mybir.dt.from_np(v.dtype), kind="ExternalInput").ap()
         for n, v in arrays.items()}
    out = nc.dram_tensor("out", (B, S, D), F32, kind="ExternalOutput").ap()
    build(nc, t, out)
    r = run_bass_kernel_spmd(nc, [{f"in_{n}": v for n, v in arrays.items()}], core_ids=[0])
    return r.results[0]["out"]
```

```python
from contextlib import ExitStack

import numpy as np

import concourse.bass as bass
from concourse import mybir

F32 = mybir.dt.float32
F16 = mybir.dt.float16
BF16 = mybir.dt.bfloat16
I32 = mybir.dt.int32
U32 = mybir.dt.uint32
ALU = mybir.AluOpType
ACT = mybir.ActivationFunctionType
AX = mybir.AxisListType

P = 128
B, S, D, H = 8, 256, 128, 16
DH = D // H
QT = S // P
NT = B * QT
HG = 4
NG = H // HG
NE, HID = 8, 512
HC = HID // P
EPS = 1e-5
STEPS, BETA = 5, 0.9
W_BLOCKS = 2 * NE * HC
W_CHUNK = W_BLOCKS // B
SLOT_TILES = NT + NE - 1
QK = 16.0
SC = QK * QK
MROW = 64.0
WS = 64.0
M0, MROWS = 96, 3 * HG
PB0 = M0 + MROWS
K_ROWS = PB0 + 3
PARTS = 3
MASKED = -1e30


def constants():
    eye = np.eye(P, dtype=np.float32)
    before = np.triu(np.ones((P, P), np.float32), 1)
    head_mask = np.zeros((P, HG), np.float32)
    for r in range(3 * 32):
        head_mask[r, (r % 32) // DH] = 1.0
    for r in range(MROWS):
        head_mask[M0 + r, r // 3] = MROW
    slopes = (2.0 ** (-8.0 / H)) ** np.arange(1, H + 1, dtype=np.float64)
    slope_col = np.tile(slopes.astype(np.float32), B)[:, None]
    route = np.zeros((P, 3, P), np.float32)
    route[:, 0] = np.tile(np.arange(NE) - NE, NT)
    run = np.ones((NE, NT), np.float32)
    run[:, 0] = 0.0
    route[:, 1] = run.reshape(-1)
    route[:, 2] = np.arange(P)
    return {"c_eye": eye, "c_before": before, "c_head_mask": head_mask, "c_slope": slope_col,
            "c_route": route}


def layer(index, sem):
    names = ["ctx_loaded", "norm_own", "xvar", "xrstd", "xn_ready", "xnT_done", "xnT_copied",
             "q_done", "q_copied", "k_done", "k_copied", "v_done", "v_copied", "q_hi", "q_lo",
             "k_hi", "k_lo", "k_rep", "k_tile", "m_zeroed", "p1_done", "max_done", "m_parts", "own",
             "mT_done", "mT_copied", "p2_done", "exp_done", "pv_done", "o_copied", "ot_done",
             "ot_norm", "o_rc", "aT_done", "aT_copied", "op_done", "x_added"]
    ly = {n: sem(f"L{index}_{n}") for n in names}
    ly.update(index=index, bias=index == 0, position=index == 1)
    ly["q_tile"] = [sem(f"L{index}_q_tile{i}") for i in range(2)]
    if ly["position"]:
        ly["k_pos"] = [[sem(f"L{index}_k_pos{i}{par}") for par in range(2)] for i in range(2)]
        ly["ot_sum"] = sem(f"L{index}_ot_sum")
    else:
        ly["x_biased"] = sem(f"L{index}_x_biased")
    return ly


def build(nc, t, out):
    with ExitStack() as ctx:
        def sb(name, shape, dt=F32):
            return ctx.enter_context(nc.sbuf_tensor(name, shape, dt))

        def psum(name, shape, dt=F32):
            return ctx.enter_context(nc.psum_tensor(name, shape, dt))

        def sem(name):
            return ctx.enter_context(nc.semaphore(name))

        X = sb("X", [P, NT + QT, D])
        eye = sb("eye", [P, P])
        eye16 = sb("eye16", [P, P], F16)
        head_mask = sb("head_mask", [P, HG])
        W = {}
        for L in range(2):
            for n in "qkvo":
                W[n, L] = sb(f"w{n}{L}", [P, D])
        qkb = sb("qkb", [P, 2])
        qkbs = sb("qkbs", [P, 2])
        vb = sb("vb", [P, D])
        ob = sb("ob", [P, D])
        ctxT = [sb(f"ctxT{i}", [P, S]) for i in range(2)]
        xn = [sb(f"xn{i}", [P, QT, D]) for i in range(2)]
        st6 = sb("st6", [P, QT, 6])
        mv = sb("mv", [P, QT, 2])
        ve = sb("ve", [P, QT])
        rstd = sb("rstd", [P, QT])
        carried_v = sb("carried_v", [P, QT])
        mhalf = sb("mhalf", [P, NT])
        xnT = sb("xnT", [P, S])
        qf, kf = sb("qf", [P, S]), sb("kf", [P, S])
        q_hi = [sb(f"q_hi{i}", [P, S], F16) for i in range(2)]
        q_lo = [sb(f"q_lo{i}", [P, S], F16) for i in range(2)]
        k_hi, k_lo = sb("k_hi", [P, S], F16), sb("k_lo", [P, S], F16)
        k_rep = sb("k_rep", [P, NG, S], F16)
        Qt = [sb(f"Qt{i}", [P, NG, S], F16) for i in range(2)]
        Kt = [sb(f"Kt{i}", [P, H, S], F16) for i in range(2)]
        Vt = [sb(f"Vt{i}", [P, QT, H, 32]) for i in range(2)]
        nm = [sb(f"nm{i}", [P, QT, H]) for i in range(2)]
        mr = sb("mr", [P, QT, 8])
        mparts = [sb(f"mparts{i}", [P, QT, H, PARTS], F16) for i in range(2)]
        Pt = [sb(f"Pt{i}", [P, HG, QT * S]) for i in range(NG)]
        Osb = [sb(f"Osb{i}", [P, NG, S]) for i in range(2)]
        rc = sb("rc", [P, QT, H])
        rsum = sb("rsum", [P, QT, H])
        attn = sb("attn", [P, QT, D])
        aT = sb("aT", [P, S])
        S1 = [psum(f"S1_{i}", [P, QT, S]) for i in range(2)]
        S2 = [psum(f"S2_{i}", [P, 2, QT, S]) for i in range(2)]
        M = [psum(f"M{i}", [P, 512]) for i in range(2)]
        M16 = [m[:, :].bitcast(F16) for m in M]
        O_BANK = (1, 0, 1, 1)

        pos_i = sb("pos_i", [P, S], I32)
        pos_f = sb("pos_f", [P, S])
        slope = sb("slope", [P, 1])
        pos_r = sb("pos_r", [P, S])
        pos_parts = sb("pos_parts", [P, PARTS, S], F16)

        mask_bias = sb("mask_bias", [P, NT, S], BF16)
        eye_bf = sb("eye_bf", [P, P], BF16)
        mask_min = sb("mask_min", [P, 1])
        mask_hit = sb("mask_hit", [P, 1])
        mask_any = sb("mask_any", [P, 1], I32)
        mk = {n: sem(f"mask_{n}") for n in ("raw", "own", "count", "any")}

        ly = [layer(0, sem), layer(1, sem)]
        loaded, loaded_x, loaded_late, pos_stored = sem("loaded"), sem("loaded_x"), sem("loaded_late"), sem("pos_stored")
        inited, vt_zeroed = sem("inited"), sem("vt_zeroed")
        kt_rows = sem("kt_rows")
        N_LOADS, N_LOADS_X, N_LATE = 6, 5, 21
        N_PARTS_MADE = 8
        N_INIT = 6 + 2 + 2 + 4
        pos_dram = nc.dram_tensor("pos_parts_dram", (B, H, PARTS, S), F16).ap()
        parts_made = sem("parts_made")
        w_hl = sb("w_hl", [P, W_BLOCKS, 2, P], F16)
        wraw = [sb(f"wraw{i}", [P, W_CHUNK, P]) for i in range(2)]
        b1c = sb("b1c", [P, HC, NE])
        b1s = sb("b1s", [P, HC, NE])
        braw = sb("braw", [P, NE * D // P])
        brest = sb("brest", [P, NE * D // P])
        bparts = sb("bparts", [P, PARTS, NE * D // P], F16)
        b2rows = sb("b2rows", [P, NE * D], F16)
        ones16 = sb("ones16", [P, P], F16)
        wg = sb("wg", [P, NE])
        bg = sb("bg", [P, NE])
        xn2 = Pt[2][:, :, :].rearrange("p i (t d) -> p (i t) d", d=D)
        before = sb("before", [P, P])
        ones32 = sb("ones32", [P, P])
        route_c = sb("route_c", [P, 3, P])
        logit = sb("logit", [P, NT, NE])
        top = sb("top", [P, NT])
        onehot = sb("onehot", [P, NT, NE])
        t1 = sb("t1", [P, NT, NE])
        t2 = sb("t2", [P, NT, NE])
        first = sb("first", [P, NT])
        gate = sb("gate", [P, NT])
        gsum = sb("gsum", [P, NT])
        tot = sb("tot", [P, NE, NT])
        cum = sb("cum", [P, NE, NT])
        rbase = sb("rbase", [P, NE, NT])
        cnt_i = sb("cnt_i", [P, NE], I32)
        cnt_s = sb("cnt_s", [P, NE], I32)
        ntile = sb("ntile", [P, NE])
        tend = sb("tend", [P, NE])
        tstart = sb("tstart", [P, NE])
        slotf = sb("slotf", [P, NT])
        slot = sb("slot", [P, NT], I32)
        cmp = sb("cmp", [P, SLOT_TILES, NE])
        expf = sb("expf", [P, SLOT_TILES])
        expert = sb("expert", [P, SLOT_TILES], I32)
        zero = sb("zero", [P, D])
        xs_dram = nc.dram_tensor("sorted_x", (SLOT_TILES * P, D), F32).ap()
        ys_dram = nc.dram_tensor("sorted_y", (SLOT_TILES * P, D), F32).ap()
        gT = [sb(f"gT{i}", [P, S]) for i in range(2)]
        st_all = sb("st_all", [P, NT, 6])
        mv_all = sb("mv_all", [P, NT, 2])
        ve_all = sb("ve_all", [P, NT])
        rstd_all = sb("rstd_all", [P, NT])
        xt = [sb(f"xt{i}", [P, D]) for i in range(2)]
        x_hl = [sb(f"x_hl{i}", [P, 2, P], F16) for i in range(2)]
        hs = [sb(f"hs{i}", [P, HID]) for i in range(2)]
        hf = [sb(f"hf{i}", [P, HID]) for i in range(2)]
        h_hi = [sb(f"h_hi{i}", [P, HID], F16) for i in range(2)]
        h_lo = [sb(f"h_lo{i}", [P, HID], F16) for i in range(2)]
        ysb = [sb(f"ysb{i}", [P, D]) for i in range(2)]
        yg = Pt[3][:, :, :].rearrange("p i (t d) -> p (i t) d", d=D)
        moe = {n: sem(f"moe_{n}") for n in (
            "wraw0", "wraw1", "split", "scaled", "w_hi", "bsplit", "brows", "zfill",
            "norm_own", "var", "rstd", "xn", "xT", "xTc", "gm", "logit",
            "r", "exp", "gate", "onehot", "ranks", "slots", "scattered", "tT", "x_hi", "x_lo", "h", "hr", "hs", "hf",
            "h_hi", "h_lo", "y", "yh", "ysb", "gathered0", "gathered1", "gathered", "x", "xt0", "xt1", "stored0", "stored1")}
        wfc = sb("wfc", [P, HID])
        wpr = sb("wpr", [P, HC, D])
        hr, h2 = ([Pt[n][:, 2 * i:2 * i + 2, :].rearrange("p a (k n) -> p (a k) n", k=QT) for i in range(2)]
                  for n in range(2))
        mem = [Pt[2 + i][:, :, :].rearrange("p i (k n) -> p (i k) n", n=S) for i in range(2)]
        spike = [sb(f"spike{i}", [P, STEPS, S], F16) for i in range(2)]
        above = sb("above", [P, STEPS, S])
        minus_one = sb("minus_one", [P, 1])
        tmp = sb("tmp", [P, S])
        fin = [sb(f"fin{i}", [P, QT, D]) for i in range(2)]
        ff = {n: sem(f"ff_{n}") for n in ("norm_own", "var", "rstd", "xn", "xT", "xTc", "h", "relu", "sq", "y",
                                          "yc", "mem", "above", "spike", "count", "out", "stored0", "stored1")}
        block = ctx.enter_context(nc.Block())

        def slots_loop(eng, slot_fn):
            for s in (-3, -2, -1, 0, 1):
                slot_fn(s, s % 2, s)
            with eng.Fori(1, 3) as i:
                for par in range(2):
                    slot_fn(2 * i + par, par, None)
            for s in (6, 7, 8):
                slot_fn(s, s % 2, s)

        def keys_ahead(ly, s):
            return s == -2

        def exists(s, d):
            return s is None or 0 <= s + d < B

        def attention_on_tensor(pe, ly, masked, ffn=None):
            def p1(b, par, h):
                if h % 8 == 0:
                    pe.wait_ge(ly["q_tile"][h // 8], 48 * b + 48)
                    pe.wait_ge(ly["k_tile"], 2 * b + h // 8 + 1)
                    pe.wait_ge(ly["m_zeroed"], 2 * b + h // 8 + 1)
                    if ly["position"]:
                        pe.wait_ge(ly["k_pos"][h // 8][par], 8 * (b - par) + 16)
                if not (isinstance(b, int) and b == 0 and h < 2):
                    pe.wait_ge(ly["max_done"], 16 * b + h - 1)
                for q in range(QT):
                    mm = pe.matmul(S1[h % 2][:, q, :], Qt[par][0:K_ROWS, h // HG, q * P:(q + 1) * P],
                                   Kt[par][0:K_ROWS, h, :], start=True, stop=not masked)
                    if masked:
                        mm = pe.matmul(S1[h % 2][:, q, :], eye_bf[:, :], mask_bias[:, bass.ds(b * QT + q, 1), :]
                                       .rearrange("p t n -> p (t n)"), start=False, stop=True)
                mm.then_inc(ly["p1_done"], 1)

            def p2(b, par, pair):
                if pair % 4 == 0:
                    pe.wait_ge(ly["mT_copied"], 2 * b + pair // 4 + 1)
                if not (isinstance(b, int) and b == 0 and pair < 2):
                    pe.wait_ge(ly["exp_done"], 8 * b + pair - 1)
                for hh in range(2):
                    h = 2 * pair + hh
                    for k in range(QT):
                        mm = pe.matmul(S2[pair % 2][:, hh, k, :], Kt[par][0:K_ROWS, h, k * P:(k + 1) * P],
                                       Qt[par][0:K_ROWS, h // HG, :], start=True, stop=not masked)
                        for q in range(QT if masked else 0):
                            mm = pe.matmul(S2[pair % 2][:, hh, k, q * P:(q + 1) * P],
                                           mask_bias[:, bass.ds(b * QT + q, 1), k * P:(k + 1) * P]
                                           .rearrange("p t n -> p (t n)"), eye_bf[:, :],
                                           start=False, stop=q == QT - 1)
                mm.then_inc(ly["p2_done"], 1)

            def pv(b, par, g):
                pe.wait_ge(ly["exp_done"], 8 * b + 2 * g + 2)
                if g == 0:
                    pe.wait_ge(ly["v_copied"], b + 1)
                for k in range(QT):
                    for i in range(HG):
                        mm = pe.matmul(M[O_BANK[g]][32 * i:32 * i + 32, 0:S], Vt[par][:, k, HG * g + i, :],
                                       Pt[g][:, i, k * S:(k + 1) * S], start=(k == 0), stop=(k == QT - 1))
                mm.then_inc(ly["pv_done"], 1)

            def m_turn(b, par, half, bank):
                pe.wait_ge(ly["m_parts"], 2 * b + half + 1)
                for g in range(2):
                    for q in range(QT):
                        h = 8 * half + HG * g
                        mm = pe.transpose(M16[bank][0:MROWS, g * S + q * P:g * S + (q + 1) * P],
                                          mparts[par][:, q, h:h + HG, :].rearrange("p h c -> p (h c)"), eye16[:, :])
                mm.then_inc(ly["mT_done"], 1)

            def slot_fn(b, par, s):
                new, nxt, cur, old, older = (exists(s, d) for d in (2, 1, 0, -1, -2))
                par1 = 1 - par
                if s == -1 and ly["bias"]:
                    pe.wait_ge(kt_rows, 2 * NG)
                    pe.wait_ge(loaded_x, 16 * N_LOADS_X)

                def pair(i):
                    if nxt:
                        p1(b + 1, par1, 2 * i)
                        p1(b + 1, par1, 2 * i + 1)
                    if cur:
                        p2(b, par, i)

                pair(0)
                if ffn and s == B:
                    pe.wait_ge(ly["exp_done"], 8 * B - 1)
                    ffn_start(ffn, -2)
                if new:
                    pe.wait_ge(ly["xn_ready"], b + 3)
                    if older:
                        pe.wait_ge(ly["x_added"], b - 1)
                    elif old:
                        pe.wait_ge(ly["o_copied"], 4 * b - 2)
                    elif cur:
                        pe.wait_ge(ly["mT_copied"], 2 * b + 1)
                    elif nxt:
                        pe.wait_ge(ly["k_copied"], b + 2)
                    else:
                        pe.wait_ge(ly["k_copied"], 1)
                    for q in range(QT):
                        mm = pe.transpose(M[0][:, q * P:(q + 1) * P], xn[par][:, q, :], eye[:, :])
                    mm.then_inc(ly["xnT_done"], 1)
                pair(1)
                if old:
                    pe.wait_ge(ly["o_copied"], 4 * b - 1)
                    pv(b - 1, par1, 3)
                if new:
                    pe.wait_ge(ly["xnT_copied"], b + 3)
                    pe.matmul(M[0][:, 0:S], W["q", ly["index"]][:, :], xnT[:, :], start=True,
                              stop=True).then_inc(ly["q_done"], 1)
                pair(2)
                if cur:
                    if old:
                        pe.wait_ge(ly["o_copied"], 4 * b)
                    m_turn(b, par, 1, 1)
                if new and not keys_ahead(ly, s):
                    pe.wait_ge(ly["q_copied"], b + 3)
                    pe.wait_ge(ly["ctx_loaded"], 16 * b + 48)
                    pe.matmul(M[0][:, 0:S], W["k", ly["index"]][:, :], ctxT[par][:, :], start=True,
                              stop=True).then_inc(ly["k_done"], 1)
                pair(3)
                if cur:
                    pe.wait_ge(ly["mT_copied"], 2 * b + 2)
                    pv(b, par, 0)
                if nxt:
                    if new:
                        pe.wait_ge(ly["k_copied"], b + 3)
                    else:
                        pe.wait_ge(ly["x_added"], b - 1)
                    for k in range(QT):
                        mm = pe.matmul(M[0][:, k * D:(k + 1) * D], ctxT[par1][:, k * P:(k + 1) * P],
                                       W["v", ly["index"]][:, :], start=True, stop=True)
                    mm.then_inc(ly["v_done"], 1)

                def o_turn(q):
                    for g in range(NG):
                        mm = pe.transpose(M[1][:, g * P:(g + 1) * P], Osb[par1][:, g, q * P:(q + 1) * P], eye[:, :])
                    mm.then_inc(ly["ot_done"], 1)

                if old:
                    pe.wait_ge(ly["o_copied"], 4 * b + 1 if cur else 4 * b)
                    o_turn(0)
                gating = s == B and ly["bias"]
                if gating:
                    gate_products(pe, 0, 2)
                pair(4)
                if ffn and s == B - 1:
                    ffn_start(ffn, -3)
                if nxt:
                    pe.wait_ge(ly["v_copied"], b + 2)
                    m_turn(b + 1, par1, 0, 0)
                pair(5)
                if cur:
                    if nxt:
                        pe.wait_ge(ly["mT_copied"], 2 * b + 3)
                    else:
                        pe.wait_ge(ly["x_added"], b - 1)
                    pv(b, par, 1)
                if old:
                    pe.wait_ge(ly["ot_norm"], 2 * b - 1)
                    o_turn(1)
                if gating:
                    gate_products(pe, 2, 4)
                pair(6)
                if old:
                    pe.wait_ge(ly["ot_norm"], 2 * b)
                    for q in range(QT):
                        mm = pe.transpose(M[1][:, q * P:(q + 1) * P], attn[:, q, :], eye[:, :])
                    mm.then_inc(ly["aT_done"], 1)
                if gating:
                    gate_products(pe, 4, GATE_AHEAD)
                pair(7)
                if old:
                    pe.wait_ge(ly["aT_copied"], b)
                    if cur:
                        pe.wait_ge(ly["o_copied"], 4 * b + 2)
                    else:
                        pe.wait_ge(ly["x_added"], b - 1)
                    for q in range(QT):
                        mm = pe.matmul(M[0][:, q * D:(q + 1) * D], aT[:, q * P:(q + 1) * P], W["o", ly["index"]][:, :],
                                       start=True, stop=True)
                    mm.then_inc(ly["op_done"], 1)
                if cur:
                    if old:
                        pe.wait_ge(ly["aT_copied"], b)
                    else:
                        pe.wait_ge(ly["o_copied"], 4 * b + 1)
                    pv(b, par, 2)

            slots_loop(pe, slot_fn)

        def first_keys_on_tensor(pe, ly):
            pe.wait_ge(ly["ctx_loaded"], 16)
            pe.matmul(M[0][:, 0:S], W["k", ly["index"]][:, :], ctxT[0][:, :], start=True, stop=True).then_inc(ly["k_done"], 1)

        def keys_on_scalar(act, ly, b, nxt):
            act.wait_ge(ly["k_done"], b + 3)
            if nxt:
                act.wait_ge(ly["k_lo"], b + 2)
            act.activation(kf[:, :], M[0][:, 0:S], ACT.Identity, bias=qkbs[:, 1:2] if ly["bias"] else 0.0,
                           scale=QK).then_inc(ly["k_copied"], 1)
            act.wait_ge(ly["k_copied"], b + 3)
            if nxt:
                act.wait_ge(ly["k_rep"], 48 * (b + 2))
            act.activation(k_hi[:, :], kf[:, :], ACT.Copy).then_inc(ly["k_hi"], 1)

        def attention_on_scalar(act, ly, ffn=None):
            def o_copy(b, par, g):
                act.wait_ge(ly["pv_done"], 4 * b + g + 1)
                act.activation(Osb[par][:, g, :], M[O_BANK[g]][:, 0:S], ACT.Copy).then_inc(ly["o_copied"], 1)

            def slot_fn(b, par, s):
                new, nxt, cur, old, older = (exists(s, d) for d in (2, 1, 0, -1, -2))

                def exp(i):
                    if not cur:
                        return
                    if i % 2 == 0 and old:
                        act.wait_ge(ly["pv_done"], 4 * b - 3 + i // 2)
                    act.wait_ge(ly["p2_done"], 8 * b + i + 1)
                    act.activation(Pt[i // 2][:, 2 * (i % 2):2 * (i % 2) + 2, :].rearrange("p a n -> p (a n)"),
                                   S2[i % 2][:, :, :, :].rearrange("p a k n -> p (a k n)"), ACT.Exp,
                                   scale=1.0 / SC).then_inc(ly["exp_done"], 1)

                def m_copy(bb, pp, half, bank):
                    act.wait_ge(ly["mT_done"], 2 * bb + half + 1)
                    act.activation(Qt[pp][M0:M0 + MROWS, 2 * half:2 * half + 2, :].rearrange("p g n -> p (g n)"),
                                   M16[bank][0:MROWS, 0:2 * S], ACT.Copy).then_inc(ly["mT_copied"], 1)

                exp(0)
                if new:
                    act.wait_ge(ly["xnT_done"], b + 3)
                    if nxt:
                        act.wait_ge(ly["q_done"], b + 2)
                    act.activation(xnT[:, :], M[0][:, 0:S], ACT.Copy).then_inc(ly["xnT_copied"], 1)
                exp(1)
                if old:
                    o_copy(b - 1, 1 - par, 3)
                if ffn and s == B:
                    ffn_start(ffn, -2)
                if new:
                    act.wait_ge(ly["q_done"], b + 3)
                    if nxt:
                        act.wait_ge(ly["q_lo"], b + 2)
                    act.activation(qf[:, :], M[0][:, 0:S], ACT.Identity, bias=qkbs[:, 0:1] if ly["bias"] else 0.0,
                                   scale=QK / float(np.sqrt(DH))).then_inc(ly["q_copied"], 1)
                    act.wait_ge(ly["q_copied"], b + 3)
                    if cur:
                        act.wait_ge(ly["q_tile"][1], 48 * b + 48)
                    act.activation(q_hi[par][:, :], qf[:, :], ACT.Copy).then_inc(ly["q_hi"], 1)
                exp(2)
                if cur:
                    m_copy(b, par, 1, 1)
                if new and not keys_ahead(ly, s):
                    keys_on_scalar(act, ly, b, nxt)
                exp(3)
                if cur:
                    if older:
                        act.wait_ge(ly["ot_done"], 2 * b - 2)
                    o_copy(b, par, 0)
                exp(4)
                if ffn and s == B - 1:
                    ffn_start(ffn, -3)
                if nxt:
                    m_copy(b + 1, 1 - par, 0, 0)
                    if ly["bias"]:
                        act.wait_ge(moe[f"wraw{1 - par}"], 8 * (b + par) + 16)
                        raw = wraw[1 - par][:, :, :].rearrange("p k n -> p (k n)")
                        act.activation(raw, raw, ACT.Copy, scale=WS).then_inc(moe["scaled"], 1)
                exp(5)
                if nxt and ly["bias"]:
                    act.wait_ge(moe["scaled"], b + 2)
                    act.activation(w_hl[:, bass.ds(W_CHUNK * (b + 1), W_CHUNK), 0, :], wraw[1 - par][:, :, :], ACT.Copy) \
                       .then_inc(moe["w_hi"], 1)
                if cur:
                    o_copy(b, par, 1)
                exp(6)
                gating = s == B and ly["bias"]
                if gating:
                    gate_copies(act, 0, 4)
                if old:
                    act.wait_ge(ly["aT_done"], b)
                    if older:
                        act.wait_ge(ly["op_done"], b - 1)
                    act.activation(aT[:, :], M[1][:, 0:S], ACT.Copy).then_inc(ly["aT_copied"], 1)
                if gating:
                    gate_copies(act, 4, GATE_AHEAD)
                exp(7)
                if cur:
                    o_copy(b, par, 2)

            slots_loop(act, slot_fn)

        def carrier_on_vector(v):
            v.tensor_copy(carried_v[:, :], mhalf[:, 0:QT])

        def norm_stats(v, b, own, var):
            for q in range(QT):
                i = v.bn_stats(st6[:, q, :], X[:, b * QT + q, :])
            i.then_inc(own, 1)
            v.wait_ge(own, 2 * b + 1)
            carrier_on_vector(v)
            for q in range(QT):
                i = v.bn_aggr(mv[:, q, :], st6[:, q, :])
            i.then_inc(own, 1)
            v.wait_ge(own, 2 * b + 2)
            v.tensor_scalar(ve[:, :], mv[:, :, 1], EPS, None, ALU.add).then_inc(var, 1)

        def norm_apply(v, b, dst, rst, done):
            v.wait_ge(rst, b + 1)
            for q in range(QT):
                i = v.tensor_scalar(dst[:, q, :], X[:, b * QT + q, :], mv[:, q, 0:1], rstd[:, q:q + 1],
                                    ALU.subtract, ALU.mult)
            i.then_inc(done, 1)

        def norm_root(pool, b, var, rst):
            pool.wait_ge(var, b + 1)
            pool.tensor_tensor(rstd[:, :], ve[:, :], mhalf[:, 0:QT], ALU.pow).then_inc(rst, 1)

        def attention_on_vector(v, ly, ffn=None):
            def reduce(b, par, h):
                v.wait_ge(ly["p1_done"], 16 * b + h + 1)
                v.tensor_reduce(nm[par][:, :, h], S1[h % 2][:, :, :], AX.X, ALU.max, negate=True)\
                 .then_inc(ly["max_done"], 1)

            def parts(b, par, half):
                hs = slice(8 * half, 8 * half + 8)
                base = 6 * b + 3 * half
                v.wait_ge(ly["max_done"], 16 * b + 8 * half + 8)
                if not (isinstance(b, int) and b < 2):
                    v.wait_ge(ly["mT_done"], 2 * b - 3 + half)
                v.tensor_scalar(mparts[par][:, :, hs, 0], nm[par][:, :, hs], 1.0 / MROW, None, ALU.mult)\
                 .then_inc(ly["own"], 1)
                v.wait_ge(ly["own"], base + 1)
                v.scalar_tensor_tensor(mr[:, :, :], nm[par][:, :, hs], 1.0 / MROW, mparts[par][:, :, hs, 0],
                                       ALU.mult, ALU.subtract).then_inc(ly["own"], 1)
                v.wait_ge(ly["own"], base + 2)
                v.tensor_copy(mparts[par][:, :, hs, 1], mr[:, :, :]).then_inc(ly["own"], 1)
                v.wait_ge(ly["own"], base + 3)
                v.tensor_tensor(mparts[par][:, :, hs, 2], mr[:, :, :], mparts[par][:, :, hs, 1],
                                ALU.subtract).then_inc(ly["m_parts"], 1)

            def zero_m(b, par, half):
                if not (isinstance(b, int) and b < 2):
                    v.wait_ge(ly["p2_done"], 8 * (b - 2) + 4 * half + 4)
                v.memset(Qt[par][M0:M0 + MROWS, 2 * half:2 * half + 2, :], 0.0).then_inc(ly["m_zeroed"], 1)

            def o_norm(b, q):
                ot = M[1][:, :].rearrange("p (h r) -> p h r", r=32)
                v.wait_ge(ly["ot_done"], 2 * b + q + 1)
                if ly["position"]:
                    v.tensor_scalar(rsum[:, q, :], ot[:, :, DH], 1.0, None, ALU.add).then_inc(ly["ot_sum"], 1)
                    v.wait_ge(ly["ot_sum"], 2 * b + q + 1)
                    v.reciprocal(rc[:, q, :], rsum[:, q, :]).then_inc(ly["o_rc"], 1)
                else:
                    v.reciprocal(rc[:, q, :], ot[:, :, DH]).then_inc(ly["o_rc"], 1)
                v.wait_ge(ly["o_rc"], 2 * b + q + 1)
                if q == 0 and not (isinstance(b, int) and b == 0):
                    v.wait_ge(ly["aT_done"], b)
                v.tensor_tensor(attn[:, q, :].rearrange("p (h d) -> p h d", d=DH), ot[:, :, 0:DH],
                                rc[:, q, :].unsqueeze(2).to_broadcast([P, H, DH]), ALU.mult).then_inc(ly["ot_norm"], 1)

            def slot_fn(b, par, s):
                nxt, cur, old = (exists(s, d) for d in (1, 0, -1))
                ahead = s is None or s <= 5

                def r(i):
                    if nxt:
                        reduce(b + 1, 1 - par, 2 * i)
                        reduce(b + 1, 1 - par, 2 * i + 1)

                r(0)
                if nxt:
                    zero_m(b + 1, 1 - par, 1)
                if s == -1 and ly["bias"]:
                    v.wait_ge(loaded_x, 16 * N_LOADS_X)
                gathering = ly["position"] and s == -1
                if s == -2 and ly["position"]:
                    v.wait_ge(moe["gathered1"], 16 * QT)
                    add_experts(v, QT, 2 * QT)
                if ahead and not gathering:
                    norm_stats(v, b + 3, ly["norm_own"], ly["xvar"])
                r(1)
                if cur:
                    parts(b, par, 1)
                r(2)
                if ahead and not gathering:
                    if nxt:
                        v.wait_ge(ly["xnT_done"], b + 2)
                    norm_apply(v, b + 3, xn[1 - par], ly["xrstd"], ly["xn_ready"])
                if s == -2 and ly["bias"]:
                    for i in range(2):
                        for g in range(NG):
                            rows_of_maximum(Kt[i], g, v.tensor_copy)
                r(3)
                if nxt:
                    parts(b + 1, 1 - par, 0)
                    v.wait_ge(ly["v_done"], b + 2)
                    if old:
                        v.wait_ge(ly["pv_done"], 4 * b)
                    src = M[0][:, 0:S].rearrange("p (k h d) -> p k h d", k=QT, h=H)
                    dst = Vt[1 - par]
                    if ly["bias"]:
                        for k in range(QT):
                            i = v.tensor_tensor(dst[:, k, :, 0:DH], src[:, k], vb[:, :].rearrange("p (h d) -> p h d", d=DH),
                                                ALU.add)
                    else:
                        i = v.tensor_copy(dst[:, :, :, 0:DH], src)
                    i.then_inc(ly["v_copied"], 1)
                r(4)
                if exists(s, 2):
                    zero_m(b + 2, par, 0)
                if gathering:
                    v.wait_ge(moe["gathered"], 16 * (NT - 2 * QT))
                    add_experts(v, 2 * QT, NT)
                    norm_stats(v, b + 3, ly["norm_own"], ly["xvar"])
                if ffn and s == B - 1:
                    ffn_start(ffn, -3)
                if s == B - 1 and ly["bias"]:
                    gate_stats(v, 0, GATE_AHEAD * QT)
                    gate_variances(v, 0, GATE_AHEAD * QT)
                if s == B and ly["bias"]:
                    v.wait_ge(ly["pv_done"], NG * B - 1)
                    gate_norms(v, 0, GATE_AHEAD)
                if old:
                    o_norm(b - 1, 0)
                r(5)
                if old:
                    o_norm(b - 1, 1)
                if ffn and s == B - 1:
                    ffn_start(ffn, -2)
                r(6)
                if old and ly["bias"]:
                    for q in range(QT):
                        i = v.tensor_tensor(X[:, (b - 1) * QT + q, :], X[:, (b - 1) * QT + q, :], ob[:, :], ALU.add)
                    i.then_inc(ly["x_biased"], 1)
                r(7)
                if gathering:
                    v.wait_ge(ly["xnT_done"], b + 2)
                    norm_apply(v, b + 3, xn[1 - par], ly["xrstd"], ly["xn_ready"])
                if old:
                    v.wait_ge(ly["op_done"], b)
                    if ly["bias"]:
                        v.wait_ge(ly["x_biased"], b)
                    for q in range(QT):
                        x = X[:, (b - 1) * QT + q, :]
                        i = v.tensor_tensor(x, M[0][:, q * D:(q + 1) * D], x, ALU.add)
                    i.then_inc(ly["x_added"], 1)

            slots_loop(v, slot_fn)

        def key_rests_on_gpsimd(pool, ly, b, nxt):
            if nxt:
                pool.wait_ge(ly["k_rep"], 48 * (b + 2))
            pool.wait_ge(ly["k_hi"], b + 3)
            pool.tensor_tensor(k_lo[:, :], kf[:, :], k_hi[:, :], ALU.subtract).then_inc(ly["k_lo"], 1)

        def key_tiles_on_gpsimd(pool, ly, b, par, cur):
            for half in range(2):
                if cur:
                    pool.wait_ge(ly["p2_done"], 8 * b + 4 * half + 4)
                if half == 0:
                    pool.wait_ge(ly["k_rep"], 48 * (b + 3))
                gs = slice(2 * half, 2 * half + 2)
                for i in range(HG):
                    dst = Kt[par][0:M0, :, :].rearrange("p (g i) n -> p g i n", i=HG)[:, gs, i, :]
                    if i == 0:
                        pool.tensor_tensor(dst, k_rep[0:M0, gs, :], head_mask[0:M0, 0:1].unsqueeze(2)
                                           .to_broadcast([M0, 2, S]), ALU.mult)
                        continue
                    kk = pool.tensor_scalar(dst, k_rep[0:M0, gs, :], head_mask[0:M0, i:i + 1], 1.0,
                                            ALU.mult, ALU.mult)
                kk.then_inc(ly["k_tile"], 1)

        def attention_on_gpsimd(pool, ly):
            def slot_fn(b, par, s):
                new, nxt, cur = (exists(s, d) for d in (2, 1, 0))
                gathering = ly["position"] and s == -1
                if (s is None or s <= 5) and not gathering:
                    norm_root(pool, b + 3, ly["xvar"], ly["xrstd"])
                if s == -3 and ly["position"]:
                    gather(pool, 2 * QT, 2 * QT + 3)
                elif s == -3:
                    key_rests_on_gpsimd(pool, ly, -2, False)
                if cur and ly["bias"]:
                    pool.wait_ge(moe["w_hi"], b + 1)
                    w = bass.ds(W_CHUNK * b, W_CHUNK)
                    pool.tensor_tensor(w_hl[:, w, 1, :], wraw[par][:, :, :], w_hl[:, w, 0, :], ALU.subtract) \
                        .then_inc(moe["split"], 1)
                if not new:
                    return
                if cur:
                    pool.wait_ge(ly["q_tile"][1], 48 * b + 48)
                pool.wait_ge(ly["q_hi"], b + 3)
                pool.tensor_tensor(q_lo[par][:, :], qf[:, :], q_hi[par][:, :], ALU.subtract).then_inc(ly["q_lo"], 1)
                if keys_ahead(ly, s) and ly["position"]:
                    gather(pool, 2 * QT + 3, NT)
                    return
                if not keys_ahead(ly, s):
                    key_rests_on_gpsimd(pool, ly, b, nxt)
                key_tiles_on_gpsimd(pool, ly, b, par, cur)
                if gathering:
                    norm_root(pool, b + 3, ly["xvar"], ly["xrstd"])

            slots_loop(pool, slot_fn)

        def load_weights(sp, n, par):
            sp.dma_start(wraw[par][:, :, :], t["w"][:, bass.ds(W_CHUNK * n, W_CHUNK), :]).then_inc(moe[f"wraw{par}"], 16)

        def context_on_sync(sp, ly, b, par):
            sp.dma_start(ctxT[par][:, :], t["ctxT"][:, b + 2, :]).then_inc(ly["ctx_loaded"], 16)

        def keys_on_sync(sp, ly, b, nxt):
            sp.wait_ge(ly["k_lo"], b + 3)
            if nxt:
                sp.wait_ge(ly["k_tile"], 2 * b + 4)
            for block, src in enumerate((k_hi, k_lo, k_hi)):
                sp.dma_start(k_rep[32 * block:32 * block + 32, :, :], src[:, :]).then_inc(ly["k_rep"], 16)

        def attention_on_sync(sp, ly, late):
            def slot_fn(b, par, s):
                new, nxt, cur = (exists(s, d) for d in (2, 1, 0))
                if not new:
                    return
                if cur:
                    sp.wait_ge(ly["v_done"], b + 1)
                    sp.wait_ge(ly["k_done"], b + 1)
                if not keys_ahead(ly, s):
                    context_on_sync(sp, ly, b, par)
                    keys_on_sync(sp, ly, b, nxt)
                for half in range(2):
                    if cur:
                        sp.wait_ge(ly["p2_done"], 8 * b + 4 * half + 4)
                    if half == 0:
                        sp.wait_ge(ly["q_lo"], b + 3)
                    for block, src in enumerate((q_hi, q_hi, q_lo)):
                        sp.dma_start(Qt[par][32 * block:32 * block + 32, 2 * half:2 * half + 2, :],
                                     src[par][64 * half:64 * half + 64, :]).then_inc(ly["q_tile"][half], 16)
                    if ly["position"]:
                        sp.dma_start(Kt[par][PB0:PB0 + PARTS, 8 * half:8 * half + 8, :],
                                     pos_dram[b + 2, 8 * half:8 * half + 8, :, :].rearrange("h c n -> c h n")) \
                          .then_inc(ly["k_pos"][half][par], 16)
                if s in (-1, 0, 1):
                    for dst, src in late[s + 1::3]:
                        sp.dma_start(dst, src).then_inc(loaded_late, 16)
                if ly["bias"] and s == -2:
                    load_weights(sp, 0, 0)
                    load_weights(sp, 1, 1)
                if ly["bias"] and cur:
                    sp.wait_ge(moe["split"], b + 1)
                    load_weights(sp, b + 2, par)

            slots_loop(sp, slot_fn)


        GATE_AHEAD = B - 2

        def gate_stats(v, start, end):
            v.wait_ge(ly[0]["x_added"], end // QT)
            for i in range(start, end):
                ii = v.bn_stats(st_all[:, i, :], X[:, i, :])
            ii.then_inc(moe["norm_own"], 1)

        def gate_variances(v, start, end):
            n = 2 if start else 0
            v.wait_ge(moe["norm_own"], n + 1)
            for i in range(start, end):
                ii = v.bn_aggr(mv_all[:, i, :], st_all[:, i, :])
            ii.then_inc(moe["norm_own"], 1)
            v.wait_ge(moe["norm_own"], n + 2)
            v.tensor_scalar(ve_all[:, start:end], mv_all[:, start:end, 1], EPS, None, ALU.add).then_inc(moe["var"], 1)

        def gate_norms(v, start, end):
            v.wait_ge(moe["rstd"], 2 if start else 1)
            for b in range(start, end):
                for i in range(b * QT, b * QT + QT):
                    ii = v.tensor_scalar(xn2[:, i, :], X[:, i, :], mv_all[:, i, 0:1], rstd_all[:, i:i + 1],
                                         ALU.subtract, ALU.mult)
                ii.then_inc(moe["xn"], 1)

        def gate_on_vector(v):
            gate_stats(v, GATE_AHEAD * QT, NT)
            gate_variances(v, GATE_AHEAD * QT, NT)
            gate_norms(v, GATE_AHEAD, B)
            v.wait_ge(loaded_late, 16 * N_LATE)
            v.wait_ge(moe["gm"], B)
            v.tensor_tensor(logit[:, :, :], S1[0][:, 0, 0:NT * NE].rearrange("p (t e) -> p t e", e=NE),
                            bg[:, :].unsqueeze(1).to_broadcast([P, NT, NE]), ALU.add).then_inc(moe["logit"], 1)

        def gate_on_gpsimd(pool):
            for n, ts in enumerate((slice(0, GATE_AHEAD * QT), slice(GATE_AHEAD * QT, NT))):
                pool.wait_ge(moe["var"], n + 1)
                pool.tensor_tensor(rstd_all[:, ts], ve_all[:, ts], mhalf[:, ts], ALU.pow).then_inc(moe["rstd"], 1)

        def gate_bank(b):
            return S2[b % 2][:, 0, :, 0:P]

        def gate_products(pe, start, end):
            if start == 0:
                pe.wait_ge(loaded_late, 16 * N_LATE)
                pe.wait_ge(ly[0]["max_done"], H * B)
            for b in range(start, end):
                if b < B:
                    pe.wait_ge(moe["xn"], b + 1)
                    if b >= 2:
                        pe.wait_ge(moe["xTc"], b - 1)
                    for q in range(QT):
                        mm = pe.transpose(gate_bank(b)[:, q, :], xn2[:, b * QT + q, :], eye[:, :])
                    mm.then_inc(moe["xT"], 1)
                if b >= 1:
                    c = b - 1
                    pe.wait_ge(moe["xTc"], b)
                    for q in range(QT):
                        i = c * QT + q
                        mm = pe.matmul(S1[0][:, 0, i * NE:(i + 1) * NE], gT[c % 2][:, q * P:(q + 1) * P], wg[:, :],
                                       start=True, stop=True)
                    mm.then_inc(moe["gm"], 1)

        def gate_on_tensor(pe):
            gate_products(pe, GATE_AHEAD, B + 1)
            pe.wait_ge(moe["onehot"], 1)
            oh = onehot[:, :, :].rearrange("p t e -> p (t e)")
            pe.matmul(M[0][:, 0:P], before[:, :], oh, start=True, stop=True).then_inc(moe["ranks"], 1)
            pe.matmul(M[1][:, 0:P], ones32[:, :], oh, start=True, stop=True).then_inc(moe["ranks"], 1)

        def gate_copies(act, start, end):
            for b in range(start, end):
                act.wait_ge(moe["xT"], b + 1)
                if b >= 2:
                    act.wait_ge(moe["gm"], b - 1)
                act.activation(gT[b % 2][:, :].rearrange("p (q n) -> p q n", q=QT), gate_bank(b), ACT.Copy) \
                   .then_inc(moe["xTc"], 1)

        def gate_on_scalar(act):
            gate_copies(act, GATE_AHEAD, B)
            act.wait_ge(moe["r"], 5)
            act.activation(t2[:, :, :].rearrange("p t e -> p (t e)"), t1[:, :, :].rearrange("p t e -> p (t e)"),
                           ACT.Exp).then_inc(moe["exp"], 1)

        def route_on_vector(v):
            count = [0]

            def step(ins):
                ins.then_inc(moe["r"], 1)
                count[0] += 1
                v.wait_ge(moe["r"], count[0])

            v.wait_ge(moe["logit"], 1)
            te = [P, NT, NE]
            num = route_c[:, 0, :].rearrange("p (t e) -> p t e", e=NE)
            step(v.tensor_reduce(top[:, :], logit[:, :, :], AX.X, ALU.max))
            step(v.tensor_tensor(t1[:, :, :], logit[:, :, :], top[:, :].unsqueeze(2).to_broadcast(te), ALU.is_equal))
            step(v.tensor_tensor(t2[:, :, :], t1[:, :, :], num, ALU.mult))
            step(v.tensor_reduce(first[:, :], t2[:, :, :], AX.X, ALU.min))
            v.tensor_tensor(onehot[:, :, :], num, first[:, :].unsqueeze(2).to_broadcast(te), ALU.is_equal) \
             .then_inc(moe["onehot"], 1)
            step(v.tensor_tensor(t1[:, :, :], logit[:, :, :], top[:, :].unsqueeze(2).to_broadcast(te), ALU.subtract))
            v.wait_ge(moe["ranks"], 2)
            step(v.tensor_copy(tot[:, :, :], M[1][:, 0:P].rearrange("p (t e) -> p e t", e=NE)))
            step(v.tensor_tensor_scan(cum[:, :, :].rearrange("p e t -> p (e t)"), route_c[:, 1, :],
                                      tot[:, :, :].rearrange("p e t -> p (e t)"), 0.0, ALU.mult, ALU.add))
            step(v.tensor_scalar(cnt_i[:, :], cum[:, :, NT - 1], float(P - 1), None, ALU.add))
            step(v.tensor_scalar(cnt_s[:, :], cnt_i[:, :], 7, None, ALU.arith_shift_right))
            step(v.tensor_copy(ntile[:, :], cnt_s[:, :]))
            step(v.tensor_tensor_scan(tend[:, :], ones32[:, 0:NE], ntile[:, :], 0.0, ALU.mult, ALU.add))
            step(v.tensor_tensor(tstart[:, :], tend[:, :], ntile[:, :], ALU.subtract))
            step(v.tensor_tensor(rbase[:, :, :], cum[:, :, :], tot[:, :, :], ALU.subtract))
            step(v.scalar_tensor_tensor(rbase[:, :, :], tstart[:, :].unsqueeze(2).to_broadcast([P, NE, NT]), float(P),
                                        rbase[:, :, :], ALU.mult, ALU.add))
            step(v.tensor_tensor(cum[:, :, :], M[0][:, 0:P].rearrange("p (t e) -> p e t", e=NE), rbase[:, :, :], ALU.add))
            step(v.tensor_tensor(cum[:, :, :], cum[:, :, :], onehot[:, :, :].rearrange("p t e -> p e t"), ALU.mult))
            step(v.tensor_reduce(slotf[:, :], cum[:, :, :].rearrange("p e t -> p t e"), AX.X, ALU.add))
            v.tensor_copy(slot[:, :], slotf[:, :]).then_inc(moe["slots"], 1)
            je = [P, SLOT_TILES, NE]
            step(v.tensor_tensor(cmp[:, :, :], tend[:, :].unsqueeze(1).to_broadcast(je),
                                 route_c[:, 2, 0:SLOT_TILES].unsqueeze(2).to_broadcast(je), ALU.is_le))
            step(v.tensor_reduce(expf[:, :], cmp[:, :, :], AX.X, ALU.add))
            v.tensor_scalar(expert[:, :], expf[:, :], float(NE - 1), None, ALU.min).then_inc(moe["slots"], 1)
            v.wait_ge(moe["exp"], 1)
            step(v.tensor_reduce(gsum[:, :], t2[:, :, :], AX.X, ALU.add))
            v.reciprocal(gate[:, :], gsum[:, :]).then_inc(moe["gate"], 1)

        def biases_on_vector(v):
            v.tensor_scalar(b1s[:, :, :], b1c[:, :, :], WS, None, ALU.mult).then_inc(moe["bsplit"], 1)
            v.memset(b2rows[:, :], 0.0).then_inc(moe["bsplit"], 1)
            v.tensor_scalar(brest[:, :], braw[:, :], WS, None, ALU.mult).then_inc(moe["bsplit"], 1)
            v.wait_ge(moe["bsplit"], 3)
            v.tensor_copy(bparts[:, 0, :], brest[:, :]).then_inc(parts_made, 1)
            v.wait_ge(parts_made, 1)
            v.tensor_tensor(brest[:, :], brest[:, :], bparts[:, 0, :], ALU.subtract).then_inc(parts_made, 1)
            v.wait_ge(parts_made, 2)
            v.tensor_copy(bparts[:, 1, :], brest[:, :]).then_inc(moe["bsplit"], 1)
            v.wait_ge(moe["bsplit"], 4)
            v.tensor_tensor(bparts[:, 2, :], brest[:, :], bparts[:, 1, :], ALU.subtract).then_inc(moe["bsplit"], 1)
            v.tensor_copy(pos_f[:, :], pos_i[:, :]).then_inc(parts_made, 1)
            v.wait_ge(parts_made, 3)
            v.tensor_scalar(pos_r[:, :], pos_f[:, :], slope[:, 0:1], SC / MROW, ALU.mult, ALU.mult).then_inc(parts_made, 1)
            v.wait_ge(parts_made, 4)
            v.tensor_copy(pos_parts[:, 0, :], pos_r[:, :]).then_inc(parts_made, 1)
            v.wait_ge(parts_made, 5)
            v.tensor_tensor(pos_r[:, :], pos_r[:, :], pos_parts[:, 0, :], ALU.subtract).then_inc(parts_made, 1)
            v.wait_ge(parts_made, 6)
            v.tensor_copy(pos_parts[:, 1, :], pos_r[:, :]).then_inc(parts_made, 1)
            v.wait_ge(parts_made, 7)
            v.tensor_tensor(pos_parts[:, 2, :], pos_r[:, :], pos_parts[:, 1, :], ALU.subtract).then_inc(parts_made, 1)

        def mask_raw(n):
            return Pt[n][:, :, :].rearrange("p i n -> p (i n)").bitcast(I32)

        def mask_on_sync(sp):
            sp.wait_ge(ly[0]["pv_done"], NG * B)
            for n in range(2):
                sp.dma_start(mask_raw(n), t["mask"][:, n * 2048:(n + 1) * 2048]).then_inc(mk["raw"], 16)

        def mask_on_vector(v):
            v.wait_ge(mk["raw"], 32)
            for n in range(2):
                v.tensor_scalar(mask_bias[:, n * NT // 2:(n + 1) * NT // 2, :].rearrange("p t n -> p (t n)"),
                                mask_raw(n), 0.0, MASKED, ALU.is_equal, ALU.mult).then_inc(mk["own"], 1)
            v.wait_ge(mk["own"], 2)
            v.tensor_reduce(mask_min[:, :], mask_bias[:, :, :].rearrange("p t n -> p (t n)"), AX.X, ALU.min) \
             .then_inc(mk["own"], 1)
            v.wait_ge(mk["own"], 3)
            v.tensor_scalar(mask_hit[:, :], mask_min[:, :], 0.0, None, ALU.is_lt).then_inc(mk["own"], 1)
            v.wait_ge(mk["count"], 1)
            v.tensor_scalar(mask_any[:, :], S2[0][:, 0, 0, 0:1], 1.0, None, ALU.min).then_inc(mk["any"], 1)

        def mask_on_tensor(pe):
            pe.wait_ge(mk["own"], 4)
            pe.matmul(S2[0][:, 0, 0, 0:1], ones32[:, :], mask_hit[:, :], start=True, stop=True).then_inc(mk["count"], 1)

        def scatter_on_gpsimd(pool):
            pool.wait_ge(moe["slots"], 1)
            pool.wait_ge(moe["xn"], B)
            pool.wait_ge(moe["zfill"], 16)
            for i in range(NT):
                pool.indirect_dma_start(xs_dram, bass.IndirectOffsetOnAxis(ap=slot[:, i:i + 1].bitcast(U32), axis=0),
                                        xn2[:, i, :], None).then_inc(moe["scattered"], 16)

        def gather(pool, start, end):
            for i in range(start, end):
                pool.indirect_dma_start(yg[:, i, :], None, ys_dram,
                                        bass.IndirectOffsetOnAxis(ap=slot[:, i:i + 1].bitcast(U32), axis=0)) \
                    .then_inc(moe[f"gathered{i // QT}" if i < 2 * QT else "gathered"], 16)

        def gather_on_gpsimd(pool):
            key_rests_on_gpsimd(pool, ly[1], -2, False)
            key_tiles_on_gpsimd(pool, ly[1], -2, 0, False)
            pool.wait_ge(moe["stored0"], 16 * ((SLOT_TILES + 1) // 2))
            pool.wait_ge(moe["stored1"], 16 * (SLOT_TILES // 2))
            gather(pool, 0, 2 * QT)

        def tile_exists(s, d):
            return s is None or 0 <= s + d < SLOT_TILES

        def tiles_loop(eng, slot_fn):
            for s in range(-3, 4):
                slot_fn(s, s % 2, s)
            with eng.Fori(2, SLOT_TILES // 2 - 2) as i:
                for par in range(2):
                    slot_fn(2 * i + par, par, None)
            for s in range(SLOT_TILES - 5, SLOT_TILES + 2):
                slot_fn(s, s % 2, s)

        def reused(b):
            return not isinstance(b, int) or b >= 2

        def experts_on_sync(sp):
            context_on_sync(sp, ly[1], -2, 0)
            sp.wait_ge(moe["scattered"], 16 * NT)
            sp.wait_ge(moe["slots"], 2)

            def load(j, par):
                if reused(j):
                    sp.wait_ge(moe["tT"], j - 1)
                sp.dma_start(xt[par][:, :], xs_dram.rearrange("(j p) d -> j p d", p=P)[j, :, :]).then_inc(moe[f"xt{par}"], 16)

            def store(j, par):
                sp.wait_ge(moe["ysb"], j + 1)
                sp.dma_start(ys_dram.rearrange("(j p) d -> j p d", p=P)[j, :, :], ysb[par][:, :]) \
                  .then_inc(moe[f"stored{par}"], 16)

            def slot_fn(j, par, s):
                if tile_exists(s, 5):
                    load(j + 5, 1 - par)
                if tile_exists(s, -2):
                    store(j - 2, par)
            load(0, 0)
            load(1, 1)
            keys_on_sync(sp, ly[1], -2, False)
            tiles_loop(sp, slot_fn)

        def experts_on_tensor(pe):
            pe.wait_ge(moe["slots"], 2)
            pe.wait_ge(moe["split"], B)
            pe.wait_ge(moe["brows"], 16 * PARTS)

            first_keys_on_tensor(pe, ly[1])

            def expert_of(j):
                return pe.value_load(expert[0:1, bass.ds(j, 1)], min_val=0, max_val=NE - 1)

            def weights(layer_of, e, c, a=0, both=False):
                w = w_hl[:, :, :, :].rearrange("p (l e c) a n -> p l e (c a n)", l=2, e=NE)
                n = (2 * c + a) * P
                return w[:, layer_of, bass.ds(e, 1), n:n + (2 * P if both else P)].rearrange("p e n -> p (e n)")

            def experts_of(j):
                _, values = nc.values_load_multi_w_load_instructions(
                    expert[0:1, bass.ds(j - 1, 4)], engines=[mybir.EngineType.PE], min_val=0, max_val=NE - 1,
                    skip_runtime_bounds_check_because="a tile's expert is a count of experts, clamped to the last")
                return values

            def first(j, par, e):
                pe.wait_ge(moe["x_lo"], j + 1)
                if reused(j):
                    pe.wait_ge(moe["hs"], j - 1)
                hb = S2[par][:, :, :, :].rearrange("p a k n -> p (a k) n")
                for c in range(HC):
                    pe.matmul(hb[:, c, :], weights(0, e, c), x_hl[par][:, :, :].rearrange("p a n -> p (a n)"),
                              start=True, stop=False)
                    mm = pe.matmul(hb[:, c, 0:P], weights(0, e, c, 1), x_hl[par][:, 0, :], start=False, stop=True)
                mm.then_inc(moe["h"], 1)

            def turn(j, par):
                pe.wait_ge(moe[f"xt{par}"], 8 * (j - par) + 16)
                if isinstance(j, int) and j == 0:
                    pe.wait_ge(ly[1]["k_copied"], 1)
                if reused(j):
                    pe.wait_ge(moe["x_lo"], j - 1)
                pe.transpose(M[par][:, 0:P], xt[par][:, :], eye[:, :]).then_inc(moe["tT"], 1)

            def second(j, par, e):
                pe.wait_ge(moe["h_lo"], j + 1)
                if reused(j):
                    pe.wait_ge(moe["ysb"], j - 1)
                o = S1[par][:, :, :].rearrange("p q n -> p (q n)")
                for c in range(HC):
                    hs = slice(c * P, (c + 1) * P)
                    pe.matmul(o[:, 0:2 * D], h_hi[par][:, hs], weights(1, e, c, both=True), start=(c == 0), stop=False)
                    pe.matmul(o[:, 0:D], h_lo[par][:, hs], weights(1, e, c), start=False, stop=False)
                pe.matmul(o[:, 0:D], ones16[:, :], b2rows[:, bass.ds(e * D, D)], start=False, stop=True).then_inc(moe["y"], 1)

            near = []

            def slot_fn(j, par, s):
                if s is None and par == 0:
                    near[:] = experts_of(j)
                if tile_exists(s, 1):
                    first(j + 1, 1 - par, near[2 + par] if s is None else expert_of(j + 1))
                if tile_exists(s, 3):
                    turn(j + 3, 1 - par)
                if tile_exists(s, -1):
                    second(j - 1, 1 - par, near[par] if s is None else expert_of(j - 1))
            tiles_loop(pe, slot_fn)

        def experts_on_scalar(act):
            keys_on_scalar(act, ly[1], -2, False)
            act.wait_ge(moe["slots"], 2)
            act.wait_ge(moe["bsplit"], 4)

            def slot_fn(j, par, s):
                if tile_exists(s, 0):
                    act.wait_ge(moe["hs"], j + 1)
                    if reused(j):
                        act.wait_ge(moe["h_lo"], j - 1)
                    act.activation(hf[par][:, :], hs[par][:, :], ACT.Silu, scale=1.0 / WS).then_inc(moe["hf"], 1)
                if tile_exists(s, 1):
                    e = act.value_load(expert[0:1, bass.ds(j + 1, 1)], min_val=0, max_val=NE - 1)
                    act.wait_ge(moe["h"], j + 2)
                    hb = S2[1 - par][:, :, :, :].rearrange("p a k n -> p (a k) n")
                    for c in range(HC):
                        i = act.activation(hs[1 - par][:, c * P:(c + 1) * P], hb[:, c, P:2 * P], ACT.Identity,
                                           bias=b1s[:, c, bass.ds(e, 1)])
                    i.then_inc(moe["hr"], 1)
                if tile_exists(s, 3):
                    act.wait_ge(moe["tT"], j + 4)
                    if reused(j + 3):
                        act.wait_ge(moe["h"], j + 2)
                    act.activation(x_hl[1 - par][:, 0, :], M[1 - par][:, 0:P], ACT.Copy).then_inc(moe["x_hi"], 1)
                if tile_exists(s, -2):
                    act.wait_ge(moe["y"], j - 1)
                    if reused(j - 2):
                        act.wait_ge(moe[f"stored{par}"], 8 * (j - 2 - par))
                    act.activation(ysb[par][:, :], S1[par][:, 0, 0:D], ACT.Copy, scale=1.0 / WS).then_inc(moe["yh"], 1)
            tiles_loop(act, slot_fn)

        def experts_on_vector(v):
            def slot_fn(j, par, s):
                if tile_exists(s, 0):
                    if reused(j):
                        v.wait_ge(moe["y"], j - 1)
                    v.wait_ge(moe["hf"], j + 1)
                    v.tensor_copy(h_hi[par][:, :], hf[par][:, :]).then_inc(moe["h_hi"], 1)
                    v.wait_ge(moe["h_hi"], j + 1)
                    v.tensor_tensor(h_lo[par][:, :], hf[par][:, :], h_hi[par][:, :], ALU.subtract).then_inc(moe["h_lo"], 1)
                if tile_exists(s, 1):
                    v.wait_ge(moe["hr"], j + 2)
                    hb = S2[1 - par][:, :, :, :].rearrange("p a k n -> p (a k) n")
                    v.tensor_tensor(hs[1 - par][:, :].rearrange("p (c n) -> p c n", n=P), hb[:, :, 0:P],
                                    hs[1 - par][:, :].rearrange("p (c n) -> p c n", n=P), ALU.add).then_inc(moe["hs"], 1)
                if tile_exists(s, 3):
                    v.wait_ge(moe["x_hi"], j + 4)
                    v.tensor_tensor(x_hl[1 - par][:, 1, :], M[1 - par][:, 0:P], x_hl[1 - par][:, 0, :], ALU.subtract) \
                     .then_inc(moe["x_lo"], 1)
                if tile_exists(s, -2):
                    v.wait_ge(moe["yh"], j - 1)
                    v.scalar_tensor_tensor(ysb[par][:, :], S1[par][:, 0, D:2 * D], 1.0 / WS, ysb[par][:, :],
                                           ALU.mult, ALU.add).then_inc(moe["ysb"], 1)
            tiles_loop(v, slot_fn)
            v.wait_ge(moe["gate"], 1)
            v.wait_ge(moe["gathered0"], 16 * QT)
            add_experts(v, 0, QT)

        def add_experts(v, start, end):
            for i in range(start, end):
                ii = v.scalar_tensor_tensor(X[:, i, :], yg[:, i, :], gate[:, i:i + 1], X[:, i, :], ALU.mult, ALU.add)
            ii.then_inc(moe["x"], 1)
            v.wait_ge(moe["x"], 1 if start == 0 else 2 if start == QT else 3)

        def ffn_start(slot_fn, s):
            slot_fn(s, s % 2, s)

        def ffn_loop(eng, slot_fn):
            for s in range(-1, 2):
                slot_fn(s, s % 2, s)
            with eng.Fori(1, 2) as i:
                for par in range(2):
                    slot_fn(2 * i + par, par, None)
            for s in range(4, 10):
                slot_fn(s, s % 2, s)

        def ffn_on_vector(v):
            def apply(b, par):
                if reused(b):
                    v.wait_ge(ff["xT"], b - 1)
                norm_apply(v, b, xn[par], ff["rstd"], ff["xn"])

            def membrane(b, par, new):
                base = 2 * (STEPS - 1) * b
                v.wait_ge(ff["yc"], b + 1)
                if reused(b):
                    v.wait_ge(ff["above"], b - 1)
                for k in range(1, STEPS):
                    if k > 1:
                        v.wait_ge(ff["mem"], base + 2 * k - 2)
                    elif not isinstance(b, int) or b >= 1:
                        v.wait_ge(ff["mem"], base)
                    v.scalar_tensor_tensor(tmp[:, :], mem[par][:, k - 1, :], BETA, mem[par][:, 0, :], ALU.mult, ALU.add) \
                        .then_inc(ff["mem"], 1)
                    v.wait_ge(ff["mem"], base + 2 * k - 1)
                    v.scalar_tensor_tensor(mem[par][:, k, :], mem[par][:, k - 1, :], 1.0, tmp[:, :], ALU.is_gt, ALU.subtract,
                                           reverse1=True).then_inc(ff["mem"], 1)
                    if k == 2 and new:
                        apply(b + 3, 1 - par)

            def result(b, par):
                v.wait_ge(ff["count"], b + 1)
                if reused(b):
                    v.wait_ge(ff[f"stored{par}"], 8 * (b - par))
                v.scalar_tensor_tensor(fin[par][:, :, :].rearrange("p q d -> p (q d)"), S1[1][:, 0, :], 1.0 / STEPS,
                                       X[:, bass.ds(QT * b, QT), :].rearrange("p q d -> p (q d)"),
                                       ALU.mult, ALU.add).then_inc(ff["out"], 1)

            def slot_fn(b, par, s):
                if exists(s, 3):
                    norm_stats(v, b + 3, ff["norm_own"], ff["var"])
                    if not exists(s, 0):
                        apply(b + 3, 1 - par)
                if exists(s, 0):
                    membrane(b, par, exists(s, 3))
                if exists(s, -2):
                    result(b - 2, par)
            return slot_fn

        def ffn_on_gpsimd(pool):
            for b in range(B):
                norm_root(pool, b, ff["var"], ff["rstd"])

        def ffn_on_tensor(pe):
            def slot_fn(b, par, s):
                if exists(s, 1):
                    pe.wait_ge(ff["sq"], b + 2)
                    if reused(b + 1):
                        pe.wait_ge(ff["yc"], b)
                    if s == -1:
                        pe.wait_ge(ly[1]["x_added"], B)
                    for q in range(QT):
                        for c in range(HC):
                            mm = pe.matmul(M[1 - par][:, q * D:(q + 1) * D], h2[1 - par][:, c, q * P:(q + 1) * P], wpr[:, c, :],
                                           start=(c == 0), stop=(c == HC - 1))
                    mm.then_inc(ff["y"], 1)
                if exists(s, 2):
                    pe.wait_ge(ff["xTc"], b + 3)
                    if reused(b + 2):
                        pe.wait_ge(ff["relu"], b + 1)
                    for c in range(HC):
                        mm = pe.matmul(S2[par][:, c // 2, c % 2, :], wfc[:, c * P:(c + 1) * P], gT[par][:, :],
                                       start=True, stop=True)
                    mm.then_inc(ff["h"], 1)
                if exists(s, 3):
                    pe.wait_ge(ff["xn"], b + 4)
                    if s != -3:
                        pe.wait_ge(ff["xTc"], b + 3)
                    for q in range(QT):
                        mm = pe.transpose(S1[0][:, q, 0:P], xn[1 - par][:, q, :], eye[:, :])
                    mm.then_inc(ff["xT"], 1)
                if exists(s, -1):
                    pe.wait_ge(ff["spike"], b)
                    if not (isinstance(b, int) and b == 1):
                        pe.wait_ge(ff["out"], b - 1)
                    for k in range(STEPS):
                        mm = pe.matmul(S1[1][:, 0, :], eye16[:, :], spike[1 - par][:, k, :], start=(k == 0),
                                       stop=(k == STEPS - 1))
                    mm.then_inc(ff["count"], 1)
            return slot_fn

        def ffn_on_scalar(act):
            def slot_fn(b, par, s):
                if exists(s, -1):
                    act.wait_ge(ff["mem"], 2 * (STEPS - 1) * b)
                    if not (isinstance(b, int) and b == 1):
                        act.wait_ge(ff["spike"], b - 1)
                    act.activation(above[:, :, :], mem[1 - par][:, 0:STEPS, :], ACT.Relu, bias=minus_one[:, :]) \
                       .then_inc(ff["above"], 1)
                if exists(s, 1):
                    act.wait_ge(ff["y"], b + 2)
                    if reused(b + 1):
                        act.wait_ge(ff["above"], b)
                    act.activation(mem[1 - par][:, 0, :], M[1 - par][:, 0:S], ACT.Copy).then_inc(ff["yc"], 1)
                if exists(s, -1):
                    act.wait_ge(ff["above"], b)
                    if reused(b - 1):
                        act.wait_ge(ff["count"], b - 2)
                    act.activation(spike[1 - par][:, :, :], above[:, :, :], ACT.Sign).then_inc(ff["spike"], 1)
                if exists(s, 2):
                    flat = hr[par].rearrange("p c n -> p (c n)")
                    act.wait_ge(ff["h"], b + 3)
                    act.activation(flat, S2[par][:, :, :, :].rearrange("p a k n -> p (a k n)"), ACT.Relu) \
                       .then_inc(ff["relu"], 1)
                    act.wait_ge(ff["relu"], b + 3)
                    if reused(b + 2):
                        act.wait_ge(ff["y"], b + 1)
                    act.activation(h2[par].rearrange("p c n -> p (c n)"), flat, ACT.Square).then_inc(ff["sq"], 1)
                if exists(s, 3):
                    act.wait_ge(ff["xT"], b + 4)
                    if reused(b + 3):
                        act.wait_ge(ff["h"], b + 2)
                    act.activation(gT[1 - par][:, :].rearrange("p (q n) -> p q n", q=QT), S1[0][:, :, 0:P], ACT.Copy) \
                       .then_inc(ff["xTc"], 1)
            return slot_fn

        def ffn_on_sync(sp):
            for b in range(B):
                sp.wait_ge(ff["out"], b + 1)
                sp.dma_start(out[b, :, :].rearrange("(q p) d -> p q d", p=P), fin[b % 2][:, :, :]) \
                  .then_inc(ff[f"stored{b % 2}"], 16)
            for par in range(2):
                sp.wait_ge(ff[f"stored{par}"], 16 * (B // 2))

        def rows_of_maximum(kt, g, copy):
            copy(kt[M0:P, HG * g:HG * g + HG, :], head_mask[M0:P, :].unsqueeze(2).to_broadcast([P - M0, HG, S])) \
                .then_inc(kt_rows, 1)

        @block.sync
        def _(sp):
            first = QT * 2
            context_on_sync(sp, ly[0], -2, 0)
            for dst, src in [(W["k", 0][:, :], t["wk0"]), (X[:, 0:first, :], t["x"][:, 0:first, :]), (W["q", 0][:, :], t["wq0"])]:
                sp.dma_start(dst, src).then_inc(loaded, 16)
            for dst, src in [(X[:, first:NT, :], t["x"][:, first:NT, :]), (W["v", 0][:, :], t["wv0"]),
                             (W["o", 0][:, :], t["wo0"])]:
                sp.dma_start(dst, src).then_inc(loaded_x, 16)
            late = [(W[n, 1][:, :], t[f"w{n}1"]) for n in "qkvo"]
            late += [(slope[:, :], t["c_slope"]), (before[:, :], t["c_before"]), (route_c[:, :, :], t["c_route"]),
                     (wg[:, :], t["wg"]), (bg[:, :], t["bg"].partition_broadcast(P)), (braw[:, :], t["braw"]),
                     (b1c[:, :, :], t["b1c"]),
                     (wfc[:, :], t["wfc"]), (wpr[:, :, :], t["wpr"])]
            late += [(pos_i[b * H:(b + 1) * H, :], t["pos"][b:b + 1, :].partition_broadcast(H)) for b in range(B)]
            assert len(late) == N_LATE
            keys_on_sync(sp, ly[0], -2, False)
            attention_on_sync(sp, ly[0], late)
            sp.wait_ge(inited, N_INIT)
            sp.dma_start(xs_dram.rearrange("(j p) d -> p j d", p=P), zero[:, :].unsqueeze(1).to_broadcast([P, SLOT_TILES, D])) \
              .then_inc(moe["zfill"], 16)
            mask_on_sync(sp)
            sp.wait_ge(moe["bsplit"], 5)
            for c in range(PARTS):
                sp.dma_start(b2rows[c:c + 1, :], bparts[:, c, :]).then_inc(moe["brows"], 16)
            sp.wait_ge(parts_made, N_PARTS_MADE)
            sp.dma_start(pos_dram.rearrange("b h c n -> (b h) c n"), pos_parts[:, :, :]).then_inc(pos_stored, 16)
            experts_on_sync(sp)
            sp.wait_ge(pos_stored, 16)
            attention_on_sync(sp, ly[1], [])
            ffn_on_sync(sp)

        @block.gpsimd
        def _(pool):
            pool.wait_ge(loaded, 16 * N_LOADS)
            pool.wait_ge(inited, N_INIT)
            attention_on_gpsimd(pool, ly[0])
            gate_on_gpsimd(pool)
            scatter_on_gpsimd(pool)
            gather_on_gpsimd(pool)
            attention_on_gpsimd(pool, ly[1])
            ffn_on_gpsimd(pool)

        @block.scalar
        def _(act):
            for dst, src in [(qkb[:, :], t["qkb"]), (eye[:, :], t["c_eye"]), (head_mask[:, :], t["c_head_mask"])]:
                act.dma_start(dst, src).then_inc(loaded, 16)
            for dst, src in [(vb[:, :], t["vb"].partition_broadcast(P)), (ob[:, :], t["ob"].partition_broadcast(P))]:
                act.dma_start(dst, src).then_inc(loaded_x, 16)
            act.wait_ge(loaded, 16 * N_LOADS)
            act.wait_ge(inited, N_INIT)
            keys_on_scalar(act, ly[0], -2, False)
            attention_on_scalar(act, ly[0])
            gate_on_scalar(act)
            experts_on_scalar(act)
            ffn = ffn_on_scalar(act)
            attention_on_scalar(act, ly[1], ffn)
            ffn_loop(act, ffn)

        @block.vector
        def _(v):
            v.memset(X[:, NT:NT + QT, :], 0.0).then_inc(inited, 1)
            v.memset(mhalf[:, :], -0.5).then_inc(inited, 1)
            v.memset(minus_one[:, :], -1.0).then_inc(inited, 1)
            v.memset(zero[:, :], 0.0).then_inc(inited, 1)
            v.memset(ones32[:, :], 1.0).then_inc(inited, 1)
            v.memset(ones16[:, :], 1.0).then_inc(inited, 1)
            for i in range(2):
                v.memset(Qt[i][M0:P, :, :], MROW).then_inc(inited, 1)
                v.memset(Vt[i][:, :, :, :], 0.0).then_inc(vt_zeroed, 1)
            v.wait_ge(vt_zeroed, 2)
            for i in range(2):
                v.memset(Vt[i][:, :, :, DH], 1.0).then_inc(inited, 1)
            v.wait_ge(loaded, 16 * N_LOADS)
            v.tensor_copy(eye16[:, :], eye[:, :]).then_inc(inited, 1)
            v.tensor_copy(eye_bf[:, :], eye[:, :]).then_inc(inited, 1)
            v.tensor_scalar(qkbs[:, 0:1], qkb[:, 0:1], QK / float(np.sqrt(DH)), None, ALU.mult).then_inc(inited, 1)
            v.tensor_scalar(qkbs[:, 1:2], qkb[:, 1:2], QK, None, ALU.mult).then_inc(inited, 1)
            v.wait_ge(inited, N_INIT)
            attention_on_vector(v, ly[0])
            gate_on_vector(v)
            route_on_vector(v)
            biases_on_vector(v)
            mask_on_vector(v)
            experts_on_vector(v)
            ffn = ffn_on_vector(v)
            attention_on_vector(v, ly[1], ffn)
            ffn_loop(v, ffn)

        @block.tensor
        def _(pe):
            pe.wait_ge(loaded, 16 * N_LOADS)
            pe.wait_ge(inited, N_INIT)
            first_keys_on_tensor(pe, ly[0])
            attention_on_tensor(pe, ly[0], False)
            gate_on_tensor(pe)
            mask_on_tensor(pe)
            experts_on_tensor(pe)
            pe.wait_ge(mk["any"], 1)
            any_masked = pe.value_load(mask_any[0:1, 0:1], min_val=0, max_val=1)
            ffn = ffn_on_tensor(pe)
            with pe.If(any_masked == 1):
                attention_on_tensor(pe, ly[1], True, ffn)
            with pe.Else():
                attention_on_tensor(pe, ly[1], False, ffn)
            ffn_loop(pe, ffn)


def q_order():
    return [(HG * (2 * hf + g2) + i) * DH + d for hf in range(2) for i in range(HG) for d in range(DH) for g2 in range(2)]


def k_order():
    return [(HG * g + i) * DH + d for i in range(HG) for d in range(DH) for g in range(NG)]


def kernel(**inputs):
    import concourse.bacc as bacc
    from concourse.bass_utils import run_bass_kernel_spmd

    a = {k: np.asarray(v) for k, v in inputs.items()}
    lay = np.ascontiguousarray
    qo, ko = q_order(), k_order()
    arrays = {
        "x": lay(a["x"].reshape(NT, P, D).transpose(1, 0, 2)),
        "ctxT": lay(a["ctx_1024"].transpose(2, 0, 1)),
        "pos": lay(a["itok_BxS2_1_8191"]),
        "qkb": lay(np.stack([a["L0_xattn_wq_b"][qo], a["L0_xattn_wk_b"][ko]], axis=1)),
        "vb": a["L0_xattn_wv_b"], "ob": a["L0_xattn_wo_b"],
        "mask": lay(a["mask_BxSxS2_if1"].reshape(NT, P, S).transpose(1, 0, 2).reshape(P, NT * S)),
        "wg": a["L0_ffn_Wg"], "bg": a["L0_ffn_bg"],
        "w": lay(np.concatenate([a["L0_ffn_W1"].transpose(1, 0, 2).reshape(P, NE * HC, P),
                                 a["L0_ffn_W2"].reshape(NE, HC, P, D).transpose(2, 0, 1, 3).reshape(P, NE * HC, D)], axis=1)),
        "braw": lay(a["L0_ffn_b2"].reshape(P, NE * D // P)),
        "b1c": lay(a["L0_ffn_b1"].reshape(NE, HC, P).transpose(2, 1, 0)),
        "wfc": lay(a["L1_ffn_W_fc"].T),
        "wpr": lay(a["L1_ffn_W_proj"].T.reshape(HC, P, D).transpose(1, 0, 2)),
    }
    for L, names in enumerate((("L0_xattn_wq_w", "L0_xattn_wk_w", "L0_xattn_wv_w", "L0_xattn_wo_w"),
                               ("L1_xattn_W_q", "L1_xattn_W_k", "L1_xattn_W_v", "L1_xattn_W_o"))):
        for n, name in zip("qkvo", names):
            w = a[name].T
            arrays[f"w{n}{L}"] = lay(w[:, qo] if n == "q" else w[:, ko] if n == "k" else w)
    arrays.update(constants())
    nc = bacc.Bacc("TRN2", target_bir_lowering=False, num_devices=1)
    t = {n: nc.dram_tensor(f"in_{n}", v.shape, mybir.dt.from_np(v.dtype), kind="ExternalInput").ap()
         for n, v in arrays.items()}
    out = nc.dram_tensor("out", (B, S, D), F32, kind="ExternalOutput").ap()
    build(nc, t, out)
    r = run_bass_kernel_spmd(nc, [{f"in_{n}": v for n, v in arrays.items()}], core_ids=[0])
    return r.results[0]["out"]
```
